# Optimizing a Trainium2 kernel written in Bass

```python
import numpy as np
import jax
import jax.numpy as jnp

def _softmax(x, axis=-1):
    return jax.nn.softmax(x, axis=axis)

def _gelu(x):
    return jax.nn.gelu(x, approximate=True)

def _silu(x):
    return jax.nn.silu(x)

def _sigmoid(x):
    return jax.nn.sigmoid(x)

def _layernorm(x, axis=-1, eps=1e-05):
    m = jnp.mean(x, axis=axis, keepdims=True)
    v = jnp.var(x, axis=axis, keepdims=True)
    return (x - m) / jnp.sqrt(v + eps)

def _scatter_add(tgt, idx, src, axis=0):
    return tgt.at[idx].add(src)

def _segment_sum(src, seg, n):
    return jax.ops.segment_sum(src, seg, n)
kernel_name = 'mk_xattn_seq_d2_seqx_r4_15ef7e'

def setup_inputs(seed: int=0):
    np.random.seed(seed)
    _w = jnp.asarray

    def _rec_inputs():
        import jax
        import jax.numpy as jnp
        _rk = jax.random.key(seed)
        x = 7.22e-05 + 1 * jax.random.normal(jax.random.fold_in(_rk, 1), (2, 512, 512), jnp.float32)
        _lenS = 512 - jax.random.randint(jax.random.fold_in(_rk, 7), (2,), 0, max(1, 512 // 4) + 1, jnp.int32)
        _lenS2 = 1024 - jax.random.randint(jax.random.fold_in(_rk, 8), (2,), 0, max(1, 1024 // 4) + 1, jnp.int32)
        _ctx_2048P = jax.random.normal(jax.random.fold_in(_rk, 11), (2, 16, 512), jnp.float32)
        _ctx_2048c = jax.random.dirichlet(jax.random.fold_in(_rk, 511), 0.3 * jnp.ones((16,), jnp.float32), (2, 1024))
        _ctx_2048t = jnp.einsum('bsk,bkd->bsd', _ctx_2048c, _ctx_2048P)
        _ctx_2048t = _ctx_2048t * jax.lax.rsqrt(jnp.mean(jnp.square(_ctx_2048t)) + 1e-12) * 0.953939
        ctx_2048 = 4.13588e-05 + 0.999923 * (_ctx_2048t + 0.3 * jax.random.normal(jax.random.fold_in(_rk, 611), (2, 1024, 512), jnp.float32))
        _validS = jnp.arange(512)[None, :] < _lenS[:, None]
        _validS2 = jnp.arange(1024)[None, :] < _lenS2[:, None]
        _causal = jnp.tril(jnp.ones((512, 512), dtype=bool))
        mask_Bx1xSxS2_ff0 = jnp.where(jnp.ones((2, 1, 512, 1024), dtype=bool), 0.0, -1000000000.0).astype(jnp.float32)
        return (x, ctx_2048, mask_Bx1xSxS2_ff0)
    x, ctx_2048, mask_Bx1xSxS2_ff0 = _rec_inputs()

    def _L0_xattn_setup():
        import jax, jax.numpy as jnp
        import numpy as np
        H = 512
        NH = 32
        KVH = 8
        HD = H // NH
        GROUPS = NH // KVH
        EPS = 1e-06
        B, L, S = (4, 256, 256)

        def _gqa_forward(hidden_state, encoder_hidden_state, encoder_attention_mask, Wq, bq, Wk, bk, Wv, bv, Wo, bo, gamma, beta):
            b, l, _ = hidden_state.shape
            s = encoder_hidden_state.shape[1]
            q = hidden_state @ Wq + bq
            k = encoder_hidden_state @ Wk + bk
            v = encoder_hidden_state @ Wv + bv
            q = q.reshape(b, l, KVH, GROUPS, HD).transpose(0, 2, 3, 1, 4)
            k = k.reshape(b, s, KVH, HD).transpose(0, 2, 1, 3)
            v = v.reshape(b, s, KVH, HD).transpose(0, 2, 1, 3)
            scale = 1.0 / jnp.sqrt(jnp.asarray(HD, q.dtype))
            scores = jnp.einsum('bkgld,bksd->bkgls', q, k) * scale
            scores = scores + encoder_attention_mask[:, :, None, :, :]
            attn = jax.nn.softmax(scores, axis=-1)
            out = jnp.einsum('bkgls,bksd->bkgld', attn, v)
            out = out.transpose(0, 3, 1, 2, 4).reshape(b, l, H)
            out = out @ Wo + bo
            x = out + hidden_state
            mu = jnp.mean(x, axis=-1, keepdims=True)
            var = jnp.var(x, axis=-1, keepdims=True)
            return (x - mu) * jax.lax.rsqrt(var + EPS) * gamma + beta
        key = jax.random.key(seed)
        ks = jax.random.split(key, 12)
        sd = 0.02
        return {'hidden_state': jax.random.normal(ks[0], (B, L, H), jnp.float32), 'encoder_hidden_state': jax.random.normal(ks[1], (B, S, H), jnp.float32), 'encoder_attention_mask': jnp.zeros((B, 1, L, S), jnp.float32), 'Wq': jax.random.normal(ks[2], (H, H), jnp.float32) * sd, 'bq': jnp.zeros((H,), jnp.float32), 'Wk': jax.random.normal(ks[3], (H, KVH * HD), jnp.float32) * sd, 'bk': jnp.zeros((KVH * HD,), jnp.float32), 'Wv': jax.random.normal(ks[4], (H, KVH * HD), jnp.float32) * sd, 'bv': jnp.zeros((KVH * HD,), jnp.float32), 'Wo': jax.random.normal(ks[5], (H, H), jnp.float32) * sd, 'bo': jnp.zeros((H,), jnp.float32), 'gamma': jnp.ones((H,), jnp.float32), 'beta': jnp.zeros((H,), jnp.float32)}
    _L0_xattn_all = _L0_xattn_setup()
    _L0_xattn_in = {k: v for k, v in _L0_xattn_all.items() if k in ('Wq', 'bq', 'Wk', 'bk', 'Wv', 'bv', 'Wo', 'bo', 'gamma', 'beta')}
    del _L0_xattn_all

    def _L1_xattn_setup():
        import jax, jax.numpy as jnp
        import numpy as np
        B, Q, S1, S2 = (4, 64, 512, 512)
        D, H, K, F = (512, 16, 128, 2048)
        LN_EPS = 1e-05

        def _layer_norm(x, scale, offset):
            mu = jnp.mean(x, axis=-1, keepdims=True)
            var = jnp.var(x, axis=-1, keepdims=True)
            return (x - mu) * jax.lax.rsqrt(var + LN_EPS) * scale + offset

        def _cross_attention(q_in, kv_in, wq, bq, wk, bk, wv, bv, wo, bo, bias_k, bias_v):
            b, q_len, _ = q_in.shape
            t = kv_in.shape[1]
            qh = (q_in @ wq + bq).reshape(b, q_len, H, K)
            kh = (kv_in @ wk + bk).reshape(b, t, H, K)
            vh = (kv_in @ wv + bv).reshape(b, t, H, K)
            kh = jnp.concatenate([kh, jnp.broadcast_to(bias_k, (b, 1, H, K))], axis=1)
            vh = jnp.concatenate([vh, jnp.broadcast_to(bias_v, (b, 1, H, K))], axis=1)
            scale = jnp.sqrt(jnp.asarray(K, q_in.dtype))
            logits = jnp.einsum('bqhk,bthk->bhqt', qh, kh) / scale
            weights = jax.nn.softmax(logits, axis=-1)
            ctx = jnp.einsum('bhqt,bthk->bqhk', weights, vh).reshape(b, q_len, H * K)
            return ctx @ wo + bo

        def _forward(x, xf_1, xf_2, ln1_scale, ln1_offset, wq1, bq1, wk1, bk1, wv1, bv1, wo1, bo1, bias_k1, bias_v1, ln2_scale, ln2_offset, wq2, bq2, wk2, bk2, wv2, bv2, wo2, bo2, bias_k2, bias_v2, ln_mlp_scale, ln_mlp_offset, w_fc1, b_fc1, w_fc2, b_fc2):
            res = x
            h = _layer_norm(x, ln1_scale, ln1_offset)
            x = res + _cross_attention(h, xf_1, wq1, bq1, wk1, bk1, wv1, bv1, wo1, bo1, bias_k1, bias_v1)
            res = x
            h = _layer_norm(x, ln2_scale, ln2_offset)
            x = res + _cross_attention(h, xf_2, wq2, bq2, wk2, bk2, wv2, bv2, wo2, bo2, bias_k2, bias_v2)
            h = _layer_norm(x, ln_mlp_scale, ln_mlp_offset)
            h = jax.nn.gelu(h @ w_fc1 + b_fc1, approximate=False) @ w_fc2 + b_fc2
            return x + h
        key = jax.random.key(seed)
        ks = iter(jax.random.split(key, 64))

        def rn(shape, s=0.02):
            return jax.random.normal(next(ks), shape, jnp.float32) * s
        inp = {'x': rn((B, Q, D), 1.0), 'xf_1': rn((B, S1, D), 1.0), 'xf_2': rn((B, S2, D), 1.0)}
        for i in (1, 2):
            inp[f'ln{i}_scale'] = jnp.ones((D,), jnp.float32)
            inp[f'ln{i}_offset'] = jnp.zeros((D,), jnp.float32)
            inp[f'wq{i}'] = rn((D, H * K))
            inp[f'bq{i}'] = jnp.zeros((H * K,), jnp.float32)
            inp[f'wk{i}'] = rn((D, H * K))
            inp[f'bk{i}'] = jnp.zeros((H * K,), jnp.float32)
            inp[f'wv{i}'] = rn((D, H * K))
            inp[f'bv{i}'] = jnp.zeros((H * K,), jnp.float32)
            inp[f'wo{i}'] = rn((H * K, D))
            inp[f'bo{i}'] = jnp.zeros((D,), jnp.float32)
            inp[f'bias_k{i}'] = rn((1, 1, H, K))
            inp[f'bias_v{i}'] = rn((1, 1, H, K))
        inp['ln_mlp_scale'] = jnp.ones((D,), jnp.float32)
        inp['ln_mlp_offset'] = jnp.zeros((D,), jnp.float32)
        inp['w_fc1'] = rn((D, F))
        inp['b_fc1'] = jnp.zeros((F,), jnp.float32)
        inp['w_fc2'] = rn((F, D))
        inp['b_fc2'] = jnp.zeros((D,), jnp.float32)
        return inp
    _L1_xattn_all = _L1_xattn_setup()
    _L1_xattn_in = {k: v for k, v in _L1_xattn_all.items() if k in ('ln1_scale', 'ln1_offset', 'wq1', 'bq1', 'wk1', 'bk1', 'wv1', 'bv1', 'wo1', 'bo1', 'bias_k1', 'bias_v1', 'ln2_scale', 'ln2_offset', 'wq2', 'bq2', 'wk2', 'bk2', 'wv2', 'bv2', 'wo2', 'bo2', 'bias_k2', 'bias_v2', 'ln_mlp_scale', 'ln_mlp_offset', 'w_fc1', 'b_fc1', 'w_fc2', 'b_fc2')}
    del _L1_xattn_all
    return {'x': x, 'ctx_2048': ctx_2048, 'mask_Bx1xSxS2_ff0': mask_Bx1xSxS2_ff0, 'L0_xattn_Wq': _L0_xattn_in['Wq'], 'L0_xattn_bq': _L0_xattn_in['bq'], 'L0_xattn_Wk': _L0_xattn_in['Wk'], 'L0_xattn_bk': _L0_xattn_in['bk'], 'L0_xattn_Wv': _L0_xattn_in['Wv'], 'L0_xattn_bv': _L0_xattn_in['bv'], 'L0_xattn_Wo': _L0_xattn_in['Wo'], 'L0_xattn_bo': _L0_xattn_in['bo'], 'L0_xattn_gamma': _L0_xattn_in['gamma'], 'L0_xattn_beta': _L0_xattn_in['beta'], 'L1_xattn_ln1_scale': _L1_xattn_in['ln1_scale'], 'L1_xattn_ln1_offset': _L1_xattn_in['ln1_offset'], 'L1_xattn_wq1': _L1_xattn_in['wq1'], 'L1_xattn_bq1': _L1_xattn_in['bq1'], 'L1_xattn_wk1': _L1_xattn_in['wk1'], 'L1_xattn_bk1': _L1_xattn_in['bk1'], 'L1_xattn_wv1': _L1_xattn_in['wv1'], 'L1_xattn_bv1': _L1_xattn_in['bv1'], 'L1_xattn_wo1': _L1_xattn_in['wo1'], 'L1_xattn_bo1': _L1_xattn_in['bo1'], 'L1_xattn_bias_k1': _L1_xattn_in['bias_k1'], 'L1_xattn_bias_v1': _L1_xattn_in['bias_v1'], 'L1_xattn_ln2_scale': _L1_xattn_in['ln2_scale'], 'L1_xattn_ln2_offset': _L1_xattn_in['ln2_offset'], 'L1_xattn_wq2': _L1_xattn_in['wq2'], 'L1_xattn_bq2': _L1_xattn_in['bq2'], 'L1_xattn_wk2': _L1_xattn_in['wk2'], 'L1_xattn_bk2': _L1_xattn_in['bk2'], 'L1_xattn_wv2': _L1_xattn_in['wv2'], 'L1_xattn_bv2': _L1_xattn_in['bv2'], 'L1_xattn_wo2': _L1_xattn_in['wo2'], 'L1_xattn_bo2': _L1_xattn_in['bo2'], 'L1_xattn_bias_k2': _L1_xattn_in['bias_k2'], 'L1_xattn_bias_v2': _L1_xattn_in['bias_v2'], 'L1_xattn_ln_mlp_scale': _L1_xattn_in['ln_mlp_scale'], 'L1_xattn_ln_mlp_offset': _L1_xattn_in['ln_mlp_offset'], 'L1_xattn_w_fc1': _L1_xattn_in['w_fc1'], 'L1_xattn_b_fc1': _L1_xattn_in['b_fc1'], 'L1_xattn_w_fc2': _L1_xattn_in['w_fc2'], 'L1_xattn_b_fc2': _L1_xattn_in['b_fc2']}

def reference(x, ctx_2048, mask_Bx1xSxS2_ff0, L0_xattn_Wq, L0_xattn_bq, L0_xattn_Wk, L0_xattn_bk, L0_xattn_Wv, L0_xattn_bv, L0_xattn_Wo, L0_xattn_bo, L0_xattn_gamma, L0_xattn_beta, L1_xattn_ln1_scale, L1_xattn_ln1_offset, L1_xattn_wq1, L1_xattn_bq1, L1_xattn_wk1, L1_xattn_bk1, L1_xattn_wv1, L1_xattn_bv1, L1_xattn_wo1, L1_xattn_bo1, L1_xattn_bias_k1, L1_xattn_bias_v1, L1_xattn_ln2_scale, L1_xattn_ln2_offset, L1_xattn_wq2, L1_xattn_bq2, L1_xattn_wk2, L1_xattn_bk2, L1_xattn_wv2, L1_xattn_bv2, L1_xattn_wo2, L1_xattn_bo2, L1_xattn_bias_k2, L1_xattn_bias_v2, L1_xattn_ln_mlp_scale, L1_xattn_ln_mlp_offset, L1_xattn_w_fc1, L1_xattn_b_fc1, L1_xattn_w_fc2, L1_xattn_b_fc2):
    import jax
    import jax.numpy as jnp

    def _L0_xattn_ref(hidden_state, encoder_hidden_state, encoder_attention_mask, Wq, bq, Wk, bk, Wv, bv, Wo, bo, gamma, beta):
        import jax, jax.numpy as jnp
        import numpy as np
        H = 512
        NH = 32
        KVH = 8
        HD = H // NH
        GROUPS = NH // KVH
        EPS = 1e-06
        B, L, S = (4, 256, 256)

        def _gqa_forward(hidden_state, encoder_hidden_state, encoder_attention_mask, Wq, bq, Wk, bk, Wv, bv, Wo, bo, gamma, beta):
            b, l, _ = hidden_state.shape
            s = encoder_hidden_state.shape[1]
            q = hidden_state @ Wq + bq
            k = encoder_hidden_state @ Wk + bk
            v = encoder_hidden_state @ Wv + bv
            q = q.reshape(b, l, KVH, GROUPS, HD).transpose(0, 2, 3, 1, 4)
            k = k.reshape(b, s, KVH, HD).transpose(0, 2, 1, 3)
            v = v.reshape(b, s, KVH, HD).transpose(0, 2, 1, 3)
            scale = 1.0 / jnp.sqrt(jnp.asarray(HD, q.dtype))
            scores = jnp.einsum('bkgld,bksd->bkgls', q, k) * scale
            scores = scores + encoder_attention_mask[:, :, None, :, :]
            attn = jax.nn.softmax(scores, axis=-1)
            out = jnp.einsum('bkgls,bksd->bkgld', attn, v)
            out = out.transpose(0, 3, 1, 2, 4).reshape(b, l, H)
            out = out @ Wo + bo
            x = out + hidden_state
            mu = jnp.mean(x, axis=-1, keepdims=True)
            var = jnp.var(x, axis=-1, keepdims=True)
            return (x - mu) * jax.lax.rsqrt(var + EPS) * gamma + beta
        return _gqa_forward(hidden_state, encoder_hidden_state, encoder_attention_mask, Wq, bq, Wk, bk, Wv, bv, Wo, bo, gamma, beta)

    def _L1_xattn_ref(x, xf_1, xf_2, ln1_scale, ln1_offset, wq1, bq1, wk1, bk1, wv1, bv1, wo1, bo1, bias_k1, bias_v1, ln2_scale, ln2_offset, wq2, bq2, wk2, bk2, wv2, bv2, wo2, bo2, bias_k2, bias_v2, ln_mlp_scale, ln_mlp_offset, w_fc1, b_fc1, w_fc2, b_fc2):
        import jax, jax.numpy as jnp
        import numpy as np
        B, Q, S1, S2 = (4, 64, 512, 512)
        D, H, K, F = (512, 16, 128, 2048)
        LN_EPS = 1e-05

        def _layer_norm(x, scale, offset):
            mu = jnp.mean(x, axis=-1, keepdims=True)
            var = jnp.var(x, axis=-1, keepdims=True)
            return (x - mu) * jax.lax.rsqrt(var + LN_EPS) * scale + offset

        def _cross_attention(q_in, kv_in, wq, bq, wk, bk, wv, bv, wo, bo, bias_k, bias_v):
            b, q_len, _ = q_in.shape
            t = kv_in.shape[1]
            qh = (q_in @ wq + bq).reshape(b, q_len, H, K)
            kh = (kv_in @ wk + bk).reshape(b, t, H, K)
            vh = (kv_in @ wv + bv).reshape(b, t, H, K)
            kh = jnp.concatenate([kh, jnp.broadcast_to(bias_k, (b, 1, H, K))], axis=1)
            vh = jnp.concatenate([vh, jnp.broadcast_to(bias_v, (b, 1, H, K))], axis=1)
            scale = jnp.sqrt(jnp.asarray(K, q_in.dtype))
            logits = jnp.einsum('bqhk,bthk->bhqt', qh, kh) / scale
            weights = jax.nn.softmax(logits, axis=-1)
            ctx = jnp.einsum('bhqt,bthk->bqhk', weights, vh).reshape(b, q_len, H * K)
            return ctx @ wo + bo

        def _forward(x, xf_1, xf_2, ln1_scale, ln1_offset, wq1, bq1, wk1, bk1, wv1, bv1, wo1, bo1, bias_k1, bias_v1, ln2_scale, ln2_offset, wq2, bq2, wk2, bk2, wv2, bv2, wo2, bo2, bias_k2, bias_v2, ln_mlp_scale, ln_mlp_offset, w_fc1, b_fc1, w_fc2, b_fc2):
            res = x
            h = _layer_norm(x, ln1_scale, ln1_offset)
            x = res + _cross_attention(h, xf_1, wq1, bq1, wk1, bk1, wv1, bv1, wo1, bo1, bias_k1, bias_v1)
            res = x
            h = _layer_norm(x, ln2_scale, ln2_offset)
            x = res + _cross_attention(h, xf_2, wq2, bq2, wk2, bk2, wv2, bv2, wo2, bo2, bias_k2, bias_v2)
            h = _layer_norm(x, ln_mlp_scale, ln_mlp_offset)
            h = jax.nn.gelu(h @ w_fc1 + b_fc1, approximate=False) @ w_fc2 + b_fc2
            return x + h
        return _forward(x, xf_1, xf_2, ln1_scale, ln1_offset, wq1, bq1, wk1, bk1, wv1, bv1, wo1, bo1, bias_k1, bias_v1, ln2_scale, ln2_offset, wq2, bq2, wk2, bk2, wv2, bv2, wo2, bo2, bias_k2, bias_v2, ln_mlp_scale, ln_mlp_offset, w_fc1, b_fc1, w_fc2, b_fc2)
    x = _L0_xattn_ref(x, ctx_2048, mask_Bx1xSxS2_ff0, L0_xattn_Wq, L0_xattn_bq, L0_xattn_Wk, L0_xattn_bk, L0_xattn_Wv, L0_xattn_bv, L0_xattn_Wo, L0_xattn_bo, L0_xattn_gamma, L0_xattn_beta)
    x = _L1_xattn_ref(x, ctx_2048, ctx_2048, L1_xattn_ln1_scale, L1_xattn_ln1_offset, L1_xattn_wq1, L1_xattn_bq1, L1_xattn_wk1, L1_xattn_bk1, L1_xattn_wv1, L1_xattn_bv1, L1_xattn_wo1, L1_xattn_bo1, L1_xattn_bias_k1, L1_xattn_bias_v1, L1_xattn_ln2_scale, L1_xattn_ln2_offset, L1_xattn_wq2, L1_xattn_bq2, L1_xattn_wk2, L1_xattn_bk2, L1_xattn_wv2, L1_xattn_bv2, L1_xattn_wo2, L1_xattn_bo2, L1_xattn_bias_k2, L1_xattn_bias_v2, L1_xattn_ln_mlp_scale, L1_xattn_ln_mlp_offset, L1_xattn_w_fc1, L1_xattn_b_fc1, L1_xattn_w_fc2, L1_xattn_b_fc2)
    return x

_drawn_inputs = setup_inputs


def setup_inputs(seed=0):
    import zlib

    import numpy as np

    out = dict(_drawn_inputs(seed))
    spreads = {'L0_xattn_bq': (0.0, 0.8),
     'L0_xattn_bk': (0.0, 2.0),
     'L0_xattn_bv': (0.0, 0.1),
     'L0_xattn_bo': (0.0, 0.1),
     'L0_xattn_gamma': (1.0, 0.2),
     'L0_xattn_beta': (0.0, 0.1),
     'L1_xattn_ln1_scale': (1.0, 0.6),
     'L1_xattn_ln1_offset': (0.0, 0.8),
     'L1_xattn_bq1': (0.0, 0.8),
     'L1_xattn_bk1': (0.0, 2.0),
     'L1_xattn_bv1': (0.0, 0.1),
     'L1_xattn_bo1': (0.0, 0.1),
     'L1_xattn_ln2_scale': (1.0, 0.6),
     'L1_xattn_ln2_offset': (0.0, 0.8),
     'L1_xattn_bq2': (0.0, 0.8),
     'L1_xattn_bk2': (0.0, 2.0),
     'L1_xattn_bv2': (0.0, 0.1),
     'L1_xattn_bo2': (0.0, 0.1),
     'L1_xattn_ln_mlp_scale': (1.0, 0.2),
     'L1_xattn_ln_mlp_offset': (0.0, 0.36),
     'L1_xattn_b_fc1': (0.0, 0.1),
     'L1_xattn_b_fc2': (0.0, 0.1)}
    factors = {'L0_xattn_Wq': 7.863,
     'L0_xattn_Wk': 7.858,
     'L1_xattn_wq1': 3.966,
     'L1_xattn_wk1': 3.872,
     'L1_xattn_bias_k1': 64.0,
     'L1_xattn_bias_v1': 64.0,
     'L1_xattn_wq2': 3.997,
     'L1_xattn_wk2': 3.952,
     'L1_xattn_bias_k2': 64.0,
     'L1_xattn_bias_v2': 64.0}
    for name, (base, spread) in spreads.items():
        noise = np.random.default_rng([zlib.crc32(name.encode()), seed]).standard_normal(out[name].shape)
        drawn = base * np.exp(spread * noise) if base else spread * noise
        out[name] = jnp.asarray(drawn.astype(out[name].dtype))
    for name, factor in factors.items():
        out[name] = (out[name] * factor).astype(out[name].dtype)
    return out
```

```python
from contextlib import ExitStack

import numpy as np

import concourse.bass as bass
from concourse import mybir

F32 = mybir.dt.float32
F32R = mybir.dt.float32r
BF16 = mybir.dt.bfloat16
F16 = mybir.dt.float16
ALU = mybir.AluOpType
ACT = mybir.ActivationFunctionType
AX = mybir.AxisListType

P = 128
B, L, S, D = 2, 512, 1024, 512
CT, LT, ST = D // P, L // P, S // P
KVH, GROUPS, HD = 8, 4, 16
NH0 = KVH * GROUPS
LAYERS, HEADS, KD = 2, 16, 128
PAIRS = HEADS // 2
F = 2048
FPAIRS = F // 256
SCALE0 = HD ** -0.5
SCALE1 = KD ** -0.5
EPS0, EPS1 = 1e-6, 1e-5
LOG_P_TOP = float(np.log(4096.0))
Q_ORDER = (0, 0, 1, 1, 0, 2)
K_ORDER = (0, 1, 0, 1, 2, 0)
STACK = HD * len(Q_ORDER)
VW = 64

U_PROJ0, U_KV0, U_TURN = 10, LT, CT
U_OUT0 = U_TURN + LT
U_L0 = U_PROJ0 + KVH * U_KV0 + U_OUT0
U_PAIR = 28
U_LAYER = U_TURN + PAIRS * U_PAIR
U_FP = 2
U_B = U_L0 + LAYERS * U_LAYER + U_TURN + FPAIRS * U_FP
H_PAIR = 10
H_LAYER = U_TURN + PAIRS * H_PAIR
H_B = U_TURN + LAYERS * H_LAYER + U_TURN
A_B = 2 + LAYERS * PAIRS + FPAIRS
O_B = LAYERS * PAIRS + FPAIRS
STEPS0 = LT * GROUPS
STEPS = 2 * LT
PASSES = ((0, 0), (0, 1), (1, 0))


def build(nc, d):
    with ExitStack() as ctx:
        sems = {}

        def sem(name):
            sems[name] = ctx.enter_context(nc.semaphore(name))
            return sems[name]

        start = (nc.sbuf_base + 31) // 32 * 32
        at = [start]

        def sb(name, shape, dt, n=1):
            size = int(np.prod(shape[1:])) * (2 if dt in (BF16, F16) else 4)
            made = []
            for i in range(n):
                made.append(nc.alloc_sbuf_tensor_at(name if n == 1 else f"{name}{i}", shape, dt, offset=at[0]))
                at[0] += (size + 31) // 32 * 32
            return made[0] if n == 1 else made

        ctxT = sb("ctxT", [P, CT, S], F32R, 2)
        hT = sb("hT", [P, CT, L], F32R, 2)
        x_res = sb("x_res", [P, LT, D], F32)
        rows = sb("rows", [P, 3, D], F32)
        stg_a = sb("stg_a", [P, 3, CT * 256], F32)
        stg_o = sb("stg_o", [P, 2, D], F32)
        stg_bv = sb("stg_bv", [1, 256], F32)
        ident = sb("ident", [P, P], F32)
        ones = sb("ones", [1, P], F32R)
        cols = sb("cols", [P, LAYERS, 4, HEADS], F32)
        cols0 = sb("cols0", [P, 5], F32)
        colf = sb("colf", [P, F // P], F32)
        bv0 = sb("bv0", [P, P], F32)
        stats = sb("stats", [P, LT, 6], F32)
        mean_var = sb("mean_var", [P, LT, 2], F32)
        lnv = sb("lnv", [P, 5, LT], F32)
        region = at[0]

        q_stack = sb("q_stack", [STACK, NH0, L], BF16)
        k_stack = sb("k_stack", [STACK, KVH, S], BF16)
        v3 = sb("v3", [P, ST, KVH, VW], BF16)
        mask = sb("mask", [P, LT, S], F32)
        w0o = sb("w0o", [P, CT, D], F32R, 2)
        parts_at = at[0]
        a0 = sb("a0", [P, LT, D], F32)
        nm0 = sb("nm0", [P, 2], F32, 2)
        red0 = sb("red0", [P, GROUPS, HD], F32)
        rden0 = sb("rden0", [P, GROUPS], F32)
        loop0 = at[0]
        sm = sb("sm", [P, S], F32, 2)
        p0 = sb("p0", [P, S], F32, 2)
        p16 = [sb(f"p16_{i}", [P, ST, P], F16, 2) for i in range(2)]
        end0 = at[0]
        at[0] = loop0
        w0q = sb("w0q", [P, CT, D], F32R, 2)
        w0kv = sb("w0kv", [P, CT, 256], F32R, 2)
        end0 = max(end0, at[0])
        at[0] = end0
        at[0] = parts_at
        parts = sb("parts", [P, 3, 512], BF16, 2)
        at[0] = region
        st_ctx = sb("st_ctx", [P, CT, S], F32)
        st_x = sb("st_x", [P, CT, L], F32)
        st_kv = sb("st_kv", [P, CT, 256], F32)
        assert at[0] - region <= NH0 * L * 2
        at[0] = end0
        tmp0 = sb("tmp0", [P, 512], F32, 2)
        ends = [at[0]]

        at[0] = region
        wa = sb("wa", [P, 3, CT, 256], F32R, 2)
        wo = sb("wo", [P, 2, D], F32R, 2)
        kT = [sb(f"kT{h}_", [P, S], F32R, 2) for h in range(2)]
        qT = [sb(f"qT{h}_", [P, L], F32R, 2) for h in range(2)]
        v = sb("v", [P, ST, 256], F32R, 2)
        p = sb("p", [P, S], F32, 2)
        pT = [sb(f"pT{i}_", [P, ST, 256], F32R, 2) for i in range(2)]
        cT = sb("cT", [P, 2, L], F32R, 2)
        cf = sb("cf", [P, 256], F32, 2)
        pextb = sb("pextb", [P, 256], F32, 2)
        bvx = sb("bvx", [1, 256], F32R, 2)
        pcol = sb("pcol", [P, 4, 2], F32)
        bkx = sb("bkx", [P, 2, 2], F32R)
        lb = sb("lb", [P, 2, LT], F32)
        nlb = sb("nlb", [P, 2, LT], F32)
        nmx = sb("nmx", [P, STEPS], F32)
        nm = sb("nm", [P, STEPS], F32)
        pext = sb("pext", [P, STEPS], F32)
        sums = sb("sums", [P, STEPS], F32)
        z = sb("z", [P, STEPS], F32)
        r = sb("r", [P, STEPS], F32)
        ends.append(at[0])
        at[0] = region + 32768
        h_tok = sb("h_tok", [P, LT, D], F32)
        at[0] = region + 32768 + 16384
        g = sb("g", [P, L], F32, 2)
        gT = [sb(f"gT{i}_", [P, L], F32R, 2) for i in range(2)]
        assert max(ends) <= nc.sbuf_usable_end, (max(ends), nc.sbuf_usable_end)

        ps_s = [ctx.enter_context(nc.psum_tensor(f"ps_s{i}", [P, S], F32)) for i in range(2)]
        ps_t = [ctx.enter_context(nc.psum_tensor(f"ps_t{i}", [P, 512], F32)) for i in range(2)]
        ps_m = [ctx.enter_context(nc.psum_tensor(f"ps_m{i}", [P, 512], F32)) for i in range(2)]

        scr_k = nc.dram_tensor("scr_k", [2, P, 3, 512], BF16, kind="Internal").ap()
        scr_q = nc.dram_tensor("scr_q", [4, P, 3, 512], BF16, kind="Internal").ap()

        const_in = sem("const_in")
        xres_in, kv_in, ctx_in, x_in = sem("xres_in"), sem("kv_in"), sem("ctx_in"), sem("x_in")
        mask_in, rows_in = sem("mask_in"), sem("rows_in")
        a_in, o_in, bv_in = sem("a_in"), sem("o_in"), sem("bv_in")
        scr_out, stack_in = sem("scr_out"), sem("stack_in")
        out_done = sem("out_done")
        const_made = sem("const_made")
        ones_made = sem("ones_made")
        in_hi, in_lo, kv_lo = sem("in_hi"), sem("in_lo"), sem("kv_lo")
        wa_hi, wa_lo = sem("wa_hi"), sem("wa_lo")
        wo_hi, wo_lo = sem("wo_hi"), sem("wo_lo")
        bv_hi, bv_lo = sem("bv_hi"), sem("bv_lo")
        bank_filled = sem("bank_filled")
        bank_free = sem("bank_free")
        hi_done = sem("hi_done")
        part_done = sem("part_done")
        v3_done = sem("v3_done")
        s0_filled, max0_done, exp0_done = sem("s0_filled"), sem("max0_done"), sem("exp0_done")
        t0_filled, t0_hi, t0_lo = sem("t0_filled"), sem("t0_hi"), sem("t0_lo")
        pv0_done = sem("pv0_done")
        a0_done = sem("a0_done")
        l0_done = sem("l0_done")
        rows_used = sem("rows_used")
        var_done, sqrt_done, ln_done = sem("var_done"), sem("sqrt_done"), sem("ln_done")
        col_done = sem("col_done")
        lb_done = sem("lb_done")
        s_filled, nm_done, exp_done = sem("s_filled"), sem("nm_done"), sem("exp_done")
        t_filled, t_hi, t_lo = sem("t_filled"), sem("t_hi"), sem("t_lo")
        px_copied, cf_done, c_hi, c_lo = sem("px_copied"), sem("cf_done"), sem("c_hi"), sem("c_lo")
        gelu_done, g_hi, g_lo = sem("gelu_done"), sem("g_hi"), sem("g_lo")
        mlp_acc, out_ready, batch_done = sem("mlp_acc"), sem("out_ready"), sem("batch_done")
        apart_sp, apart_pe, apart_dve = sem("apart_sp"), sem("apart_pe"), sem("apart_dve")
        dve_step = sem("dve_step")

        block = ctx.enter_context(nc.Block())

        def f32(t):
            return t.bitcast(F32)

        @block.sync
        def _(sp):
            for dst, name in ((cols, "cols"), (cols0, "cols0"), (colf, "colf"), (bv0, "bv0")):
                src = d[name]
                sp.dma_start(dst[:], src.partition_broadcast(P) if name == "bv0" else src).then_inc(const_in, 16)

            def apart():
                sp.sem_inc(apart_sp, 1)

            def load_rows(k, group):
                sp.wait_ge(rows_used, k + 1)
                sp.dma_start(rows[:], group.partition_broadcast(P)).then_inc(rows_in, 16)

            def load_a(use, dst, src):
                sp.wait_ge(wa_lo, 3 * use + 3)
                sp.dma_start(dst, src).then_inc(a_in, 16)

            def load_o(use, src):
                sp.wait_ge(wo_lo, use + 1)
                sp.dma_start(stg_o[:], src).then_inc(o_in, 16)

            with sp.Fori(0, B) as b:
                sp.wait_ge(batch_done, b + 1)
                sp.dma_start(st_kv[:], d["w0kv"]).then_inc(kv_in, 16)
                sp.dma_start(st_ctx[:], d["ctxT"][b, :, :, :]).then_inc(ctx_in, 16)
                sp.dma_start(st_x[:], d["xT"][b, :, :, :]).then_inc(x_in, 16)
                load_a(b * A_B, stg_a[:, 0:2, :], d["w0q"])
                sp.dma_start(mask[:], d["mask"][b, :, :, :]).then_inc(mask_in, 16)
                sp.dma_start(x_res[:], d["x"][b, :, :, :]).then_inc(xres_in, 16)
                load_rows(b * 4, d["rows"][0, :, :])
                load_a(b * A_B + 1, stg_a[:, 0:2, :], d["w0o"])
                for i in range(6):
                    sp.wait_ge(part_done, b * 6 + i + 1)
                    scr = scr_k[i, :, :, :] if i < 2 else scr_q[i - 2, :, :, :]
                    sp.dma_start(scr, parts[i % 2][:]).then_inc(scr_out, 16)
                    sp.wait_ge(scr_out, 16 * (b * 6 + i + 1))
                    apart()
                    if i == 2:
                        sp.wait_ge(in_lo, (b + 1) * (CT + 1))
                        sp.wait_ge(kv_lo, b + 1)
                    for j in range(len(Q_ORDER)):
                        part = (K_ORDER if i < 2 else Q_ORDER)[j]
                        rows_j = slice(HD * j, HD * j + HD)
                        dst = (k_stack[rows_j, :, i * 512:(i + 1) * 512] if i < 2 else
                               q_stack[rows_j, (i - 2) * 8:(i - 1) * 8, :])
                        src = scr[:, part, :].rearrange("(a e) n -> e a n", e=HD)
                        sp.dma_start(dst, src).then_inc(stack_in, 16)
                with sp.Fori(0, LAYERS) as y:
                    load_rows(b * 4 + 1 + y, d["rows"][y + 1, :, :])
                    with sp.Fori(0, PAIRS) as pr:
                        load_a(b * A_B + 2 + y * PAIRS + pr, stg_a[:], d["wqkv"][y * PAIRS + pr, :, :, :])
                        load_o(b * O_B + y * PAIRS + pr, d["wo"][y * PAIRS + pr, :, :, :])
                        sp.wait_ge(bv_lo, (b * LAYERS + y) * PAIRS + pr + 1)
                        sp.dma_start(stg_bv[:], d["bv"][y * PAIRS + pr, :, :]).then_inc(bv_in, 16)
                load_rows(b * 4 + 3, d["rows"][3, :, :])
                with sp.Fori(0, FPAIRS) as fp:
                    load_a(b * A_B + 2 + LAYERS * PAIRS + fp, stg_a[:, 0, :], d["w1"][fp, :, :])
                    load_o(b * O_B + LAYERS * PAIRS + fp, d["w2"][fp, :, :, :])
                for lt in range(LT):
                    sp.wait_ge(out_ready, b * LT + lt + 1)
                    sp.dma_start(d["out"][b, :, lt, :], x_res[:, lt, :]).then_inc(out_done, 16)
                sp.wait_ge(out_done, 16 * LT * (b + 1))
                apart()

        @block.gpsimd
        def _(pool):
            nc.gpsimd.memset(ident[:], 0.0).then_inc(const_made, 1)
            pool.wait_ge(const_made, 1)
            nc.gpsimd.affine_select(out=ident[:], in_=ident[:], compare_op=ALU.not_equal, fill=1.0, base=0,
                                    pattern=[[-1, P]], channel_multiplier=1).then_inc(const_made, 1)
            pool.sem_inc(wa_lo, 3)
            pool.sem_inc(wo_lo, 1)

            def lo_a(count, slots, inc):
                pool.wait_ge(wa_hi, count)
                flat = [w[:].rearrange("p s c n -> p s (c n)") for w in wa]
                nc.gpsimd.tensor_tensor(flat[1][:, slots, :], stg_a[:, slots, :], f32(flat[0][:, slots, :]),
                                        ALU.subtract).then_inc(wa_lo, inc)

            def lo_o(use):
                pool.wait_ge(wo_hi, use + 1)
                nc.gpsimd.tensor_tensor(wo[1][:], stg_o[:], f32(wo[0][:]), ALU.subtract).then_inc(wo_lo, 1)

            def lo_w0(use, w):
                pool.wait_ge(wa_hi, 3 * use + 3)
                flat = [t[:].rearrange("p (s c) n -> p s (c n)", s=2) for t in w]
                nc.gpsimd.tensor_tensor(flat[1], stg_a[:, 0:2, :], f32(flat[0]), ALU.subtract).then_inc(wa_lo, 3)

            with pool.Fori(0, B) as b:
                pool.wait_ge(in_hi, b * (CT + 2) + 1)
                nc.gpsimd.tensor_tensor(w0kv[1][:], st_kv[:], f32(w0kv[0][:]), ALU.subtract).then_inc(kv_lo, 1)
                lo_w0(b * A_B, w0q)
                lo_w0(b * A_B + 1, w0o)
                for s in range(3):
                    lo_a((b * A_B + 2) * 3 + s + 1, s, 1)
                with pool.Fori(0, LAYERS * PAIRS) as it:
                    lo_o(b * O_B + it)
                    for s in range(3):
                        lo_a((b * A_B + 3 + it) * 3 + s + 1, s, 1)
                with pool.Fori(0, FPAIRS - 1) as fp:
                    lo_o(b * O_B + LAYERS * PAIRS + fp)
                    lo_a((b * A_B + 3 + LAYERS * PAIRS + fp) * 3 + 3, 0, 3)
                lo_o(b * O_B + O_B - 1)

        @block.scalar
        def _(act):
            def copy(out, in_):
                return nc.scalar.activation(out, in_, ACT.Copy)

            def split_w0(use, w):
                act.wait_ge(a_in, 16 * (use + 1))
                copy(w[0][:].rearrange("p (s c) n -> p s (c n)", s=2), stg_a[:, 0:2, :]).then_inc(wa_hi, 3)

            def split_a(use, slots):
                act.wait_ge(a_in, 16 * (use + 1))
                for s in slots:
                    copy(wa[0][:, s].rearrange("p c n -> p (c n)"), stg_a[:, s, :]).then_inc(wa_hi, 3 // len(slots))

            def split_o(use):
                act.wait_ge(o_in, 16 * (use + 1))
                copy(wo[0][:], stg_o[:]).then_inc(wo_hi, 1)

            def hi_bank(n, out, bias=None, in_=None):
                act.wait_ge(bank_filled, n + 1)
                src = ps_m[n_par(n)][:] if in_ is None else in_
                if bias is None:
                    return copy(out, src)
                return nc.scalar.activation(out, src, ACT.Identity, bias=bias)

            def turn_hi(n0):
                for c in range(CT):
                    act.wait_ge(bank_filled, n0 + c + 1)
                    copy(hT[0][:, c, :], ps_m[c % 2][:]).then_inc(hi_done, 1)

            def n_par(n):
                return n % 2

            def root(k):
                act.wait_ge(var_done, k + 1)
                nc.scalar.activation(lnv[:, 1, :], lnv[:, 0, :], ACT.Sqrt).then_inc(sqrt_done, 1)

            with act.Fori(0, B) as b:
                act.wait_ge(kv_in, 16 * (b + 1))
                copy(w0kv[0][:], st_kv[:]).then_inc(in_hi, 1)
                act.wait_ge(ctx_in, 16 * (b + 1))
                for c in range(CT):
                    copy(ctxT[0][:, c, :], st_ctx[:, c, :]).then_inc(in_hi, 1)
                act.wait_ge(x_in, 16 * (b + 1))
                copy(hT[0][:], st_x[:]).then_inc(in_hi, 1)
                split_w0(b * A_B, w0q)
                split_w0(b * A_B + 1, w0o)

                with act.Fori(0, KVH) as kv:
                    t0 = (b * KVH + kv) * STEPS0

                    def exp0(t):
                        act.wait_ge(max0_done, t0 + t + 1)
                        nc.scalar.activation(p0[t % 2][:], sm[t % 2][:], ACT.Exp,
                                             bias=nm0[1][:, t % 2:t % 2 + 1]).then_inc(exp0_done, 1)

                    exp0(0)
                    exp0(1)
                    for t in range(STEPS0):
                        act.wait_ge(pv0_done, t0 + t + 1)
                        for q in range(2):
                            act.wait_ge(t0_filled, 2 * (t0 + t) + q + 1)
                            copy(p16[t % 2][0][:, 4 * q:4 * q + 4, :],
                                 ps_t[q][:].rearrange("p (s n) -> p s n", s=4)).then_inc(t0_hi, 1)
                        if t + 2 < STEPS0:
                            exp0(t + 2)
                turn_hi(b * U_B + U_PROJ0 + KVH * U_KV0)
                root(b * 4)
                act.wait_ge(l0_done, b + 1)
                split_a(b * A_B + 2, range(3))

                with act.Fori(0, LAYERS) as y:
                    root(b * 4 + 1 + y)
                    turn_hi(b * U_B + U_L0 + y * U_LAYER)
                    with act.Fori(0, PAIRS) as pr:
                        it = (b * LAYERS + y) * PAIRS + pr
                        n0 = b * U_B + U_L0 + y * U_LAYER + U_TURN + pr * U_PAIR
                        T = it * STEPS

                        def qk(n, out, col):
                            act.wait_ge(bank_filled, n0 + n + 1)
                            nc.scalar.activation(out, ps_m[n % 2][:], ACT.Identity, bias=col).then_inc(hi_done, 1)

                        def exp(t):
                            h, lt = divmod(t, LT)
                            act.wait_ge(nm_done, T + t + 1)
                            nc.scalar.activation(pext[:, t:t + 1], lb[:, h, lt:lt + 1], ACT.Exp,
                                                 bias=nm[:, t:t + 1], scale=SCALE1)
                            nc.scalar.activation(p[t % 2][:], ps_s[t % 2][:], ACT.Exp, bias=nm[:, t:t + 1],
                                                 scale=SCALE1, accum_out=sums[:, t:t + 1]).then_inc(exp_done, 1)

                        def turned(t):
                            j, off = t // 2, (t % 2) * P
                            for q in range(2):
                                act.wait_ge(t_filled, 2 * (T + t) + q + 1)
                                copy(pT[j % 2][0][:, 4 * q:4 * q + 4, off:off + P],
                                     ps_t[q][:].rearrange("p (s n) -> p s n", s=4)).then_inc(t_hi, 1)

                        def px_copy(j):
                            n = PX[j]
                            act.wait_ge(bank_filled, n0 + n + 1)
                            copy(pextb[j % 2][:], ps_m[n % 2][:, 0:256]).then_inc(px_copied, 1)

                        def ctx_hi(j):
                            act.wait_ge(cf_done, 4 * it + j + 1)
                            h, off = j // 2, (j % 2) * 256
                            copy(cT[0][:, h, off:off + 256], cf[j % 2][:]).then_inc(c_hi, 1)

                        act.wait_ge(col_done, it + 1)
                        qk(0, qT[0][0][:], pcol[:, 0, 0:1])
                        qk(1, kT[0][0][:, 0:512], pcol[:, 1, 0:1])
                        qk(2, kT[0][0][:, 512:1024], pcol[:, 1, 0:1])
                        act.wait_ge(bv_in, 16 * (it + 1))
                        copy(bvx[0][:], stg_bv[:]).then_inc(bv_hi, 1)
                        qk(4, qT[1][0][:], pcol[:, 0, 1:2])
                        exp(0)
                        qk(5, kT[1][0][:, 0:512], pcol[:, 1, 1:2])
                        exp(1)
                        qk(6, kT[1][0][:, 512:1024], pcol[:, 1, 1:2])
                        for i in range(4):
                            act.wait_ge(bank_filled, n0 + 8 + i + 1)
                            copy(v[0][:, 2 * i:2 * i + 2, :],
                                 ps_m[i % 2][:].rearrange("p (s n) -> p s n", s=2)).then_inc(hi_done, 1)
                        split_o(b * O_B + y * PAIRS + pr)
                        for t in range(STEPS):
                            turned(t)
                            if t + 2 < STEPS:
                                exp(t + 2)
                            if t % 2 == 0 and t >= 2:
                                px_copy(t // 2 - 1)
                            if t % 2 == 1 and t >= 3:
                                ctx_hi((t - 3) // 2)
                            if 2 <= t <= 4:
                                act.wait_ge(a_in, 16 * (b * A_B + 3 + y * PAIRS + pr + 1))
                                copy(wa[0][:, t - 2].rearrange("p c n -> p (c n)"),
                                     stg_a[:, t - 2, :]).then_inc(wa_hi, 1)
                        px_copy(3)
                        ctx_hi(3)

                root(b * 4 + 3)
                n_mlp = b * U_B + U_L0 + LAYERS * U_LAYER
                turn_hi(n_mlp)

                def mlp(fp, last):
                    n0 = n_mlp + U_TURN + fp * U_FP
                    for i in range(2):
                        k = (b * FPAIRS + fp) * 2 + i
                        act.wait_ge(bank_filled, n0 + i + 1)
                        nc.scalar.activation(g[i][:], ps_m[i][:], ACT.Gelu,
                                             bias=colf[:, bass.ds(fp * 2 + i, 1)]).then_inc(gelu_done, 1)
                        act.wait_ge(gelu_done, k + 1)
                        copy(gT[i][0][:], g[i][:]).then_inc(g_hi, 1)
                        if i == 0:
                            split_o(b * O_B + LAYERS * PAIRS + fp)
                    if not last:
                        split_a(b * A_B + 3 + LAYERS * PAIRS + fp, range(1))

                with act.Fori(0, FPAIRS - 1) as fp:
                    mlp(fp, False)
                mlp(FPAIRS - 1, True)

        @block.tensor
        def _(pe):
            def passes(out, lhs, rhs, start=True, stop=True):
                n_tiles = lhs[2]
                for c in range(n_tiles):
                    for i, (x, y) in enumerate(PASSES):
                        mm = nc.tensor.matmul(out, lhs[0](x, c), rhs(y, c), start=start and c == 0 and i == 0,
                                              stop=stop and c == n_tiles - 1 and i == 2)
                return mm

            def free(n):
                pe.wait_ge(bank_free, n + 1)

            def drained(n):
                pe.wait_ge(bank_free, n + 3)

            def turn(n0, src):
                for c in range(CT):
                    free(n0 + c)
                    for lt in range(LT):
                        mm = nc.tensor.transpose(ps_m[c % 2][:, lt * P:(lt + 1) * P], src[:, lt, c * P:(c + 1) * P],
                                                 ident[:])
                    mm.then_inc(bank_filled, 1)

            def apart():
                pe.sem_inc(apart_pe, 1)

            pe.wait_ge(const_made, 2)
            pe.wait_ge(ones_made, 1)
            pe.sem_inc(pv0_done, 2)
            with pe.Fori(0, B) as b:
                nb = b * U_B
                pe.wait_ge(kv_lo, b + 1)
                pe.wait_ge(in_lo, b * (CT + 1) + CT)
                for i in range(2):
                    free(nb + i)
                    passes(ps_m[i][:], (lambda x, c: w0kv[x][:, c, 0:P], None, CT),
                           lambda y, c: ctxT[y][:, c, i * 512:(i + 1) * 512]).then_inc(bank_filled, 1)
                for i in range(4):
                    free(nb + 2 + i)
                    for s in range(2):
                        st = 2 * i + s
                        mm = passes(ps_m[i % 2][:, s * 256:(s + 1) * 256],
                                    (lambda x, c: ctxT[x][:, c, st * P:(st + 1) * P], None, CT),
                                    lambda y, c: w0kv[y][:, c, :])
                    mm.then_inc(bank_filled, 1)
                pe.wait_ge(in_lo, (b + 1) * (CT + 1))
                pe.wait_ge(wa_lo, 3 * (b * A_B) + 6)
                for i in range(4):
                    free(nb + 6 + i)
                    passes(ps_m[i % 2][:], (lambda x, c: w0q[x][:, c, i * P:(i + 1) * P], None, CT),
                           lambda y, c: hT[y][:, c, :]).then_inc(bank_filled, 1)

                pe.wait_ge(stack_in, 16 * 36 * (b + 1))
                pe.wait_ge(v3_done, b * 5 + 5)
                apart()
                with pe.Fori(0, KVH) as kv:
                    t0 = (b * KVH + kv) * STEPS0
                    n0 = nb + U_PROJ0 + kv * U_KV0

                    def scores(t):
                        lt, gr = divmod(t, GROUPS)
                        for n in range(2):
                            mm = nc.tensor.matmul(ps_s[t % 2][:, n * 512:(n + 1) * 512],
                                                  q_stack[:, bass.ds(kv * GROUPS + gr, 1), lt * P:(lt + 1) * P],
                                                  k_stack[:, bass.ds(kv, 1), n * 512:(n + 1) * 512],
                                                  start=True, stop=True)
                        mm.then_inc(s0_filled, 1)

                    def values(t):
                        lt, gr = divmod(t, GROUPS)
                        if gr == 0:
                            free(n0 + lt)
                        pe.wait_ge(t0_lo, 2 * (t0 + t + 1) + 2)
                        for st in range(ST):
                            for x in range(2):
                                mm = nc.tensor.matmul(ps_m[lt % 2][:, gr * VW:gr * VW + 49], p16[t % 2][x][:, st, :],
                                                      v3[:, st, bass.ds(kv, 1), 0:49],
                                                      start=st == 0 and x == 0, stop=st == ST - 1 and x == 1)
                        mm.then_inc(pv0_done, 1)
                        if gr == GROUPS - 1:
                            pe.wait_ge(pv0_done, t0 + t + 1 + 2)
                            pe.sem_inc(bank_filled, 1)

                    scores(0)
                    scores(1)
                    for t in range(STEPS0):
                        pe.wait_ge(exp0_done, t0 + t + 1)
                        for q in range(2):
                            pe.wait_ge(t0_lo, 2 * (t0 + t) + q + 1)
                            for s in range(4):
                                st = 4 * q + s
                                mm = nc.tensor.transpose(ps_t[q][:, s * P:(s + 1) * P],
                                                         p0[t % 2][:, st * P:(st + 1) * P], ident[:])
                            mm.then_inc(t0_filled, 1)
                        if t + 2 < STEPS0:
                            scores(t + 2)
                        if t:
                            values(t - 1)
                    values(STEPS0 - 1)
                n0 = nb + U_PROJ0 + KVH * U_KV0
                pe.wait_ge(a0_done, KVH * LT * (b + 1))
                turn(n0, a0)
                drained(n0 + U_TURN - 1)
                pe.wait_ge(wa_lo, 3 * (b * A_B + 1) + 6)
                for lt in range(LT):
                    free(n0 + U_TURN + lt)
                    passes(ps_m[lt % 2][:], (lambda x, c: hT[x][:, c, lt * P:(lt + 1) * P], None, CT),
                           lambda y, c: w0o[y][:, c, :]).then_inc(bank_filled, 1)

                with pe.Fori(0, LAYERS) as y:
                    ny = nb + U_L0 + y * U_LAYER
                    pe.wait_ge(ln_done, b * 4 + 2 + y)
                    turn(ny, h_tok)
                    drained(ny + U_TURN - 1)
                    apart()
                    with pe.Fori(0, PAIRS) as pr:
                        it = (b * LAYERS + y) * PAIRS + pr
                        n0 = ny + U_TURN + pr * U_PAIR
                        T = it * STEPS
                        w_done = 3 * (b * A_B + 2 + y * PAIRS + pr) + 3

                        def project(n, slot, h, src, tokens):
                            free(n0 + n)
                            passes(ps_m[n % 2][:], (lambda x, c: wa[x][:, slot, c, h * P:(h + 1) * P], None, CT),
                                   lambda q, c: src[q][:, c, tokens]).then_inc(bank_filled, 1)

                        def extra_logits(h):
                            n = 3 + 4 * h
                            free(n0 + n)
                            drained(n0 + 4 * h)
                            for lt in range(LT):
                                for x in range(2):
                                    mm = nc.tensor.matmul(ps_m[n % 2][:, 2 * lt:2 * lt + 2],
                                                          qT[h][x][:, lt * P:(lt + 1) * P], bkx[:, h, :],
                                                          start=x == 0, stop=x == 1)
                            mm.then_inc(bank_filled, 1)

                        def scores(t):
                            h, lt = divmod(t, LT)
                            if lt == 0:
                                drained(n0 + 4 * h + 2)
                            for n in range(2):
                                for i, (x, q) in enumerate(PASSES):
                                    mm = nc.tensor.matmul(ps_s[t % 2][:, n * 512:(n + 1) * 512],
                                                          qT[h][x][:, lt * P:(lt + 1) * P],
                                                          kT[h][q][:, n * 512:(n + 1) * 512],
                                                          start=i == 0, stop=i == 2)
                            mm.then_inc(s_filled, 1)

                        def values(j):
                            h = j // 2
                            n = PX[j]
                            free(n0 + n)
                            for s in range(2):
                                t = 2 * j + s
                                mm = nc.tensor.transpose(ps_m[n % 2][:, s * P:(s + 1) * P],
                                                         pext[:, t:t + 1].to_broadcast([P, P]), ident[:])
                            mm.then_inc(bank_filled, 1)
                            n += 1
                            free(n0 + n)
                            if j == 0:
                                drained(n0 + 11)
                            pe.wait_ge(t_lo, 2 * (T + 2 * j + 2) + 2)
                            out = ps_m[n % 2][:, 0:256]
                            passes(out, (lambda x, st: v[x][:, st, h * P:(h + 1) * P], None, ST),
                                   lambda q, st: pT[j % 2][q][:, st, :]).then_inc(bank_filled, 1)

                        def output(h):
                            pe.wait_ge(c_lo, 4 * it + 2 * h + 2)
                            if h == 0:
                                pe.wait_ge(wo_lo, b * O_B + y * PAIRS + pr + 2)
                            for lt in range(LT):
                                n = OUT[h] + lt
                                free(n0 + n)
                                passes(ps_m[n % 2][:], (lambda x, c: cT[x][:, h, lt * P:(lt + 1) * P], None, 1),
                                       lambda q, c: wo[q][:, h, :]).then_inc(bank_filled, 1)

                        pe.wait_ge(col_done, it + 1)
                        pe.wait_ge(wa_lo, w_done + 1)
                        project(0, 0, 0, hT, slice(0, L))
                        pe.wait_ge(wa_lo, w_done + 2)
                        project(1, 1, 0, ctxT, slice(0, 512))
                        project(2, 1, 0, ctxT, slice(512, 1024))
                        extra_logits(0)
                        project(4, 0, 1, hT, slice(0, L))
                        scores(0)
                        scores(1)
                        project(5, 1, 1, ctxT, slice(0, 512))
                        project(6, 1, 1, ctxT, slice(512, 1024))
                        extra_logits(1)
                        pe.wait_ge(wa_lo, w_done + 3)
                        pe.wait_ge(bv_lo, it + 2)
                        for i in range(4):
                            free(n0 + 8 + i)
                            for s in range(2):
                                st = 2 * i + s
                                out = ps_m[i % 2][:, s * 256:(s + 1) * 256]
                                for x in range(2):
                                    nc.tensor.matmul(out, ones[:], bvx[x][:], start=x == 0, stop=False)
                                mm = passes(out, (lambda x, c: ctxT[x][:, c, st * P:(st + 1) * P], None, CT),
                                            lambda q, c: wa[q][:, 2, c, :], start=False)
                            mm.then_inc(bank_filled, 1)
                        for t in range(STEPS):
                            pe.wait_ge(exp_done, T + t + 1)
                            for q in range(2):
                                pe.wait_ge(t_lo, 2 * (T + t) + q + 1)
                                for s in range(4):
                                    st = 4 * q + s
                                    mm = nc.tensor.transpose(ps_t[q][:, s * P:(s + 1) * P],
                                                             p[t % 2][:, st * P:(st + 1) * P], ident[:])
                                mm.then_inc(t_filled, 1)
                            if t + 2 < STEPS:
                                scores(t + 2)
                            if t % 2 == 0 and t >= 2:
                                values(t // 2 - 1)
                            if t == 6:
                                output(0)
                        values(3)
                        output(1)

                n_mlp = nb + U_L0 + LAYERS * U_LAYER
                pe.wait_ge(ln_done, b * 4 + 4)
                turn(n_mlp, h_tok)
                drained(n_mlp + U_TURN - 1)
                apart()

                def mlp(fp, first, last):
                    n0 = n_mlp + U_TURN + fp * U_FP
                    pe.wait_ge(wa_lo, 3 * (b * A_B + 2 + LAYERS * PAIRS + fp) + 6)
                    for i in range(2):
                        free(n0 + i)
                        passes(ps_m[i][:], (lambda x, c: wa[x][:, 0, c, i * P:(i + 1) * P], None, CT),
                               lambda q, c: hT[q][:, c, :]).then_inc(bank_filled, 1)
                    pe.wait_ge(wo_lo, b * O_B + LAYERS * PAIRS + fp + 2)
                    for i in range(2):
                        drained(n0 + i)
                        for lt in range(LT):
                            mm = passes(ps_s[lt // 2][:, (lt % 2) * 512:(lt % 2 + 1) * 512],
                                        (lambda x, c: gT[i][x][:, lt * P:(lt + 1) * P], None, 1),
                                        lambda q, c: wo[q][:, i, :], start=first and i == 0, stop=last and i == 1)
                    return mm

                mlp(0, True, False)
                with pe.Fori(1, FPAIRS - 1) as fp:
                    mlp(fp, False, False)
                mlp(FPAIRS - 1, False, True).then_inc(mlp_acc, 1)

        @block.vector
        def _(dve):
            step = [0, 0]

            def link(ins):
                step[1] += 1
                ins.then_inc(dve_step, 1)
                dve.wait_ge(dve_step, step[0] + step[1])

            def apart():
                dve.sem_inc(apart_dve, 1)

            def section(start, count=None):
                if count is not None:
                    assert step[1] == count, (step[1], count)
                step[0], step[1] = start, 0

            sub = ALU.subtract
            nc.vector.memset(ones[:].bitcast(F32), 1.0).then_inc(ones_made, 1)
            dve.sem_inc(bank_free, 2)
            dve.sem_inc(t0_lo, 2)
            dve.sem_inc(t_lo, 2)
            dve.sem_inc(rows_used, 1)
            dve.sem_inc(bv_lo, 1)
            dve.sem_inc(batch_done, 1)
            dve.wait_ge(const_in, 16 * 4)

            def turn_lo(n0, h0):
                for c in range(CT):
                    dve.wait_ge(hi_done, h0 + c + 1)
                    nc.vector.tensor_tensor(hT[1][:, c, :], ps_m[c % 2][:], f32(hT[0][:, c, :]), sub)\
                        .then_inc(bank_free, 1)

            def norm(k, eps, out):
                for lt in range(LT):
                    link(nc.vector.bn_stats(stats[:, lt, :], x_res[:, lt, :]))
                apart()
                for lt in range(LT):
                    link(nc.vector.bn_aggr(mean_var[:, lt, :], stats[:, lt, :]))
                    if lt < LT - 1:
                        apart()
                nc.vector.tensor_scalar(lnv[:, 0, :], mean_var[:, :, 1], eps, None, ALU.add).then_inc(var_done, 1)
                dve.wait_ge(sqrt_done, k + 1)
                link(nc.vector.reciprocal(lnv[:, 2, :], lnv[:, 1, :]))
                link(nc.vector.tensor_tensor(lnv[:, 2, :], lnv[:, 2, :], lnv[:, 0, :], ALU.mult))
                link(nc.vector.tensor_tensor(lnv[:, 3, :], lnv[:, 2, :], lnv[:, 1, :], ALU.add))
                link(nc.vector.reciprocal(lnv[:, 4, :], lnv[:, 3, :]))
                link(nc.vector.tensor_scalar(lnv[:, 4, :], lnv[:, 4, :], 2.0, None, ALU.mult))
                dve.wait_ge(rows_in, 16 * (k + 1))
                for lt in range(LT):
                    link(nc.vector.tensor_scalar(out[:, lt, :], x_res[:, lt, :], mean_var[:, lt, 0:1],
                                                 lnv[:, 4, lt:lt + 1], sub, ALU.mult))
                    link(nc.vector.tensor_tensor(out[:, lt, :], out[:, lt, :], rows[:, 0, :], ALU.mult))
                    link(nc.vector.tensor_tensor(out[:, lt, :], out[:, lt, :], rows[:, 1, :], ALU.add))

            def add_row2():
                for lt in range(LT):
                    link(nc.vector.tensor_tensor(x_res[:, lt, :], x_res[:, lt, :], rows[:, 2, :], ALU.add))

            with dve.Fori(0, B) as b:
                nb, hb, sb_ = b * U_B, b * H_B, b * DVE_B
                section(sb_)
                for c in range(CT):
                    dve.wait_ge(in_hi, b * (CT + 2) + 1 + c + 1)
                    nc.vector.tensor_tensor(ctxT[1][:, c, :], st_ctx[:, c, :], f32(ctxT[0][:, c, :]), sub)\
                        .then_inc(in_lo, 1)
                dve.wait_ge(in_hi, (b + 1) * (CT + 2))
                nc.vector.tensor_tensor(hT[1][:], st_x[:], f32(hT[0][:]), sub).then_inc(in_lo, 1)

                def three_parts(i, n, col, scale):
                    dve.wait_ge(bank_filled, nb + n + 1)
                    t, u = tmp0[0][:], tmp0[1][:]
                    link(nc.vector.tensor_scalar(t, ps_m[n % 2][:], col, scale, ALU.add, ALU.mult))
                    dve.sem_inc(bank_free, 1)
                    if i >= 2:
                        dve.wait_ge(scr_out, 16 * (b * 6 + i - 1))
                    part = parts[i % 2]
                    link(nc.vector.tensor_copy(part[:, 0, :], t))
                    link(nc.vector.tensor_tensor(u, t, part[:, 0, :], sub))
                    link(nc.vector.tensor_copy(part[:, 1, :], u))
                    nc.vector.tensor_tensor(part[:, 2, :], u, part[:, 1, :], sub).then_inc(part_done, 1)
                    dve.wait_ge(part_done, b * 6 + i + 1)

                for i in range(2):
                    three_parts(i, i, cols0[:, 4:5], 1.0)
                nc.vector.memset(v3[:, :, :, 48:49], 1.0).then_inc(v3_done, 1)
                for i in range(4):
                    dve.wait_ge(bank_filled, nb + 2 + i + 1)
                    t = tmp0[0][:, 0:256].rearrange("p (s n) -> p s n", s=2)
                    link(nc.vector.tensor_tensor(t, ps_m[i % 2][:].rearrange("p (s n) -> p s n", s=2)[:, :, P:256],
                                                 bv0[:].unsqueeze(1).to_broadcast([P, 2, P]), ALU.add))
                    dve.sem_inc(bank_free, 1)
                    t = tmp0[0][:, 0:256].rearrange("p (s a e) -> p s a e", s=2, e=HD)
                    u = tmp0[1][:, 0:256].rearrange("p (s a e) -> p s a e", s=2, e=HD)
                    dst = [v3[:, 2 * i:2 * i + 2, :, x * HD:(x + 1) * HD] for x in range(3)]
                    link(nc.vector.tensor_copy(dst[0], t))
                    link(nc.vector.tensor_tensor(u, t, dst[0], sub))
                    link(nc.vector.tensor_copy(dst[1], u))
                    nc.vector.tensor_tensor(dst[2], u, dst[1], sub).then_inc(v3_done, 1)
                    dve.wait_ge(v3_done, b * 5 + i + 2)
                for i in range(4):
                    three_parts(2 + i, 6 + i, cols0[:, i:i + 1], SCALE0)

                dve.wait_ge(mask_in, 16 * (b + 1))
                apart()
                with dve.Fori(0, KVH) as kv:
                    t0 = (b * KVH + kv) * STEPS0
                    n0 = nb + U_PROJ0 + kv * U_KV0
                    section(sb_ + DVE_PROJ0 + kv * DVE_KV0, DVE_PROJ0)

                    def maxima(t):
                        lt, i = t // GROUPS, t % 2
                        dve.wait_ge(s0_filled, t0 + t + 1)
                        apart()
                        link(nc.vector.tensor_tensor_reduce(sm[i][:], ps_s[i][:], mask[:, lt, :], 1.0, -3.0e38,
                                                            ALU.add, ALU.max, nm0[0][:, i:i + 1]))
                        nc.vector.tensor_scalar(nm0[1][:, i:i + 1], nm0[0][:, i:i + 1], -1.0, LOG_P_TOP,
                                                ALU.mult, ALU.add).then_inc(max0_done, 1)

                    def normalised(lt):
                        dve.wait_ge(bank_filled, n0 + lt + 1)
                        out = ps_m[lt % 2][:, 0:GROUPS * VW].rearrange("p (g w) -> p g w", w=VW)
                        nc.vector.reciprocal(rden0[:], out[:, :, 48])
                        link(nc.vector.tensor_reduce(red0[:], out[:, :, 0:48].rearrange("p g (x e) -> p g e x", x=3),
                                                     AX.X, ALU.add))
                        dve.sem_inc(bank_free, 1)
                        dst = a0[:, lt, bass.ds(kv * GROUPS * HD, GROUPS * HD)].rearrange("p (g e) -> p g e", g=GROUPS)
                        nc.vector.tensor_tensor(dst, red0[:], rden0[:].unsqueeze(2).to_broadcast([P, GROUPS, HD]),
                                                ALU.mult).then_inc(a0_done, 1)

                    maxima(0)
                    maxima(1)
                    for t in range(STEPS0):
                        for q in range(2):
                            dve.wait_ge(t0_hi, 2 * (t0 + t) + q + 1)
                            part = p16[t % 2]
                            nc.vector.tensor_tensor(part[1][:, 4 * q:4 * q + 4, :],
                                                    ps_t[q][:].rearrange("p (s n) -> p s n", s=4),
                                                    part[0][:, 4 * q:4 * q + 4, :], sub).then_inc(t0_lo, 1)
                        if t + 2 < STEPS0:
                            maxima(t + 2)
                        if t % GROUPS == 1 and t > GROUPS:
                            normalised(t // GROUPS - 1)
                    normalised(LT - 1)
                section(sb_ + DVE_PROJ0 + KVH * DVE_KV0, DVE_KV0)
                n0 = nb + U_PROJ0 + KVH * U_KV0
                turn_lo(n0, hb)
                dve.wait_ge(xres_in, 16 * (b + 1))
                dve.wait_ge(rows_in, 16 * (b * 4 + 1))
                for lt in range(LT):
                    dve.wait_ge(bank_filled, n0 + U_TURN + lt + 1)
                    link(nc.vector.tensor_tensor(x_res[:, lt, :], ps_m[lt % 2][:], x_res[:, lt, :], ALU.add))
                    dve.sem_inc(bank_free, 1)
                add_row2()
                norm(b * 4, EPS0, x_res)
                dve.sem_inc(rows_used, 1)
                dve.sem_inc(ln_done, 1)
                dve.sem_inc(l0_done, 1)

                with dve.Fori(0, LAYERS) as y:
                    ny, hy = nb + U_L0 + y * U_LAYER, hb + U_TURN + y * H_LAYER
                    s_y = sb_ + DVE_PROJ0 + KVH * DVE_KV0 + DVE_OUT0 + y * DVE_LAYER
                    section(s_y, DVE_OUT0)
                    norm(b * 4 + 1 + y, EPS1, h_tok)
                    dve.sem_inc(ln_done, 1)
                    add_row2()
                    dve.sem_inc(rows_used, 1)
                    turn_lo(ny, hy)
                    with dve.Fori(0, PAIRS) as pr:
                        it = (b * LAYERS + y) * PAIRS + pr
                        n0 = ny + U_TURN + pr * U_PAIR
                        h0 = hy + U_TURN + pr * H_PAIR
                        T = it * STEPS
                        section(s_y + DVE_LN + pr * DVE_PAIR, DVE_LN)

                        def qk(k, n, col, part):
                            dve.wait_ge(hi_done, h0 + k + 1)
                            nc.vector.scalar_tensor_tensor(out=part[1], in0=ps_m[n % 2][:], scalar=col,
                                                           in1=f32(part[0]), op0=ALU.add, op1=sub)\
                                .then_inc(bank_free, 1)

                        def extra_logits(h):
                            n = 3 + 4 * h
                            dve.wait_ge(bank_filled, n0 + n + 1)
                            src = ps_m[n % 2][:, 0:2 * LT].rearrange("p (l x) -> p l x", x=2)
                            nc.vector.tensor_reduce(lb[:, h, :], src, AX.X, ALU.add)
                            link(nc.vector.tensor_reduce(nlb[:, h, :], src, AX.X, ALU.add, negate=True))
                            dve.sem_inc(bank_free, 1)

                        def maxima(t):
                            h, lt = divmod(t, LT)
                            dve.wait_ge(s_filled, T + t + 1)
                            link(nc.vector.tensor_reduce(nmx[:, t:t + 1], ps_s[t % 2][:], AX.X, ALU.max, negate=True))
                            nc.vector.tensor_scalar(nm[:, t:t + 1], nmx[:, t:t + 1], nlb[:, h, lt:lt + 1], SCALE1,
                                                    ALU.min, ALU.mult).then_inc(nm_done, 1)

                        def turned(t):
                            j, off = t // 2, (t % 2) * P
                            for q in range(2):
                                dve.wait_ge(t_hi, 2 * (T + t) + q + 1)
                                part = [x[:, 4 * q:4 * q + 4, off:off + P] for x in pT[j % 2]]
                                nc.vector.tensor_tensor(part[1], ps_t[q][:].rearrange("p (s n) -> p s n", s=4),
                                                        f32(part[0]), sub).then_inc(t_lo, 1)

                        def extra_value(j):
                            h, n = j // 2, PX[j] + 1
                            dve.wait_ge(px_copied, 4 * it + j + 1)
                            dve.wait_ge(bank_filled, n0 + n + 1)
                            link(nc.vector.scalar_tensor_tensor(out=cf[j % 2][:], in0=pextb[j % 2][:],
                                                                scalar=pcol[:, 3, h:h + 1], in1=ps_m[n % 2][:, 0:256],
                                                                op0=ALU.mult, op1=ALU.add))
                            dve.sem_inc(bank_free, 2)
                            dve.sem_inc(cf_done, 1)

                        def result_lo(j):
                            h, off = j // 2, (j % 2) * 256
                            dve.wait_ge(c_hi, 4 * it + j + 1)
                            nc.vector.tensor_tensor(cT[1][:, h, off:off + 256], cf[j % 2][:],
                                                    f32(cT[0][:, h, off:off + 256]), sub).then_inc(c_lo, 1)

                        def denominators(h):
                            hs = slice(h * LT, (h + 1) * LT)
                            dve.wait_ge(exp_done, T + (h + 1) * LT)
                            link(nc.vector.tensor_tensor(z[:, hs], sums[:, hs], pext[:, hs], ALU.add))
                            link(nc.vector.reciprocal(r[:, hs], z[:, hs]))

                        def output(h):
                            for lt in range(LT):
                                n = OUT[h] + lt
                                dve.wait_ge(bank_filled, n0 + n + 1)
                                t = h * LT + lt
                                link(nc.vector.scalar_tensor_tensor(
                                    out=x_res[:, lt, :], in0=ps_m[n % 2][:], scalar=r[:, t:t + 1],
                                    in1=x_res[:, lt, :], op0=ALU.mult, op1=ALU.add))
                                dve.sem_inc(bank_free, 1)

                        link(nc.vector.tensor_copy(pcol[:], cols[:, bass.ds(y, 1), :, bass.ds(pr * 2, 2)]))
                        link(nc.vector.tensor_copy(bkx[:, :, 0], pcol[:, 2, :]))
                        nc.vector.tensor_tensor(bkx[:, :, 1], pcol[:, 2, :], f32(bkx[:, :, 0]), sub)\
                            .then_inc(col_done, 1)
                        qk(0, 0, pcol[:, 0, 0:1], [x[:] for x in qT[0]])
                        qk(1, 1, pcol[:, 1, 0:1], [x[:, 0:512] for x in kT[0]])
                        qk(2, 2, pcol[:, 1, 0:1], [x[:, 512:1024] for x in kT[0]])
                        extra_logits(0)
                        dve.wait_ge(bv_hi, it + 1)
                        nc.vector.tensor_tensor(bvx[1][:], stg_bv[:], f32(bvx[0][:]), sub).then_inc(bv_lo, 1)
                        qk(3, 4, pcol[:, 0, 1:2], [x[:] for x in qT[1]])
                        maxima(0)
                        maxima(1)
                        qk(4, 5, pcol[:, 1, 1:2], [x[:, 0:512] for x in kT[1]])
                        qk(5, 6, pcol[:, 1, 1:2], [x[:, 512:1024] for x in kT[1]])
                        extra_logits(1)
                        for i in range(4):
                            dve.wait_ge(hi_done, h0 + 6 + i + 1)
                            nc.vector.tensor_tensor(v[1][:, 2 * i:2 * i + 2, :],
                                                    ps_m[i % 2][:].rearrange("p (s n) -> p s n", s=2),
                                                    f32(v[0][:, 2 * i:2 * i + 2, :]), sub).then_inc(bank_free, 1)
                        for t in range(STEPS):
                            turned(t)
                            if t + 2 < STEPS:
                                maxima(t + 2)
                            if t % 2 == 0 and t >= 2:
                                extra_value(t // 2 - 1)
                            if t % 2 == 1 and t >= 3:
                                result_lo((t - 3) // 2)
                            if t == 4:
                                denominators(0)
                            if t == 6:
                                output(0)
                        denominators(1)
                        extra_value(3)
                        result_lo(3)
                        output(1)

                n_mlp = nb + U_L0 + LAYERS * U_LAYER
                section(sb_ + DVE_PROJ0 + KVH * DVE_KV0 + DVE_OUT0 + LAYERS * DVE_LAYER, DVE_PAIR)
                norm(b * 4 + 3, EPS1, h_tok)
                dve.sem_inc(ln_done, 1)
                add_row2()
                dve.sem_inc(rows_used, 1)
                turn_lo(n_mlp, hb + U_TURN + LAYERS * H_LAYER)
                with dve.Fori(0, FPAIRS) as fp:
                    for i in range(2):
                        dve.wait_ge(g_hi, (b * FPAIRS + fp) * 2 + i + 1)
                        nc.vector.tensor_tensor(gT[i][1][:], g[i][:], f32(gT[i][0][:]), sub).then_inc(bank_free, 1)
                dve.wait_ge(mlp_acc, b + 1)
                for lt in range(LT):
                    nc.vector.tensor_tensor(x_res[:, lt, :], ps_s[lt // 2][:, (lt % 2) * 512:(lt % 2 + 1) * 512],
                                            x_res[:, lt, :], ALU.add).then_inc(out_ready, 1)
                dve.wait_ge(out_ready, LT * (b + 1))
                dve.sem_inc(batch_done, 1)
                assert step[1] == DVE_LN, step


PX = (12, 14, 16, 22)
OUT = (18, 24)
DVE_NORM = 2 * LT + 5 + 3 * LT
DVE_PROJ0 = 6 * 4 + 4 * 4
DVE_KV0 = STEPS0 + LT
DVE_OUT0 = LT + LT + DVE_NORM
DVE_LN = DVE_NORM + LT
DVE_PAIR = 2 + 2 + STEPS + 4 + 4 + 2 * LT
DVE_LAYER = DVE_LN + PAIRS * DVE_PAIR
DVE_B = DVE_PROJ0 + KVH * DVE_KV0 + DVE_OUT0 + LAYERS * DVE_LAYER + DVE_LN


def laid_out(inputs):
    i = {k: np.asarray(v) for k, v in inputs.items()}
    x, c = i["x"], i["ctx_2048"]

    def tiles(w):
        return w.reshape(-1, P, w.shape[1]).transpose(1, 0, 2)

    def both(name):
        return [i[f"L1_xattn_{name}{y}"] for y in (1, 2)]

    d = {
        "x": x.reshape(B, LT, P, D).transpose(0, 2, 1, 3),
        "xT": x.transpose(0, 2, 1).reshape(B, CT, P, L).transpose(0, 2, 1, 3),
        "ctxT": c.transpose(0, 2, 1).reshape(B, CT, P, S).transpose(0, 2, 1, 3),
        "mask": i["mask_Bx1xSxS2_ff0"].reshape(B, LT, P, S).transpose(0, 2, 1, 3),
        "w0q": tiles(i["L0_xattn_Wq"]).reshape(P, 2, CT * 256),
        "w0o": tiles(i["L0_xattn_Wo"]).reshape(P, 2, CT * 256),
        "w0kv": tiles(np.concatenate([i["L0_xattn_Wk"], i["L0_xattn_Wv"]], axis=1)),
        "cols0": np.concatenate([i["L0_xattn_bq"].reshape(CT, P).T, i["L0_xattn_bk"].reshape(1, P).T], axis=1),
        "bv0": i["L0_xattn_bv"],
    }
    d["wqkv"] = np.stack([np.stack([tiles(w).reshape(P, CT, PAIRS, 256).transpose(2, 0, 1, 3)
                                    for w in ws], axis=2)
                          for ws in zip(both("wq"), both("wk"), both("wv"))]).reshape(LAYERS * PAIRS, P, 3, CT * 256)
    d["wo"] = np.stack([w.reshape(PAIRS, 2, P, D).transpose(0, 2, 1, 3) for w in both("wo")])\
        .reshape(LAYERS * PAIRS, P, 2, D)
    d["bv"] = np.stack(both("bv")).reshape(LAYERS * PAIRS, 1, 256)
    d["cols"] = np.stack([np.stack([a.reshape(HEADS, KD).T for a in cs], axis=1)
                          for cs in zip(both("bq"), both("bk"), both("bias_k"), both("bias_v"))], axis=1)
    rows = [[i["L0_xattn_gamma"], i["L0_xattn_beta"], i["L0_xattn_bo"]]]
    rows += [[i[f"L1_xattn_ln{y}_scale"], i[f"L1_xattn_ln{y}_offset"], i[f"L1_xattn_bo{y}"]] for y in (1, 2)]
    rows += [[i["L1_xattn_ln_mlp_scale"], i["L1_xattn_ln_mlp_offset"], i["L1_xattn_b_fc2"]]]
    d["rows"] = np.stack([np.stack(g) for g in rows])
    d["w1"] = tiles(i["L1_xattn_w_fc1"]).reshape(P, CT, FPAIRS, 256).transpose(2, 0, 1, 3).reshape(FPAIRS, P, CT * 256)
    d["w2"] = i["L1_xattn_w_fc2"].reshape(FPAIRS, 2, P, D).transpose(0, 2, 1, 3)
    d["colf"] = i["L1_xattn_b_fc1"].reshape(F // P, P).T
    return {k: np.ascontiguousarray(a) for k, a in d.items()}


def kernel(**inputs):
    import concourse.bacc as bacc
    from concourse.bass_utils import run_bass_kernel_spmd

    nc = bacc.Bacc("TRN2", target_bir_lowering=False, num_devices=1)
    arrays = laid_out(inputs)
    d = {k: nc.dram_tensor(f"in_{k}", a.shape, F32, kind="ExternalInput").ap() for k, a in arrays.items()}
    d["out"] = nc.dram_tensor("out", [B, P, LT, D], F32, kind="ExternalOutput").ap()
    build(nc, d)
    got = run_bass_kernel_spmd(nc, [{f"in_{k}": a for k, a in arrays.items()}], core_ids=[0]).results[0]["out"]
    return np.ascontiguousarray(np.asarray(got).reshape(B, P, LT, D).transpose(0, 2, 1, 3).reshape(B, L, D))
```

```python
from contextlib import ExitStack

import numpy as np

import concourse.bass as bass
from concourse import mybir

F32 = mybir.dt.float32
F32R = mybir.dt.float32r
BF16 = mybir.dt.bfloat16
F16 = mybir.dt.float16
ALU = mybir.AluOpType
ACT = mybir.ActivationFunctionType
AX = mybir.AxisListType

P = 128
B, L, S, D = 2, 512, 1024, 512
CT, LT, ST = D // P, L // P, S // P
KVH, GROUPS, HD = 8, 4, 16
NH0 = KVH * GROUPS
LAYERS, HEADS, KD = 2, 16, 128
PAIRS = HEADS // 2
F = 2048
FPAIRS = F // 256
SCALE0 = HD ** -0.5
SCALE1 = KD ** -0.5
EPS0, EPS1 = 1e-6, 1e-5
LOG_P_TOP = float(np.log(4096.0))
Q_ORDER = (0, 0, 1, 1, 0, 2)
K_ORDER = (0, 1, 0, 1, 2, 0)
STACK = HD * len(Q_ORDER)
VW = 64

STEPS0 = LT * GROUPS
STEPS = 2 * LT
PRO_K0, PRO_K1, PRO_V, PRO_Q0, PRO_EX0, PRO_Q1, PRO_EX1 = 0, 2, (4, 5, 7, 10), 6, 8, 9, 11
PV = (0, 3, 10, 15)
Q0, K0, EX0, OUT0, Q1, K1, EX1, V, OUT1 = 1, (2, 4), 5, 6, 11, (12, 13), 14, (16, 17, 18, 19), 20
LAST_PV, LAST_OUT0, LAST_OUT1 = (0, 1, 6, 7), 2, 8
U_PRO, U_PAIR, U_LAST = 12, 24, 12
U_PROJ0, U_OUT0 = 10, LT
U_L0 = U_PROJ0 + U_OUT0
U_LAYER = U_PRO + (PAIRS - 1) * U_PAIR + U_LAST
U_MLP = 2 * FPAIRS
U_B = U_L0 + LAYERS * U_LAYER + U_MLP
FP_K0, FP_K1, FP_V, FP_Q0, FP_Q1 = (0, 1), (2, 3), (4, 5, 7, 9), 6, 8
F_Q0, F_K0, F_Q1, F_K1, F_V = 0, (1, 2), 3, (4, 5), (6, 7, 8, 9)
F_PAIR = 10
F_LAYER = PAIRS * F_PAIR
QK_B = 2 + LAYERS * PAIRS + FPAIRS // 2
V_B = LAYERS * PAIRS
O_B = LAYERS * PAIRS + FPAIRS
TURNS = 2 + LAYERS
TURN_ORDER = (2, 3, 0, 1)
PASSES = ((0, 0), (0, 1), (1, 0))


def build(nc, d):
    with ExitStack() as ctx:
        sems = {}

        def sem(name):
            sems[name] = ctx.enter_context(nc.semaphore(name))
            return sems[name]

        start = (nc.sbuf_base + 31) // 32 * 32
        at = [start]

        def sb(name, shape, dt, n=1):
            size = int(np.prod(shape[1:])) * (2 if dt in (BF16, F16) else 4)
            made = []
            for i in range(n):
                made.append(nc.alloc_sbuf_tensor_at(name if n == 1 else f"{name}{i}", shape, dt, offset=at[0]))
                at[0] += (size + 31) // 32 * 32
            return made[0] if n == 1 else made

        ctxT = sb("ctxT", [P, CT, S], F32R, 2)
        hT = sb("hT", [P, CT, L], F32R, 2)
        x_res = sb("x_res", [P, LT, D], F32)
        row = sb("row", [P, D], F32)
        stg_qk = sb("stg_qk", [P, 2, CT * 256], F32)
        stg_v = sb("stg_v", [P, CT * 256], F32)
        stg_o = sb("stg_o", [P, 2, D], F32)
        bv_row = sb("bv_row", [P, 256], F32)
        ident = sb("ident", [P, P], F32)
        cols = sb("cols", [P, LAYERS * 4 * HEADS], F32)
        lnc = sb("lnc", [P, (LAYERS + 1) * 2 * CT], F32)
        cols0 = sb("cols0", [P, 5], F32)
        colf = sb("colf", [P, F // P], F32)
        bv0 = sb("bv0", [P, P], F32)
        stats = sb("stats", [P, LT, 6], F32)
        mean_var = sb("mean_var", [P, LT, 2], F32)
        lnv = sb("lnv", [P, 5, LT], F32)
        region = at[0]

        q_stack = sb("q_stack", [STACK, NH0, L], BF16)
        k_stack = sb("k_stack", [STACK, KVH, S], BF16)
        v3 = sb("v3", [P, ST, KVH, VW], BF16)
        mask = sb("mask", [P, LT, S], F32)
        w0o = sb("w0o", [P, CT, D], F32R, 2)
        parts_at = at[0]
        a0 = sb("a0", [P, LT, D], F32)
        nm0 = sb("nm0", [P, 2], F32, 2)
        red0 = sb("red0", [P, GROUPS, HD], F32)
        rden0 = sb("rden0", [P, GROUPS], F32)
        loop0 = at[0]
        sm = sb("sm", [P, S], F32, 2)
        p0 = sb("p0", [P, S], F32, 2)
        p16 = [sb(f"p16_{i}", [P, ST, P], F16, 2) for i in range(2)]
        end0 = at[0]
        at[0] = loop0
        w0q = sb("w0q", [P, CT, D], F32R, 2)
        w0kv = sb("w0kv", [P, CT, 256], F32R, 2)
        end0 = max(end0, at[0])
        at[0] = end0
        at[0] = parts_at
        parts = sb("parts", [P, 3, 512], BF16, 2)
        at[0] = region
        st_ctx = sb("st_ctx", [P, CT, S], F32)
        st_x = sb("st_x", [P, CT, L], F32)
        st_kv = sb("st_kv", [P, CT, 256], F32)
        assert at[0] - region <= NH0 * L * 2
        at[0] = end0
        tmp0 = sb("tmp0", [P, 512], F32, 2)
        ends = [at[0]]

        at[0] = region
        wa = sb("wa", [P, 3, CT, 256], F32R, 2)
        wo = sb("wo", [P, 2, D], F32R, 2)
        proj = sb("proj", [P, 512], F32, 2)
        projected_at = at[0]
        kT = [sb(f"kT{h}_", [P, S], F32R, 2) for h in range(2)]
        qT = [sb(f"qT{h}_", [P, L], F32R, 2) for h in range(2)]
        v = sb("v", [P, ST, 256], F32R, 2)
        p = sb("p", [P, S], F32, 2)
        turned_at = at[0]
        pT = [sb(f"pT{i}_", [P, ST, 256], F32R, 2) for i in range(2)]
        cT = sb("cT", [P, 2, L], F32R, 2)
        cf = sb("cf", [P, 256], F32, 2)
        pextb = sb("pextb", [P, 256], F32, 2)
        bkx = sb("bkx", [P, 2, 2], F32R)
        lb = sb("lb", [P, 2, LT], F32)
        nlb = sb("nlb", [P, 2, LT], F32)
        nmx = sb("nmx", [P, STEPS], F32)
        nm = sb("nm", [P, STEPS], F32)
        pext = sb("pext", [P, STEPS], F32)
        sums = sb("sums", [P, STEPS], F32)
        z = sb("z", [P, STEPS], F32)
        r = sb("r", [P, STEPS], F32)
        ends.append(at[0])
        at[0] = turned_at
        h_tok = sb("h_tok", [P, LT, D], F32)
        h_fea = sb("h_fea", [P, CT, L], F32)
        at[0] = projected_at
        g = sb("g", [P, L], F32, 2)
        gT = [[sb(f"gT{k}{i}_", [P, L], F32R, 2) for i in range(2)] for k in range(2)]
        assert at[0] <= turned_at
        assert max(ends) <= nc.sbuf_usable_end, (max(ends), nc.sbuf_usable_end)

        ps_s = [ctx.enter_context(nc.psum_tensor(f"ps_s{i}", [P, S], F32)) for i in range(2)]
        ps_t = [ctx.enter_context(nc.psum_tensor(f"ps_t{i}", [P, 512], F32)) for i in range(2)]
        ps_m = [ctx.enter_context(nc.psum_tensor(f"ps_m{i}", [P, 512], F32)) for i in range(2)]

        scr_k = nc.dram_tensor("scr_k", [2, P, 3, 512], BF16, kind="Internal").ap()
        scr_q = nc.dram_tensor("scr_q", [4, P, 3, 512], BF16, kind="Internal").ap()

        const_in = sem("const_in")
        xres_in, kv_in, ctx_in, x_in = sem("xres_in"), sem("kv_in"), sem("ctx_in"), sem("x_in")
        mask_in, row_in, rows0_in = sem("mask_in"), sem("row_in"), sem("rows0_in")
        qk_in, v_in, o_in, bv_in = sem("qk_in"), sem("v_in"), sem("o_in"), sem("bv_in")
        scr_out, stack_in = sem("scr_out"), sem("stack_in")
        out_done = sem("out_done")
        const_made = sem("const_made")
        in_hi, in_lo, kv_lo = sem("in_hi"), sem("in_lo"), sem("kv_lo")
        qk_hi, qk_lo = sem("qk_hi"), sem("qk_lo")
        v_hi, v_lo = sem("v_hi"), sem("v_lo")
        o_hi, o_lo = sem("o_hi"), sem("o_lo")
        bank_filled = sem("bank_filled")
        bank_free = sem("bank_free")
        part_done = sem("part_done")
        v3_done = sem("v3_done")
        s0_filled, raw0_done, max0_done, exp0_done = sem("s0_filled"), sem("raw0_done"), sem("max0_done"), sem("exp0_done")
        t0_filled, t0_hi, t0_lo = sem("t0_filled"), sem("t0_hi"), sem("t0_lo")
        pv0_done, pv0_free = sem("pv0_done"), sem("pv0_free")
        a0_done = sem("a0_done")
        l0_done = sem("l0_done")
        row_added = sem("row_added")
        var_done, sqrt_done, ln_done = sem("var_done"), sem("sqrt_done"), sem("ln_done")
        turn_filled, h_done, h_hi, h_lo = sem("turn_filled"), sem("h_done"), sem("h_hi"), sem("h_lo")
        col_done = sem("col_done")
        proj_hi, proj_lo = sem("proj_hi"), sem("proj_lo")
        s_filled, raw_done, nm_done, exp_done = sem("s_filled"), sem("raw_done"), sem("nm_done"), sem("exp_done")
        t_filled, t_hi, t_lo = sem("t_filled"), sem("t_hi"), sem("t_lo")
        px_copied, c_hi, c_lo = sem("px_copied"), sem("c_hi"), sem("c_lo")
        den_done = sem("den_done")
        g_hi, g_lo, mlp_out = sem("g_hi"), sem("g_lo"), sem("mlp_out")
        out_ready, batch_done = sem("out_ready"), sem("batch_done")
        apart_sp, apart_pe, apart_dve = sem("apart_sp"), sem("apart_pe"), sem("apart_dve")
        dve_step = sem("dve_step")

        block = ctx.enter_context(nc.Block())

        def f32(t):
            return t.bitcast(F32)

        def k_half(h, i):
            return [x[:, i * 512:(i + 1) * 512] for x in kT[h]]

        def q_all(h):
            return [x[:] for x in qT[h]]

        def v_tiles(i):
            return [x[:, 2 * i:2 * i + 2, :] for x in v]

        def turned_bank(c):
            return ps_s[c // 2][:, c % 2 * 512:(c % 2 + 1) * 512]

        @block.sync
        def _(sp):
            for dst, name in ((cols, "cols"), (cols0, "cols0"), (colf, "colf"), (lnc, "lnc"), (bv0, "bv0")):
                src = d[name]
                sp.dma_start(dst[:], src.partition_broadcast(P) if name == "bv0" else src).then_inc(const_in, 16)

            def apart():
                sp.sem_inc(apart_sp, 1)

            def load_row(k, i):
                sp.wait_ge(row_added, k + 1)
                sp.dma_start(row[:], d["rows"][i, :].partition_broadcast(P)).then_inc(row_in, 16)

            def load_qk(use, src):
                sp.wait_ge(qk_lo, 2 * use + 2)
                sp.dma_start(stg_qk[:], src).then_inc(qk_in, 16)

            def load_v(use, src):
                sp.wait_ge(v_lo, use + 1)
                sp.dma_start(stg_v[:], src).then_inc(v_in, 16)

            def load_o(use, src):
                sp.wait_ge(o_lo, use + 1)
                sp.dma_start(stg_o[:], src).then_inc(o_in, 16)

            def load_bv(k, f):
                sp.wait_ge(proj_lo, 2 + F_PAIR * k)
                sp.dma_start(bv_row[:], d["bv"][f, :].partition_broadcast(P)).then_inc(bv_in, 16)

            with sp.Fori(0, B) as b:
                sp.wait_ge(batch_done, b + 1)
                sp.dma_start(st_kv[:], d["w0kv"]).then_inc(kv_in, 16)
                sp.dma_start(st_ctx[:], d["ctxT"][b, :, :, :]).then_inc(ctx_in, 16)
                sp.dma_start(st_x[:], d["xT"][b, :, :, :]).then_inc(x_in, 16)
                load_qk(b * QK_B, d["w0q"])
                sp.dma_start(mask[:], d["mask"][b, :, :, :]).then_inc(mask_in, 16)
                sp.dma_start(x_res[:], d["x"][b, :, :, :]).then_inc(xres_in, 16)
                load_row(b * TURNS, 0)
                sp.dma_start(stg_o[:], d["rows0"].partition_broadcast(P)).then_inc(rows0_in, 16)
                load_qk(b * QK_B + 1, d["w0o"])
                for i in range(6):
                    sp.wait_ge(part_done, b * 6 + i + 1)
                    scr = scr_k[i, :, :, :] if i < 2 else scr_q[i - 2, :, :, :]
                    sp.dma_start(scr, parts[i % 2][:]).then_inc(scr_out, 16)
                    sp.wait_ge(scr_out, 16 * (b * 6 + i + 1))
                    apart()
                    if i == 2:
                        sp.wait_ge(in_lo, (b + 1) * (CT + 1))
                        sp.wait_ge(kv_lo, b + 1)
                    for j in range(len(Q_ORDER)):
                        part = (K_ORDER if i < 2 else Q_ORDER)[j]
                        rows_j = slice(HD * j, HD * j + HD)
                        dst = (k_stack[rows_j, :, i * 512:(i + 1) * 512] if i < 2 else
                               q_stack[rows_j, (i - 2) * 8:(i - 1) * 8, :])
                        src = scr[:, part, :].rearrange("(a e) n -> e a n", e=HD)
                        sp.dma_start(dst, src).then_inc(stack_in, 16)
                load_qk(b * QK_B + 2, d["wqk"][0, :, :, :])
                sp.wait_ge(l0_done, b + 1)
                apart()
                with sp.Fori(0, LAYERS) as y:
                    load_row(b * TURNS + 1 + y, y + 1)
                    f0 = y * PAIRS
                    load_v(b * V_B + f0, d["wv"][f0, :, :])
                    load_bv(b * V_B + f0, f0)
                    load_qk(b * QK_B + 3 + f0, d["wqk"][f0 + 1, :, :, :])
                    with sp.Fori(0, PAIRS - 1) as pr:
                        f = f0 + pr
                        load_o(b * O_B + f, d["wo"][f, :, :, :])
                        load_v(b * V_B + f + 1, d["wv"][f + 1, :, :])
                        load_bv(b * V_B + f + 1, f + 1)
                        load_qk(b * QK_B + 4 + f, d["wqk"][f + 2, :, :, :])
                    load_o(b * O_B + f0 + PAIRS - 1, d["wo"][f0 + PAIRS - 1, :, :, :])
                load_row(b * TURNS + 3, 3)
                load_o(b * O_B + V_B, d["wo"][V_B, :, :, :])
                for j in range(FPAIRS // 2):
                    if j < FPAIRS // 2 - 1:
                        load_qk(b * QK_B + 3 + V_B + j, d["wqk"][V_B + 1 + j, :, :, :])
                    for fp in range(2 * j + 1, min(2 * j + 3, FPAIRS)):
                        load_o(b * O_B + V_B + fp, d["wo"][V_B + fp, :, :, :])
                for lt in range(LT):
                    sp.wait_ge(out_ready, b * LT + lt + 1)
                    sp.dma_start(d["out"][b, :, lt, :], x_res[:, lt, :]).then_inc(out_done, 16)
                sp.wait_ge(out_done, 16 * LT * (b + 1))
                apart()

        @block.gpsimd
        def _(pool):
            nc.gpsimd.memset(ident[:], 0.0).then_inc(const_made, 1)
            pool.wait_ge(const_made, 1)
            nc.gpsimd.affine_select(out=ident[:], in_=ident[:], compare_op=ALU.not_equal, fill=1.0, base=0,
                                    pattern=[[-1, P]], channel_multiplier=1).then_inc(const_made, 1)
            pool.sem_inc(proj_lo, 2)
            pool.sem_inc(qk_lo, 2)
            pool.sem_inc(v_lo, 1)
            pool.sem_inc(o_lo, 1)
            pool.sem_inc(row_added, 1)

            def lo(out, x, hi):
                return nc.gpsimd.tensor_tensor(out, x, f32(hi), ALU.subtract)

            def lo_qk(use, slot):
                pool.wait_ge(qk_hi, 2 * use + slot + 1)
                flat = [w[:, slot].rearrange("p c n -> p (c n)") for w in wa]
                lo(flat[1], stg_qk[:, slot, :], flat[0]).then_inc(qk_lo, 1)

            def lo_v(use):
                pool.wait_ge(v_hi, use + 1)
                flat = [w[:, 2].rearrange("p c n -> p (c n)") for w in wa]
                lo(flat[1], stg_v[:], flat[0]).then_inc(v_lo, 1)

            def lo_o(use):
                pool.wait_ge(o_hi, use + 1)
                lo(wo[1][:], stg_o[:], wo[0][:]).then_inc(o_lo, 1)

            def lo_w0(use, w):
                pool.wait_ge(qk_hi, 2 * use + 2)
                flat = [t[:].rearrange("p (s c) n -> p s (c n)", s=2) for t in w]
                lo(flat[1], stg_qk[:], flat[0]).then_inc(qk_lo, 2)

            def add_row(k):
                pool.wait_ge(row_in, 16 * (k + 1))
                nc.gpsimd.tensor_tensor(x_res[:], x_res[:], row[:].unsqueeze(1).to_broadcast([P, LT, D]),
                                        ALU.add).then_inc(row_added, 1)

            def lo_turn(k):
                for i in range(2):
                    pool.wait_ge(h_hi, CT * k + i + 1)
                    c = TURN_ORDER[i]
                    lo(hT[1][:, c, :], h_fea[:, c, :], hT[0][:, c, :]).then_inc(h_lo, 1)

            with pool.Fori(0, B) as b:
                pool.wait_ge(in_hi, b * (CT + 2) + 1)
                lo(w0kv[1][:], st_kv[:], w0kv[0][:]).then_inc(kv_lo, 1)
                lo_w0(b * QK_B, w0q)
                pool.wait_ge(xres_in, 16 * (b + 1))
                add_row(b * TURNS)
                lo_w0(b * QK_B + 1, w0o)
                lo_qk(b * QK_B + 2, 0)
                lo_qk(b * QK_B + 2, 1)
                with pool.Fori(0, LAYERS) as y:
                    def lo_proj(k, dst):
                        pool.wait_ge(proj_hi, F0 + k + 1)
                        x = proj[k % 2][:]
                        if len(dst[1].shape) == 3:
                            x = x.rearrange("p (s n) -> p s n", s=2)
                        lo(dst[1], x, dst[0]).then_inc(proj_lo, 1)

                    def lo_c(j):
                        pool.wait_ge(c_hi, 4 * it + j + 1)
                        h, off = j // 2, (j % 2) * 256
                        lo(cT[1][:, h, off:off + 256], cf[j % 2][:], cT[0][:, h, off:off + 256]).then_inc(c_lo, 1)

                    it = (b * LAYERS + y) * PAIRS
                    f0 = y * PAIRS
                    F0 = it * F_PAIR
                    lo_v(b * V_B + f0)
                    for h in range(2):
                        for i in range(2):
                            lo_proj((FP_K0, FP_K1)[h][i], k_half(h, i))
                    lo_turn(b * TURNS + 1 + y)
                    pool.wait_ge(ln_done, (b * 3 + y + 1) * LT)
                    lo_proj(FP_V[0], v_tiles(0))
                    lo_proj(FP_V[1], v_tiles(1))
                    lo_proj(FP_Q0, q_all(0))
                    lo_proj(FP_V[2], v_tiles(2))
                    lo_proj(FP_Q1, q_all(1))
                    lo_proj(FP_V[3], v_tiles(3))
                    add_row(b * TURNS + 1 + y)
                    lo_qk(b * QK_B + 3 + f0, 0)
                    lo_qk(b * QK_B + 3 + f0, 1)
                    with pool.Fori(0, PAIRS - 1) as pr:
                        it = (b * LAYERS + y) * PAIRS + pr
                        f = f0 + pr
                        F0 = (it + 1) * F_PAIR
                        lo_c(0)
                        lo_proj(F_Q0, q_all(0))
                        lo_o(b * O_B + f)
                        lo_proj(F_K0[0], k_half(0, 0))
                        lo_v(b * V_B + f + 1)
                        lo_c(1)
                        lo_proj(F_K0[1], k_half(0, 1))
                        lo_c(2)
                        lo_proj(F_Q1, q_all(1))
                        lo_proj(F_K1[0], k_half(1, 0))
                        lo_proj(F_K1[1], k_half(1, 1))
                        lo_c(3)
                        lo_proj(F_V[0], v_tiles(0))
                        lo_proj(F_V[1], v_tiles(1))
                        lo_qk(b * QK_B + 4 + f, 0)
                        lo_proj(F_V[2], v_tiles(2))
                        lo_proj(F_V[3], v_tiles(3))
                        lo_qk(b * QK_B + 4 + f, 1)
                    it = (b * LAYERS + y) * PAIRS + PAIRS - 1
                    lo_c(0)
                    lo_o(b * O_B + f0 + PAIRS - 1)
                    for j in range(1, 4):
                        lo_c(j)
                lo_turn(b * TURNS + 3)
                pool.wait_ge(ln_done, (b * 3 + 3) * LT)
                add_row(b * TURNS + 3)
                lo_o(b * O_B + V_B)
                for j in range(FPAIRS // 2):
                    more = j < FPAIRS // 2 - 1
                    if more:
                        lo_qk(b * QK_B + 3 + V_B + j, 0)
                    lo_o(b * O_B + V_B + 2 * j + 1)
                    if more:
                        lo_qk(b * QK_B + 3 + V_B + j, 1)
                        lo_o(b * O_B + V_B + 2 * j + 2)

        @block.scalar
        def _(act):
            def copy(out, in_):
                return nc.scalar.activation(out, in_, ACT.Copy)

            def split_w0(use, w):
                act.wait_ge(qk_in, 16 * (use + 1))
                copy(w[0][:].rearrange("p (s c) n -> p s (c n)", s=2), stg_qk[:]).then_inc(qk_hi, 2)

            def split_qk(use, slot):
                act.wait_ge(qk_in, 16 * (use + 1))
                copy(wa[0][:, slot].rearrange("p c n -> p (c n)"), stg_qk[:, slot, :]).then_inc(qk_hi, 1)

            def split_v(use):
                act.wait_ge(v_in, 16 * (use + 1))
                copy(wa[0][:, 2].rearrange("p c n -> p (c n)"), stg_v[:]).then_inc(v_hi, 1)

            def split_o(use):
                act.wait_ge(o_in, 16 * (use + 1))
                copy(wo[0][:], stg_o[:]).then_inc(o_hi, 1)

            def root(k):
                act.wait_ge(var_done, k + 1)
                nc.scalar.activation(lnv[:, 1, :], lnv[:, 0, :], ACT.Sqrt).then_inc(sqrt_done, 1)

            def turn_hi(k):
                for i, c in enumerate(TURN_ORDER):
                    act.wait_ge(h_done, CT * k + i + 1)
                    copy(hT[0][:, c, :], h_fea[:, c, :]).then_inc(h_hi, 1)

            with act.Fori(0, B) as b:
                act.wait_ge(kv_in, 16 * (b + 1))
                copy(w0kv[0][:], st_kv[:]).then_inc(in_hi, 1)
                act.wait_ge(ctx_in, 16 * (b + 1))
                for c in range(CT):
                    copy(ctxT[0][:, c, :], st_ctx[:, c, :]).then_inc(in_hi, 1)
                act.wait_ge(x_in, 16 * (b + 1))
                copy(hT[0][:], st_x[:]).then_inc(in_hi, 1)
                split_w0(b * QK_B, w0q)
                split_w0(b * QK_B + 1, w0o)

                def exp0(t):
                    act.wait_ge(max0_done, t0 + t + 1)
                    nc.scalar.activation(p0[t % 2][:], sm[t % 2][:], ACT.Exp,
                                         bias=nm0[1][:, t % 2:t % 2 + 1]).then_inc(exp0_done, 1)

                def step0(t, ahead):
                    act.wait_ge(pv0_done, t0 + t + 1)
                    for q in range(2):
                        act.wait_ge(t0_filled, 2 * (t0 + t) + q + 1)
                        copy(p16[t % 2][0][:, 4 * q:4 * q + 4, :],
                             ps_t[q][:].rearrange("p (s n) -> p s n", s=4)).then_inc(t0_hi, 1)
                    if ahead:
                        exp0(t + 2)

                t0 = b * KVH * STEPS0
                exp0(0)
                exp0(1)
                with act.Fori(0, KVH - 1) as kv:
                    t0 = (b * KVH + kv) * STEPS0
                    for t in range(STEPS0):
                        step0(t, True)
                t0 = (b * KVH + KVH - 1) * STEPS0
                for t in range(STEPS0):
                    step0(t, t + 2 < STEPS0)
                for i, c in enumerate(TURN_ORDER):
                    act.wait_ge(turn_filled, CT * (b * TURNS) + i + 1)
                    copy(hT[0][:, c, :], turned_bank(c)).then_inc(h_hi, 1)
                root(b * TURNS)
                act.wait_ge(l0_done, b + 1)
                split_qk(b * QK_B + 2, 0)
                split_qk(b * QK_B + 2, 1)

                with act.Fori(0, LAYERS) as y:
                    def hi_proj(n, k, dst):
                        act.wait_ge(bank_free, n0 + n + 3)
                        x = proj[k % 2][:]
                        if len(dst[0].shape) == 3:
                            x = x.rearrange("p (s n) -> p s n", s=2)
                        copy(dst[0], x).then_inc(proj_hi, 1)

                    def exp(t):
                        h, lt, i = t // LT % 2, t % LT, t % STEPS
                        act.wait_ge(nm_done, T + t + 1)
                        nc.scalar.activation(pext[:, i:i + 1], lb[:, h, lt:lt + 1], ACT.Exp,
                                             bias=nm[:, i:i + 1], scale=SCALE1)
                        nc.scalar.activation(p[t % 2][:], ps_s[t % 2][:], ACT.Exp, bias=nm[:, i:i + 1],
                                             scale=SCALE1, accum_out=sums[:, i:i + 1]).then_inc(exp_done, 1)

                    def turned(t):
                        off = (t % 2) * P
                        for q in range(2):
                            act.wait_ge(t_filled, 2 * (T + t) + q + 1)
                            copy(pT[t // 2 % 2][0][:, 4 * q:4 * q + 4, off:off + P],
                                 ps_t[q][:].rearrange("p (s n) -> p s n", s=4)).then_inc(t_hi, 1)

                    def c_halves(n, j):
                        act.wait_ge(bank_filled, n0 + n + 1)
                        copy(pextb[j % 2][:], ps_m[n % 2][:, 256:512]).then_inc(px_copied, 1)
                        act.wait_ge(bank_free, n0 + n + 3)
                        h, off = j // 2, (j % 2) * 256
                        copy(cT[0][:, h, off:off + 256], cf[j % 2][:]).then_inc(c_hi, 1)

                    it = (b * LAYERS + y) * PAIRS
                    f0 = y * PAIRS
                    T = it * STEPS
                    n0 = b * U_B + U_L0 + y * U_LAYER
                    split_v(b * V_B + f0)
                    root(b * TURNS + 1 + y)
                    for h in range(2):
                        for i in range(2):
                            hi_proj((PRO_K0, PRO_K1)[h] + i, (FP_K0, FP_K1)[h][i], k_half(h, i))
                    turn_hi(b * 3 + y)
                    hi_proj(PRO_V[0], FP_V[0], v_tiles(0))
                    hi_proj(PRO_V[1], FP_V[1], v_tiles(1))
                    hi_proj(PRO_Q0, FP_Q0, q_all(0))
                    hi_proj(PRO_V[2], FP_V[2], v_tiles(2))
                    exp(0)
                    hi_proj(PRO_Q1, FP_Q1, q_all(1))
                    hi_proj(PRO_V[3], FP_V[3], v_tiles(3))
                    exp(1)
                    turned(0)
                    exp(2)
                    split_qk(b * QK_B + 3 + f0, 0)
                    turned(1)
                    exp(3)
                    split_qk(b * QK_B + 3 + f0, 1)
                    with act.Fori(0, PAIRS - 1) as pr:
                        it = (b * LAYERS + y) * PAIRS + pr
                        f = f0 + pr
                        T = it * STEPS
                        n0 = b * U_B + U_L0 + y * U_LAYER + U_PRO + pr * U_PAIR
                        for t in range(2, STEPS + 2):
                            turned(t)
                            exp(t + 2)
                            if t % 2 == 0:
                                c_halves(PV[t // 2 - 1], t // 2 - 1)
                            if t == 2:
                                hi_proj(Q0, F_Q0, q_all(0))
                                split_o(b * O_B + f)
                            if t == 3:
                                hi_proj(K0[0], F_K0[0], k_half(0, 0))
                                split_v(b * V_B + f + 1)
                            if t == 4:
                                hi_proj(K0[1], F_K0[1], k_half(0, 1))
                            if t == 6:
                                hi_proj(Q1, F_Q1, q_all(1))
                            if t == 7:
                                hi_proj(K1[0], F_K1[0], k_half(1, 0))
                                hi_proj(K1[1], F_K1[1], k_half(1, 1))
                            if t >= STEPS:
                                for i in range(2 * (t - STEPS), 2 * (t - STEPS) + 2):
                                    hi_proj(V[i], F_V[i], v_tiles(i))
                                split_qk(b * QK_B + 4 + f, t - STEPS)
                    it = (b * LAYERS + y) * PAIRS + PAIRS - 1
                    T = it * STEPS
                    n0 = b * U_B + U_L0 + (y + 1) * U_LAYER - U_LAST
                    for t in range(2, STEPS):
                        turned(t)
                        if t + 2 < STEPS:
                            exp(t + 2)
                        if t % 2 == 0:
                            c_halves(LAST_PV[t // 2 - 1], t // 2 - 1)
                        if t == 2:
                            split_o(b * O_B + f0 + PAIRS - 1)
                    c_halves(LAST_PV[3], 3)

                root(b * TURNS + 3)
                turn_hi(b * 3 + 2)
                split_o(b * O_B + V_B)

                def gelu(fp):
                    act.wait_ge(g_lo, (b * FPAIRS + fp) * 2 + 2)
                    for i in range(2):
                        act.wait_ge(bank_filled, b * U_B + U_B - U_MLP + 2 * fp + i + 1)
                        nc.scalar.activation(g[i][:], ps_m[i][:], ACT.Gelu,
                                             bias=colf[:, fp * 2 + i:fp * 2 + i + 1]).then_inc(bank_free, 1)
                    for i in range(2):
                        act.wait_ge(bank_free, b * U_B + U_B - U_MLP + 2 * fp + i + 3)
                        copy(gT[fp % 2][i][0][:], g[i][:]).then_inc(g_hi, 1)

                gelu(0)
                for j in range(FPAIRS // 2):
                    more = j < FPAIRS // 2 - 1
                    if more:
                        split_qk(b * QK_B + 3 + V_B + j, 0)
                    gelu(2 * j + 1)
                    act.wait_ge(mlp_out, b * FPAIRS + 2 * j + 1)
                    split_o(b * O_B + V_B + 2 * j + 1)
                    if more:
                        split_qk(b * QK_B + 3 + V_B + j, 1)
                        gelu(2 * j + 2)
                        act.wait_ge(mlp_out, b * FPAIRS + 2 * j + 2)
                        split_o(b * O_B + V_B + 2 * j + 2)

        @block.tensor
        def _(pe):
            def passes(out, lhs, rhs, n_tiles, start=True, stop=True):
                for c in range(n_tiles):
                    for i, (x, y) in enumerate(PASSES):
                        mm = nc.tensor.matmul(out, lhs(x, c), rhs(y, c), start=start and c == 0 and i == 0,
                                              stop=stop and c == n_tiles - 1 and i == 2)
                return mm

            def free(n):
                pe.wait_ge(bank_free, n + 1)

            def turn(k, src, ready=None):
                for lt in range(LT):
                    if ready is not None:
                        pe.wait_ge(ln_done, ready + lt + 1)
                    for c in TURN_ORDER:
                        mm = nc.tensor.transpose(turned_bank(c)[:, lt * P:(lt + 1) * P],
                                                 src[:, lt, c * P:(c + 1) * P], ident[:])
                        if lt == LT - 1:
                            mm.then_inc(turn_filled, 1)

            def apart():
                pe.sem_inc(apart_pe, 1)

            pe.wait_ge(const_made, 2)
            pe.sem_inc(pv0_done, 2)
            with pe.Fori(0, B) as b:
                nb = b * U_B
                pe.wait_ge(kv_lo, b + 1)
                pe.wait_ge(in_lo, b * (CT + 1) + CT)
                for i in range(2):
                    free(nb + i)
                    passes(ps_m[i][:], lambda x, c: w0kv[x][:, c, 0:P],
                           lambda y, c: ctxT[y][:, c, i * 512:(i + 1) * 512], CT).then_inc(bank_filled, 1)
                for i in range(4):
                    free(nb + 2 + i)
                    for s in range(2):
                        st = 2 * i + s
                        mm = passes(ps_m[i % 2][:, s * 256:(s + 1) * 256],
                                    lambda x, c: ctxT[x][:, c, st * P:(st + 1) * P],
                                    lambda y, c: w0kv[y][:, c, :], CT)
                    mm.then_inc(bank_filled, 1)
                pe.wait_ge(in_lo, (b + 1) * (CT + 1))
                pe.wait_ge(qk_lo, 2 * (b * QK_B) + 4)
                for i in range(4):
                    free(nb + 6 + i)
                    passes(ps_m[i % 2][:], lambda x, c: w0q[x][:, c, i * P:(i + 1) * P],
                           lambda y, c: hT[y][:, c, :], CT).then_inc(bank_filled, 1)

                pe.wait_ge(stack_in, 16 * 36 * (b + 1))
                pe.wait_ge(v3_done, b * 5 + 5)
                apart()

                def scores0(t):
                    lt, gr = divmod(t % STEPS0, GROUPS)
                    head = kv + t // STEPS0
                    if t >= 2:
                        pe.wait_ge(raw0_done, t0 + t - 1)
                    for n in range(2):
                        mm = nc.tensor.matmul(ps_s[t % 2][:, n * 512:(n + 1) * 512],
                                              q_stack[:, bass.ds(head * GROUPS + gr, 1), lt * P:(lt + 1) * P],
                                              k_stack[:, bass.ds(head, 1), n * 512:(n + 1) * 512],
                                              start=True, stop=True)
                    mm.then_inc(s0_filled, 1)

                def turned0(t):
                    pe.wait_ge(exp0_done, t0 + t + 1)
                    for q in range(2):
                        pe.wait_ge(t0_lo, 2 * (t0 + t) + q + 1)
                        for s in range(4):
                            st = 4 * q + s
                            mm = nc.tensor.transpose(ps_t[q][:, s * P:(s + 1) * P],
                                                     p0[t % 2][:, st * P:(st + 1) * P], ident[:])
                        mm.then_inc(t0_filled, 1)

                def values0(t):
                    lt, gr = divmod(t, GROUPS)
                    if gr == 0:
                        pe.wait_ge(pv0_free, turns0 * LT + lt + 1)
                    pe.wait_ge(t0_lo, 2 * (t0 + t + 1) + 2)
                    for st in range(ST):
                        for x in range(2):
                            mm = nc.tensor.matmul(ps_m[lt % 2][:, gr * VW:gr * VW + 49], p16[t % 2][x][:, st, :],
                                                  v3[:, st, bass.ds(kv, 1), 0:49],
                                                  start=st == 0 and x == 0, stop=st == ST - 1 and x == 1)
                    mm.then_inc(pv0_done, 1)

                kv, turns0 = 0, b * KVH
                t0 = turns0 * STEPS0
                for t in range(3):
                    scores0(t)
                turned0(0)
                scores0(3)
                with pe.Fori(0, KVH - 1) as kv:
                    turns0 = b * KVH + kv
                    t0 = turns0 * STEPS0
                    for t in range(1, STEPS0 + 1):
                        turned0(t)
                        scores0(t + 3)
                        values0(t - 1)
                kv, turns0 = KVH - 1, b * KVH + KVH - 1
                t0 = turns0 * STEPS0
                for t in range(1, STEPS0):
                    turned0(t)
                    if t + 3 < STEPS0:
                        scores0(t + 3)
                    values0(t - 1)
                values0(STEPS0 - 1)

                n0 = nb + U_PROJ0
                pe.wait_ge(a0_done, KVH * LT * (b + 1))
                turn(b * TURNS, a0)
                pe.wait_ge(h_lo, CT * (b * TURNS + 1))
                pe.wait_ge(qk_lo, 2 * (b * QK_B) + 6)
                for lt in range(LT):
                    free(n0 + lt)
                    passes(ps_m[lt % 2][:], lambda x, c: hT[x][:, c, lt * P:(lt + 1) * P],
                           lambda y, c: w0o[y][:, c, :], CT).then_inc(bank_filled, 1)

                with pe.Fori(0, LAYERS) as y:
                    def project(n, slot, h, src, tokens):
                        free(n0 + n)
                        passes(ps_m[n % 2][:], lambda x, c: wa[x][:, slot, c, h * P:(h + 1) * P],
                               lambda q, c: src[q][:, c, tokens], CT).then_inc(bank_filled, 1)

                    def project_k(n, h, i):
                        project(n, 1, h, ctxT, slice(i * 512, (i + 1) * 512))

                    def project_q(n, h):
                        project(n, 0, h, hT, slice(0, L))

                    def project_v(n, i):
                        free(n0 + n)
                        for s in range(2):
                            st = 2 * i + s
                            mm = passes(ps_m[n % 2][:, s * 256:(s + 1) * 256],
                                        lambda x, c: ctxT[x][:, c, st * P:(st + 1) * P],
                                        lambda q, c: wa[q][:, 2, c, :], CT)
                        mm.then_inc(bank_filled, 1)

                    def projected(k):
                        pe.wait_ge(proj_lo, F0 + k + 3)

                    def extra_logits(n, k, h):
                        free(n0 + n)
                        projected(k)
                        for lt in range(LT):
                            for x in range(2):
                                mm = nc.tensor.matmul(ps_m[n % 2][:, 2 * lt:2 * lt + 2],
                                                      qT[h][x][:, lt * P:(lt + 1) * P], bkx[:, h, :],
                                                      start=x == 0, stop=x == 1)
                        mm.then_inc(bank_filled, 1)

                    def scores(t):
                        h, lt = t // LT % 2, t % LT
                        for n in range(2):
                            mm = passes(ps_s[t % 2][:, n * 512:(n + 1) * 512],
                                        lambda x, c: qT[h][x][:, lt * P:(lt + 1) * P],
                                        lambda q, c: kT[h][q][:, n * 512:(n + 1) * 512], 1)
                        mm.then_inc(s_filled, 1)

                    def turned(t):
                        pe.wait_ge(exp_done, T + t + 1)
                        for q in range(2):
                            pe.wait_ge(t_lo, 2 * (T + t) + q + 1)
                            for s in range(4):
                                st = 4 * q + s
                                mm = nc.tensor.transpose(ps_t[q][:, s * P:(s + 1) * P],
                                                         p[t % 2][:, st * P:(st + 1) * P], ident[:])
                            mm.then_inc(t_filled, 1)

                    def values(n, j):
                        h = j // 2
                        free(n0 + n)
                        for s in range(2):
                            t = 2 * j + s
                            nc.tensor.transpose(ps_m[n % 2][:, 256 + s * P:256 + (s + 1) * P],
                                                pext[:, t:t + 1].to_broadcast([P, P]), ident[:])
                        pe.wait_ge(t_lo, 2 * (T + 2 * j + 2) + 2)
                        passes(ps_m[n % 2][:, 0:256], lambda x, st: v[x][:, st, h * P:(h + 1) * P],
                               lambda q, st: pT[j % 2][q][:, st, :], ST).then_inc(bank_filled, 1)

                    def output(n, h):
                        pe.wait_ge(c_lo, 4 * it + 2 * h + 2)
                        for lt in range(LT):
                            free(n0 + n + lt)
                            passes(ps_m[(n + lt) % 2][:], lambda x, c: cT[x][:, h, lt * P:(lt + 1) * P],
                                   lambda q, c: wo[q][:, h, :], 1).then_inc(bank_filled, 1)

                    it = (b * LAYERS + y) * PAIRS
                    f0 = y * PAIRS
                    F0, T = it * F_PAIR, it * STEPS
                    n0 = nb + U_L0 + y * U_LAYER
                    pe.wait_ge(qk_lo, 2 * (b * QK_B + 2 + f0) + 4)
                    for h in range(2):
                        for i in range(2):
                            project_k((PRO_K0, PRO_K1)[h] + i, h, i)
                    turn(b * TURNS + 1 + y, h_tok, (b * 3 + y) * LT)
                    pe.wait_ge(v_lo, b * V_B + f0 + 2)
                    project_v(PRO_V[0], 0)
                    project_v(PRO_V[1], 1)
                    pe.wait_ge(h_lo, CT * (b * TURNS + 2 + y))
                    project_q(PRO_Q0, 0)
                    project_v(PRO_V[2], 2)
                    pe.wait_ge(col_done, 2 * (it + 1))
                    extra_logits(PRO_EX0, FP_Q0, 0)
                    scores(0)
                    project_q(PRO_Q1, 1)
                    project_v(PRO_V[3], 3)
                    extra_logits(PRO_EX1, FP_Q1, 1)
                    scores(1)
                    turned(0)
                    scores(2)
                    turned(1)
                    scores(3)
                    with pe.Fori(0, PAIRS - 1) as pr:
                        it = (b * LAYERS + y) * PAIRS + pr
                        f = f0 + pr
                        F0, T = (it + 1) * F_PAIR, it * STEPS
                        n0 = nb + U_L0 + y * U_LAYER + U_PRO + pr * U_PAIR
                        turned(2)
                        projected(FP_Q1 - F_PAIR)
                        scores(4)
                        projected(-1)
                        values(PV[0], 0)
                        pe.wait_ge(qk_lo, 2 * (b * QK_B + 3 + f) + 4)
                        project_q(Q0, 0)
                        turned(3)
                        scores(5)
                        project_k(K0[0], 0, 0)
                        turned(4)
                        scores(6)
                        values(PV[1], 1)
                        project_k(K0[1], 0, 1)
                        turned(5)
                        scores(7)
                        pe.wait_ge(col_done, 2 * (it + 2))
                        extra_logits(EX0, F_Q0, 0)
                        pe.wait_ge(o_lo, b * O_B + f + 2)
                        output(OUT0, 0)
                        turned(6)
                        projected(F_K0[1])
                        scores(8)
                        values(PV[2], 2)
                        project_q(Q1, 1)
                        turned(7)
                        scores(9)
                        project_k(K1[0], 1, 0)
                        project_k(K1[1], 1, 1)
                        extra_logits(EX1, F_Q1, 1)
                        turned(8)
                        scores(10)
                        values(PV[3], 3)
                        pe.wait_ge(v_lo, b * V_B + f + 3)
                        project_v(V[0], 0)
                        project_v(V[1], 1)
                        turned(9)
                        scores(11)
                        project_v(V[2], 2)
                        project_v(V[3], 3)
                        output(OUT1, 1)
                    it = (b * LAYERS + y) * PAIRS + PAIRS - 1
                    F0, T = (it + 1) * F_PAIR, it * STEPS
                    n0 = nb + U_L0 + (y + 1) * U_LAYER - U_LAST
                    turned(2)
                    projected(FP_Q1 - F_PAIR)
                    scores(4)
                    projected(-1)
                    values(LAST_PV[0], 0)
                    turned(3)
                    scores(5)
                    turned(4)
                    scores(6)
                    values(LAST_PV[1], 1)
                    turned(5)
                    scores(7)
                    turned(6)
                    pe.wait_ge(o_lo, b * O_B + f0 + PAIRS + 1)
                    output(LAST_OUT0, 0)
                    values(LAST_PV[2], 2)
                    turned(7)
                    values(LAST_PV[3], 3)
                    output(LAST_OUT1, 1)

                n0 = nb + U_B - U_MLP
                turn(b * TURNS + 3, h_tok, (b * 3 + 2) * LT)
                pe.wait_ge(h_lo, CT * (b * TURNS + 4))

                def hidden(fp):
                    slot = fp % 2
                    pe.wait_ge(qk_lo, 2 * (b * QK_B + 2 + V_B + fp // 2) + slot + 3)
                    for i in range(2):
                        free(n0 + 2 * fp + i)
                        passes(ps_m[i][:], lambda x, c: wa[x][:, slot, c, i * P:(i + 1) * P],
                               lambda q, c: hT[q][:, c, :], CT).then_inc(bank_filled, 1)

                def product(fp):
                    pe.wait_ge(o_lo, b * O_B + V_B + fp + 2)
                    for i in range(2):
                        pe.wait_ge(g_lo, (b * FPAIRS + fp) * 2 + i + 3)
                        for lt in range(LT):
                            mm = passes(ps_s[lt // 2][:, (lt % 2) * 512:(lt % 2 + 1) * 512],
                                        lambda x, c: gT[fp % 2][i][x][:, lt * P:(lt + 1) * P],
                                        lambda q, c: wo[q][:, i, :], 1,
                                        start=fp == 0 and i == 0, stop=fp == FPAIRS - 1 and i == 1)
                    mm.then_inc(mlp_out, 1)

                hidden(0)
                for fp in range(FPAIRS):
                    if fp + 1 < FPAIRS:
                        hidden(fp + 1)
                    product(fp)

        @block.vector
        def _(dve):
            step = [0, 0]

            def link(ins):
                step[1] += 1
                ins.then_inc(dve_step, 1)
                dve.wait_ge(dve_step, step[0] + step[1])

            def apart():
                dve.sem_inc(apart_dve, 1)

            def section(start, count=None):
                if count is not None:
                    assert step[1] == count, (step[1], count)
                step[0], step[1] = start, 0

            sub = ALU.subtract
            dve.sem_inc(bank_free, 2)
            dve.sem_inc(pv0_free, 2)
            dve.sem_inc(t0_lo, 2)
            dve.sem_inc(t_lo, 2)
            dve.sem_inc(g_lo, 2)
            dve.sem_inc(batch_done, 1)
            dve.wait_ge(const_in, 16 * 5)

            def norm(k, eps, between):
                for lt in range(LT):
                    mm = nc.vector.bn_stats(stats[:, lt, :], x_res[:, lt, :])
                link(mm)
                apart()
                for lt in range(LT):
                    mm = nc.vector.bn_aggr(mean_var[:, lt, :], stats[:, lt, :])
                link(mm)
                nc.vector.tensor_scalar(lnv[:, 0, :], mean_var[:, :, 1], eps, None, ALU.add).then_inc(var_done, 1)
                between()
                dve.wait_ge(sqrt_done, k + 1)
                link(nc.vector.reciprocal(lnv[:, 2, :], lnv[:, 1, :]))
                link(nc.vector.tensor_tensor(lnv[:, 2, :], lnv[:, 2, :], lnv[:, 0, :], ALU.mult))
                link(nc.vector.tensor_tensor(lnv[:, 3, :], lnv[:, 2, :], lnv[:, 1, :], ALU.add))
                link(nc.vector.reciprocal(lnv[:, 4, :], lnv[:, 3, :]))
                link(nc.vector.tensor_scalar(lnv[:, 4, :], lnv[:, 4, :], 2.0, None, ALU.mult))

            def normal(out, lt):
                return nc.vector.tensor_scalar(out[:, lt, :], x_res[:, lt, :], mean_var[:, lt, 0:1],
                                               lnv[:, 4, lt:lt + 1], sub, ALU.mult)

            def tokens_normal():
                for lt in range(LT):
                    normal(h_tok, lt).then_inc(ln_done, 1)

            def features(k, col):
                def column(i, c):
                    if isinstance(col, int):
                        return lnc[:, col + i * CT + c:col + i * CT + c + 1]
                    return lnc[:, bass.ds(col + i * CT + c, 1)]

                for i, c in enumerate(TURN_ORDER):
                    dve.wait_ge(turn_filled, CT * k + i + 1)
                    nc.vector.tensor_scalar(h_fea[:, c, :], turned_bank(c), column(0, c), column(1, c),
                                            ALU.mult, ALU.add).then_inc(h_done, 1)
                for i in range(2, CT):
                    c = TURN_ORDER[i]
                    dve.wait_ge(h_hi, CT * k + i + 1)
                    nc.vector.tensor_tensor(hT[1][:, c, :], h_fea[:, c, :], f32(hT[0][:, c, :]), sub).then_inc(h_lo, 1)

            with dve.Fori(0, B) as b:
                nb = b * U_B
                section(b * DVE_B)
                for c in range(CT):
                    dve.wait_ge(in_hi, b * (CT + 2) + 1 + c + 1)
                    nc.vector.tensor_tensor(ctxT[1][:, c, :], st_ctx[:, c, :], f32(ctxT[0][:, c, :]), sub)\
                        .then_inc(in_lo, 1)
                dve.wait_ge(in_hi, (b + 1) * (CT + 2))
                nc.vector.tensor_tensor(hT[1][:], st_x[:], f32(hT[0][:]), sub).then_inc(in_lo, 1)

                def three_parts(i, n, col, scale):
                    dve.wait_ge(bank_filled, nb + n + 1)
                    t, u = tmp0[0][:], tmp0[1][:]
                    link(nc.vector.tensor_scalar(t, ps_m[n % 2][:], col, scale, ALU.add, ALU.mult))
                    dve.sem_inc(bank_free, 1)
                    if i >= 2:
                        dve.wait_ge(scr_out, 16 * (b * 6 + i - 1))
                    part = parts[i % 2]
                    link(nc.vector.tensor_copy(part[:, 0, :], t))
                    link(nc.vector.tensor_tensor(u, t, part[:, 0, :], sub))
                    link(nc.vector.tensor_copy(part[:, 1, :], u))
                    nc.vector.tensor_tensor(part[:, 2, :], u, part[:, 1, :], sub).then_inc(part_done, 1)
                    dve.wait_ge(part_done, b * 6 + i + 1)

                for i in range(2):
                    three_parts(i, i, cols0[:, 4:5], 1.0)
                nc.vector.memset(v3[:, :, :, 48:49], 1.0).then_inc(v3_done, 1)
                for i in range(4):
                    dve.wait_ge(bank_filled, nb + 2 + i + 1)
                    t = tmp0[0][:, 0:256].rearrange("p (s n) -> p s n", s=2)
                    link(nc.vector.tensor_tensor(t, ps_m[i % 2][:].rearrange("p (s n) -> p s n", s=2)[:, :, P:256],
                                                 bv0[:].unsqueeze(1).to_broadcast([P, 2, P]), ALU.add))
                    dve.sem_inc(bank_free, 1)
                    t = tmp0[0][:, 0:256].rearrange("p (s a e) -> p s a e", s=2, e=HD)
                    u = tmp0[1][:, 0:256].rearrange("p (s a e) -> p s a e", s=2, e=HD)
                    dst = [v3[:, 2 * i:2 * i + 2, :, x * HD:(x + 1) * HD] for x in range(3)]
                    link(nc.vector.tensor_copy(dst[0], t))
                    link(nc.vector.tensor_tensor(u, t, dst[0], sub))
                    link(nc.vector.tensor_copy(dst[1], u))
                    nc.vector.tensor_tensor(dst[2], u, dst[1], sub).then_inc(v3_done, 1)
                    dve.wait_ge(v3_done, b * 5 + i + 2)
                for i in range(4):
                    three_parts(2 + i, 6 + i, cols0[:, i:i + 1], SCALE0)
                section(b * DVE_B + DVE_PROJ0, DVE_PROJ0)

                dve.wait_ge(mask_in, 16 * (b + 1))
                apart()

                def maxima0(t):
                    lt, i = t % STEPS0 // GROUPS, t % 2
                    if t >= 2:
                        dve.wait_ge(exp0_done, t0 + t - 1)
                    dve.wait_ge(s0_filled, t0 + t + 1)
                    apart()
                    nc.vector.tensor_tensor_reduce(sm[i][:], ps_s[i][:], mask[:, lt, :], 1.0, -3.0e38,
                                                   ALU.add, ALU.max, nm0[0][:, i:i + 1]).then_inc(raw0_done, 1)

                def shift0(t):
                    i = t % 2
                    dve.wait_ge(raw0_done, t0 + t + 1)
                    nc.vector.tensor_scalar(nm0[1][:, i:i + 1], nm0[0][:, i:i + 1], -1.0, LOG_P_TOP,
                                            ALU.mult, ALU.add).then_inc(max0_done, 1)

                def lo0(t, q):
                    dve.wait_ge(t0_hi, 2 * (t0 + t) + q + 1)
                    part = p16[t % 2]
                    nc.vector.tensor_tensor(part[1][:, 4 * q:4 * q + 4, :],
                                            ps_t[q][:].rearrange("p (s n) -> p s n", s=4),
                                            part[0][:, 4 * q:4 * q + 4, :], sub).then_inc(t0_lo, 1)

                def normalised(lt):
                    dve.wait_ge(pv0_done, t0 + (lt + 1) * GROUPS + 2)
                    out = ps_m[lt % 2][:, 0:GROUPS * VW].rearrange("p (g w) -> p g w", w=VW)
                    nc.vector.reciprocal(rden0[:], out[:, :, 48])
                    nc.vector.tensor_reduce(red0[:], out[:, :, 0:48].rearrange("p g (x e) -> p g e x", x=3),
                                            AX.X, ALU.add).then_inc(pv0_free, 1)
                    dve.wait_ge(pv0_free, turns0 * LT + lt + 3)
                    dst = a0[:, lt, bass.ds(kv * GROUPS * HD, GROUPS * HD)].rearrange("p (g e) -> p g e", g=GROUPS)
                    nc.vector.tensor_tensor(dst, red0[:], rden0[:].unsqueeze(2).to_broadcast([P, GROUPS, HD]),
                                            ALU.mult).then_inc(a0_done, 1)

                def step0(t, ahead=True):
                    if ahead:
                        maxima0(t + 2)
                    lo0(t, 0)
                    if ahead:
                        shift0(t + 2)
                    lo0(t, 1)

                turns0 = b * KVH
                t0 = turns0 * STEPS0
                for t in range(2):
                    maxima0(t)
                    shift0(t)
                for t in range(2):
                    step0(t)
                with dve.Fori(0, KVH - 1) as kv:
                    turns0 = b * KVH + kv
                    t0 = turns0 * STEPS0
                    for t in range(2, STEPS0 + 2):
                        step0(t)
                        if t % GROUPS == 1:
                            normalised(t // GROUPS - 1)
                kv, turns0 = KVH - 1, b * KVH + KVH - 1
                t0 = turns0 * STEPS0
                for t in range(2, STEPS0):
                    step0(t, t + 2 < STEPS0)
                    if t % GROUPS == 1:
                        normalised(t // GROUPS - 1)
                normalised(LT - 1)

                n0 = nb + U_PROJ0
                for i, c in enumerate(TURN_ORDER):
                    dve.wait_ge(h_hi, CT * (b * TURNS) + i + 1)
                    nc.vector.tensor_tensor(hT[1][:, c, :], turned_bank(c), f32(hT[0][:, c, :]), sub).then_inc(h_lo, 1)
                dve.wait_ge(row_added, b * TURNS + 2)
                for lt in range(LT):
                    dve.wait_ge(bank_filled, n0 + lt + 1)
                    nc.vector.tensor_tensor(x_res[:, lt, :], ps_m[lt % 2][:], x_res[:, lt, :], ALU.add)\
                        .then_inc(bank_free, 1)
                dve.wait_ge(bank_free, n0 + LT + 2)
                apart()
                norm(b * TURNS, EPS0, lambda: None)
                for lt in range(LT):
                    mm = normal(x_res, lt)
                link(mm)
                dve.wait_ge(rows0_in, 16 * (b + 1))
                for i, op in enumerate((ALU.mult, ALU.add)):
                    for lt in range(LT):
                        mm = nc.vector.tensor_tensor(x_res[:, lt, :], x_res[:, lt, :], stg_o[:, i, :], op)
                    link(mm)
                dve.sem_inc(l0_done, 1)

                with dve.Fori(0, LAYERS) as y:
                    def column(kind, h):
                        return cols[:, bass.ds(at_cols + kind * HEADS + h, 1)]

                    def add_column(n, k, kind, h):
                        dve.wait_ge(bank_filled, n0 + n + 1)
                        dve.wait_ge(proj_lo, F0 + k + 1)
                        nc.vector.tensor_scalar(proj[k % 2][:], ps_m[n % 2][:], column(kind, h), None, ALU.add)\
                            .then_inc(bank_free, 1)

                    def add_bv(n, k):
                        dve.wait_ge(bank_filled, n0 + n + 1)
                        dve.wait_ge(proj_lo, F0 + k + 1)
                        nc.vector.tensor_tensor(proj[k % 2][:].rearrange("p (s n) -> p s n", s=2),
                                                ps_m[n % 2][:].rearrange("p (s n) -> p s n", s=2),
                                                bv_row[:].unsqueeze(1).to_broadcast([P, 2, 256]), ALU.add)\
                            .then_inc(bank_free, 1)

                    def extra_columns(pair):
                        bias_k = cols[:, bass.ds(at_cols + 2 * HEADS, 2)]
                        nc.vector.tensor_copy(bkx[:, :, 0], bias_k).then_inc(col_done, 1)
                        dve.wait_ge(col_done, 2 * pair + 1)
                        nc.vector.tensor_tensor(bkx[:, :, 1], bias_k, f32(bkx[:, :, 0]), sub).then_inc(col_done, 1)

                    def extra_logits(n, h):
                        dve.wait_ge(bank_filled, n0 + n + 1)
                        src = ps_m[n % 2][:, 0:2 * LT].rearrange("p (l x) -> p l x", x=2)
                        nc.vector.tensor_reduce(lb[:, h, :], src, AX.X, ALU.add)
                        nc.vector.tensor_reduce(nlb[:, h, :], src, AX.X, ALU.add, negate=True).then_inc(bank_free, 1)

                    def maxima(t, extra=None):
                        h, lt, i = t // LT % 2, t % LT, t % STEPS
                        dve.wait_ge(s_filled, T + t + 1)
                        nc.vector.tensor_reduce(nmx[:, i:i + 1], ps_s[t % 2][:], AX.X, ALU.max, negate=True)\
                            .then_inc(raw_done, 1)
                        dve.wait_ge(raw_done, T + t + 1)
                        if extra is not None:
                            dve.wait_ge(bank_free, n0 + extra + 3)
                        nc.vector.tensor_scalar(nm[:, i:i + 1], nmx[:, i:i + 1], nlb[:, h, lt:lt + 1], SCALE1,
                                                ALU.min, ALU.mult).then_inc(nm_done, 1)

                    def turned(t):
                        off = (t % 2) * P
                        for q in range(2):
                            dve.wait_ge(t_hi, 2 * (T + t) + q + 1)
                            part = [x[:, 4 * q:4 * q + 4, off:off + P] for x in pT[t // 2 % 2]]
                            nc.vector.tensor_tensor(part[1], ps_t[q][:].rearrange("p (s n) -> p s n", s=4),
                                                    f32(part[0]), sub).then_inc(t_lo, 1)

                    def extra_value(n, j):
                        h = j // 2
                        dve.wait_ge(px_copied, 4 * it + j + 1)
                        if j >= 2:
                            dve.wait_ge(c_lo, 4 * it + j - 1)
                        nc.vector.scalar_tensor_tensor(out=cf[j % 2][:], in0=pextb[j % 2][:],
                                                       scalar=column(3, h), in1=ps_m[n % 2][:, 0:256],
                                                       op0=ALU.mult, op1=ALU.add).then_inc(bank_free, 1)

                    def denominators(h):
                        hs = slice(h * LT, (h + 1) * LT)
                        dve.wait_ge(exp_done, T + (h + 1) * LT)
                        nc.vector.tensor_tensor(z[:, hs], sums[:, hs], pext[:, hs], ALU.add).then_inc(den_done, 1)
                        dve.wait_ge(den_done, 4 * it + 2 * h + 1)
                        nc.vector.reciprocal(r[:, hs], z[:, hs]).then_inc(den_done, 1)

                    def output(n, h):
                        dve.wait_ge(den_done, 4 * it + 2 * h + 2)
                        for lt in range(LT):
                            dve.wait_ge(bank_filled, n0 + n + lt + 1)
                            t = h * LT + lt
                            nc.vector.scalar_tensor_tensor(
                                out=x_res[:, lt, :], in0=ps_m[(n + lt) % 2][:], scalar=r[:, t:t + 1],
                                in1=x_res[:, lt, :], op0=ALU.mult, op1=ALU.add).then_inc(bank_free, 1)

                    it = (b * LAYERS + y) * PAIRS
                    F0, T = it * F_PAIR, it * STEPS
                    n0 = nb + U_L0 + y * U_LAYER
                    at_cols = y * 4 * HEADS
                    section(b * DVE_B + DVE_PROJ0 + DVE_OUT0 + y * DVE_NORM, DVE_OUT0)

                    def between():
                        for i in range(2):
                            add_column(PRO_K0 + i, FP_K0[i], 1, 0)

                    dve.wait_ge(bank_free, n0 + 2)
                    apart()
                    norm(b * TURNS + 1 + y, EPS1, between)
                    tokens_normal()
                    for i in range(2):
                        add_column(PRO_K1 + i, FP_K1[i], 1, 1)
                    extra_columns(it)
                    features(b * TURNS + 1 + y, y * 2 * CT)
                    dve.wait_ge(bv_in, 16 * (b * V_B + y * PAIRS + 1))
                    add_bv(PRO_V[0], FP_V[0])
                    add_bv(PRO_V[1], FP_V[1])
                    add_column(PRO_Q0, FP_Q0, 0, 0)
                    add_bv(PRO_V[2], FP_V[2])
                    extra_logits(PRO_EX0, 0)
                    maxima(0, PRO_EX0)
                    add_column(PRO_Q1, FP_Q1, 0, 1)
                    add_bv(PRO_V[3], FP_V[3])
                    extra_logits(PRO_EX1, 1)
                    maxima(1, PRO_EX1)
                    turned(0)
                    maxima(2)
                    turned(1)
                    maxima(3)
                    dve.wait_ge(row_added, b * TURNS + 2 + y + 1)
                    apart()
                    with dve.Fori(0, PAIRS - 1) as pr:
                        it = (b * LAYERS + y) * PAIRS + pr
                        F0, T = (it + 1) * F_PAIR, it * STEPS
                        n0 = nb + U_L0 + y * U_LAYER + U_PRO + pr * U_PAIR
                        at_this = y * 4 * HEADS + pr * 2
                        at_next = at_this + 2
                        for t in range(2, STEPS + 2):
                            turned(t)
                            maxima(t + 2, {6: EX0, 8: EX1}.get(t))
                            if t % 2 == 0:
                                at_cols = at_this
                                extra_value(PV[t // 2 - 1], t // 2 - 1)
                                at_cols = at_next
                            if t == 2:
                                extra_columns(it + 1)
                                add_column(Q0, F_Q0, 0, 0)
                                denominators(0)
                            if t == 3:
                                add_column(K0[0], F_K0[0], 1, 0)
                            if t == 4:
                                add_column(K0[1], F_K0[1], 1, 0)
                            if t == 5:
                                extra_logits(EX0, 0)
                                output(OUT0, 0)
                            if t == 6:
                                add_column(Q1, F_Q1, 0, 1)
                                denominators(1)
                            if t == 7:
                                add_column(K1[0], F_K1[0], 1, 1)
                                add_column(K1[1], F_K1[1], 1, 1)
                                extra_logits(EX1, 1)
                            if t == 8:
                                dve.wait_ge(bv_in, 16 * (b * V_B + y * PAIRS + pr + 2))
                            if t >= STEPS:
                                for i in range(2 * (t - STEPS), 2 * (t - STEPS) + 2):
                                    add_bv(V[i], F_V[i])
                        output(OUT1, 1)
                    it = (b * LAYERS + y) * PAIRS + PAIRS - 1
                    T = it * STEPS
                    n0 = nb + U_L0 + (y + 1) * U_LAYER - U_LAST
                    at_cols = y * 4 * HEADS + (PAIRS - 1) * 2
                    for t in range(2, STEPS):
                        turned(t)
                        if t + 2 < STEPS:
                            maxima(t + 2)
                        if t == 2:
                            denominators(0)
                        if t == 6:
                            denominators(1)
                            output(LAST_OUT0, 0)
                        if t % 2 == 0:
                            extra_value(LAST_PV[t // 2 - 1], t // 2 - 1)
                    extra_value(LAST_PV[3], 3)
                    output(LAST_OUT1, 1)

                section(b * DVE_B + DVE_PROJ0 + DVE_OUT0 + LAYERS * DVE_NORM, DVE_NORM)
                dve.wait_ge(bank_free, nb + U_B - U_MLP + 2)
                apart()
                norm(b * TURNS + 3, EPS1, lambda: None)
                tokens_normal()
                features(b * TURNS + 3, LAYERS * 2 * CT)
                for fp in range(FPAIRS):
                    for i in range(2):
                        dve.wait_ge(g_hi, (b * FPAIRS + fp) * 2 + i + 1)
                        nc.vector.tensor_tensor(gT[fp % 2][i][1][:], g[i][:], f32(gT[fp % 2][i][0][:]), sub)\
                            .then_inc(g_lo, 1)
                dve.wait_ge(row_added, b * TURNS + 5)
                dve.wait_ge(mlp_out, FPAIRS * (b + 1))
                for lt in range(LT):
                    nc.vector.tensor_tensor(x_res[:, lt, :], ps_s[lt // 2][:, (lt % 2) * 512:(lt % 2 + 1) * 512],
                                            x_res[:, lt, :], ALU.add).then_inc(out_ready, 1)
                dve.wait_ge(out_ready, LT * (b + 1))
                dve.sem_inc(batch_done, 1)
                assert step[1] == DVE_NORM, step


DVE_NORM = 2 + 5
DVE_PROJ0 = 6 * 4 + 4 * 4
DVE_OUT0 = DVE_NORM + 3
DVE_B = DVE_PROJ0 + DVE_OUT0 + (LAYERS + 1) * DVE_NORM


def laid_out(inputs):
    i = {k: np.asarray(v) for k, v in inputs.items()}
    x, c = i["x"], i["ctx_2048"]

    def tiles(w):
        return w.reshape(-1, P, w.shape[1]).transpose(1, 0, 2)

    def both(name):
        return [i[f"L1_xattn_{name}{y}"] for y in (1, 2)]

    d = {
        "x": x.reshape(B, LT, P, D).transpose(0, 2, 1, 3),
        "xT": x.transpose(0, 2, 1).reshape(B, CT, P, L).transpose(0, 2, 1, 3),
        "ctxT": c.transpose(0, 2, 1).reshape(B, CT, P, S).transpose(0, 2, 1, 3),
        "mask": i["mask_Bx1xSxS2_ff0"].reshape(B, LT, P, S).transpose(0, 2, 1, 3),
        "w0q": tiles(i["L0_xattn_Wq"]).reshape(P, 2, CT * 256),
        "w0o": tiles(i["L0_xattn_Wo"]).reshape(P, 2, CT * 256),
        "w0kv": tiles(np.concatenate([i["L0_xattn_Wk"], i["L0_xattn_Wv"]], axis=1)),
        "cols0": np.concatenate([i["L0_xattn_bq"].reshape(CT, P).T, i["L0_xattn_bk"].reshape(1, P).T], axis=1),
        "bv0": i["L0_xattn_bv"],
    }
    qkv = np.stack([np.stack([tiles(w).reshape(P, CT, PAIRS, 256).transpose(2, 0, 1, 3) for w in ws], axis=2)
                    for ws in zip(both("wq"), both("wk"), both("wv"))]).reshape(LAYERS * PAIRS, P, 3, CT * 256)
    w1 = tiles(i["L1_xattn_w_fc1"]).reshape(P, CT, FPAIRS // 2, 2, 256).transpose(2, 0, 3, 1, 4)
    d["wqk"] = np.concatenate([qkv[:, :, 0:2], w1.reshape(FPAIRS // 2, P, 2, CT * 256)])
    d["wv"] = qkv[:, :, 2]
    d["wo"] = np.concatenate([w.reshape(-1, 2, P, D).transpose(0, 2, 1, 3) for w in (*both("wo"), i["L1_xattn_w_fc2"])])
    d["bv"] = np.stack(both("bv")).reshape(LAYERS * PAIRS, 256)
    d["cols"] = np.stack([np.stack([a.reshape(HEADS, KD).T for a in cs], axis=1)
                          for cs in zip(both("bq"), both("bk"), both("bias_k"), both("bias_v"))], axis=1)\
        .reshape(P, LAYERS * 4 * HEADS)
    norms = [np.stack([i[f"L1_xattn_ln{n}_{w}"].reshape(CT, P).T for w in ("scale", "offset")], axis=1)
             for n in ("1", "2", "_mlp")]
    d["lnc"] = np.stack(norms, axis=1).reshape(P, (LAYERS + 1) * 2 * CT)
    d["rows0"] = np.stack([i["L0_xattn_gamma"], i["L0_xattn_beta"]])
    d["rows"] = np.stack([i[n] for n in ("L0_xattn_bo", "L1_xattn_bo1", "L1_xattn_bo2", "L1_xattn_b_fc2")])
    d["colf"] = i["L1_xattn_b_fc1"].reshape(F // P, P).T
    return {k: np.ascontiguousarray(a) for k, a in d.items()}


def kernel(**inputs):
    import concourse.bacc as bacc
    from concourse.bass_utils import run_bass_kernel_spmd

    nc = bacc.Bacc("TRN2", target_bir_lowering=False, num_devices=1)
    arrays = laid_out(inputs)
    d = {k: nc.dram_tensor(f"in_{k}", a.shape, F32, kind="ExternalInput").ap() for k, a in arrays.items()}
    d["out"] = nc.dram_tensor("out", [B, P, LT, D], F32, kind="ExternalOutput").ap()
    build(nc, d)
    got = run_bass_kernel_spmd(nc, [{f"in_{k}": a for k, a in arrays.items()}], core_ids=[0]).results[0]["out"]
    return np.ascontiguousarray(np.asarray(got).reshape(B, P, LT, D).transpose(0, 2, 1, 3).reshape(B, L, D))
```

```python
from contextlib import ExitStack

import numpy as np

import concourse.bass as bass
from concourse import mybir

F32 = mybir.dt.float32
F32R = mybir.dt.float32r
BF16 = mybir.dt.bfloat16
F16 = mybir.dt.float16
ALU = mybir.AluOpType
ACT = mybir.ActivationFunctionType
AX = mybir.AxisListType

P = 128
B, L, S, D = 2, 512, 1024, 512
CT, LT, ST = D // P, L // P, S // P
KVH, GROUPS, HD = 8, 4, 16
NH0 = KVH * GROUPS
LAYERS, HEADS, KD = 2, 16, 128
PAIRS = HEADS // 2
F = 2048
FPAIRS = F // 256
SCALE0 = HD ** -0.5
SCALE1 = KD ** -0.5
EPS0, EPS1 = 1e-6, 1e-5
P_TOP = 4096.0
Q_ORDER = (0, 0, 1, 1, 0, 2)
K_ORDER = (0, 1, 0, 1, 2, 0)
STACK = HD * len(Q_ORDER)
VW = 64

STEPS0 = LT * GROUPS
STEPS = 2 * LT
P_V, P_Q = (2, 3, 5, 6), (4, 7, 8, 9)
T_OUT, T_K0, T_K1, T_V, T_START = 0, (4, 5), (6, 7), (8, 9), 10
S_V2, S_Q0, S_Q1, S_EX0, S_EX1, S_V3, U_START = range(7)
PV = (1, 3, 8, 15)
Q0, K0, EX0, OUT0, Q1 = 0, (2, 4), 5, (6, 7, 9, 11), 10
K1, EX1, V, OUT1 = (12, 13), 14, (16, 17, 19, 22), (18, 20, 21, 23)
L_PV, L_K0, L_OUT0, L_K1 = (0, 3, 7, 11), (1, 2), (5, 6, 8, 10), (4, 9)
L_V, L_OUT1, L_START = (12, 17), (13, 14, 15, 16), 18
E_PV, E_OUT0, E_OUT1 = (0, 1, 4, 7), (2, 3, 5, 6), (8, 9, 10, 11)
U_PROJ0, U_TAIL, U_PAIR, U_LAST, U_MLP = 10, T_START + U_START, 24, L_START + U_START, 2 * FPAIRS
U_LOOP = [U_PROJ0 + U_TAIL + y * ((PAIRS - 1) * U_PAIR + U_LAST) for y in range(LAYERS)]
U_END = [u + (PAIRS - 1) * U_PAIR for u in U_LOOP]
U_B = U_END[-1] + 12 + U_MLP
F_Q0, F_K0, F_Q1, F_K1, F_V = 0, (1, 2), 3, (4, 5), (6, 7, 8, 9)
FS_K0, FS_K1, FS_V, FS_Q0, FS_Q1 = (0, 1), (2, 3), (4, 5, 6, 9), 7, 8
F_PAIR = 10
QK_B = 2 + LAYERS * PAIRS + FPAIRS // 2
V_B = LAYERS * PAIRS
O_B = LAYERS * PAIRS + FPAIRS
TURNS = 2 + LAYERS
TURN_ORDER = (2, 3, 0, 1)
PASSES = ((0, 0), (0, 1), (1, 0))


def build(nc, d):
    with ExitStack() as ctx:
        sems = {}

        def sem(name):
            sems[name] = ctx.enter_context(nc.semaphore(name))
            return sems[name]

        start = (nc.sbuf_base + 31) // 32 * 32
        at = [start]

        def sb(name, shape, dt, n=1):
            size = int(np.prod(shape[1:])) * (2 if dt in (BF16, F16) else 4)
            made = []
            for i in range(n):
                made.append(nc.alloc_sbuf_tensor_at(name if n == 1 else f"{name}{i}", shape, dt, offset=at[0]))
                at[0] += (size + 31) // 32 * 32
            return made[0] if n == 1 else made

        ctxT = sb("ctxT", [P, CT, S], F32R, 2)
        hT = sb("hT", [P, CT, L], F32R, 2)
        x_res = sb("x_res", [P, LT, D], F32)
        row = sb("row", [P, D], F32)
        stg_qk = sb("stg_qk", [P, 2, CT * 256], F32)
        stg_v = sb("stg_v", [P, CT * 256], F32)
        stg_o = sb("stg_o", [P, 2, D], F32)
        bv_row = sb("bv_row", [P, 256], F32)
        ident = sb("ident", [P, P], F32)
        zero = sb("zero", [P, 1], F32)
        cols = sb("cols", [P, LAYERS * 4 * HEADS], F32)
        lnc = sb("lnc", [P, (LAYERS + 1) * 2 * CT], F32)
        cols0 = sb("cols0", [P, 5], F32)
        cols0q = sb("cols0q", [P, 4], F32)
        colf = sb("colf", [P, F // P], F32)
        bv0 = sb("bv0", [P, P], F32)
        stats = sb("stats", [P, LT, 6], F32)
        mean_var = sb("mean_var", [P, LT, 2], F32)
        lnv = sb("lnv", [P, 5, LT], F32)
        region = at[0]

        q_stack = sb("q_stack", [STACK, NH0, L], BF16)
        k_stack = sb("k_stack", [STACK, KVH, S], BF16)
        v3 = sb("v3", [P, ST, KVH, VW], BF16)
        mask = sb("mask", [P, LT, S], F32)
        loop0 = at[0]
        sm = sb("sm", [P, S], F32, 2)
        p0 = sb("p0", [P, S], F32, 2)
        p16 = [sb(f"p16_{i}", [P, ST, P], F16, 2) for i in range(2)]
        p32 = sb("p32", [P, ST // 2, P], F32, 2)
        end0 = at[0]
        at[0] = loop0
        w0q = sb("w0q", [P, CT, D], F32R, 2)
        w0kv = sb("w0kv", [P, CT, 256], F32R, 2)
        assert at[0] <= end0
        at[0] = inputs_at = end0
        w0o = sb("w0o", [P, CT, D], F32R, 2)
        parts_at = at[0]
        a0 = sb("a0", [P, LT, D], F32)
        nm0 = sb("nm0", [P, 2], F32)
        red0 = sb("red0", [P, GROUPS, HD], F32)
        rden0 = sb("rden0", [P, GROUPS], F32)
        tmp0 = sb("tmp0", [P, 512], F32, 2)
        tmp_lo = sb("tmp_lo", [P, 512], F32)
        ends = [at[0]]
        at[0] = parts_at
        parts = sb("parts", [P, 3, 512], BF16, 2)
        at[0] = inputs_at
        st_ctx = sb("st_ctx", [P, CT, S], F32)
        st_x = sb("st_x", [P, CT, L], F32)
        st_kv = sb("st_kv", [P, CT, 256], F32)
        ends.append(at[0])

        at[0] = region
        wa = sb("wa", [P, 3, CT, 256], F32R, 2)
        wo = sb("wo", [P, 2, D], F32R, 2)
        proj = sb("proj", [P, 512], F32, 2)
        projected_at = at[0]
        kT = [sb(f"kT{h}_", [P, S], F32R, 2) for h in range(2)]
        qT = [sb(f"qT{h}_", [P, L], F32R, 2) for h in range(2)]
        v = sb("v", [P, ST, 256], F32R, 2)
        p = sb("p", [P, S], F32, 2)
        turned_at = at[0]
        pT = [sb(f"pT{i}_", [P, ST, 256], F32R, 2) for i in range(2)]
        cT = sb("cT", [P, 2, L], F32R, 2)
        cf = sb("cf", [P, 256], F32, 2)
        pextb = sb("pextb", [P, 256], F32, 2)
        bkx = sb("bkx", [P, 2, 2], F32R)
        lb = sb("lb", [P, 2, LT], F32)
        nlb = sb("nlb", [P, 2, LT], F32)
        nmx = sb("nmx", [P, STEPS], F32)
        nm = sb("nm", [P, STEPS], F32)
        pext = sb("pext", [P, STEPS], F32)
        sums = sb("sums", [P, STEPS], F32)
        z = sb("z", [P, STEPS], F32)
        r = sb("r", [P, STEPS], F32)
        ends.append(at[0])
        at[0] = turned_at
        h_tok = sb("h_tok", [P, LT, D], F32)
        h_fea = sb("h_fea", [P, CT, L], F32)
        at[0] = projected_at
        g = sb("g", [P, L], F32, 2)
        gT = [[sb(f"gT{k}{i}_", [P, L], F32R, 2) for i in range(2)] for k in range(2)]
        at[0] = max(at[0], loop0)
        wo_even = sb("wo_even", [P, 2, D], F32R, 2)
        assert at[0] <= turned_at
        w2 = (wo_even, wo)
        assert max(ends) <= nc.sbuf_usable_end, (max(ends), nc.sbuf_usable_end)

        ps_s = [ctx.enter_context(nc.psum_tensor(f"ps_s{i}", [P, S], F32)) for i in range(2)]
        ps_t = [ctx.enter_context(nc.psum_tensor(f"ps_t{i}", [P, 512], F32)) for i in range(2)]
        ps_m = [ctx.enter_context(nc.psum_tensor(f"ps_m{i}", [P, 512], F32)) for i in range(2)]

        scr_k = nc.dram_tensor("scr_k", [2, P, 3, 512], BF16, kind="Internal").ap()
        scr_q = nc.dram_tensor("scr_q", [4, P, 3, 512], BF16, kind="Internal").ap()

        const_in = sem("const_in")
        xres_in, kv_in, ctx_in, x_in = sem("xres_in"), sem("kv_in"), [sem(f"ctx_in{c}") for c in range(CT)], sem("x_in")
        mask_in, row_in, rows0_in = sem("mask_in"), sem("row_in"), sem("rows0_in")
        qk_in, v_in, o_in, bv_in = sem("qk_in"), sem("v_in"), sem("o_in"), sem("bv_in")
        scr_out, stack_in, stack_rest = sem("scr_out"), sem("stack_in"), sem("stack_rest")
        out_done = sem("out_done")
        const_made, zero_made = sem("const_made"), sem("zero_made")
        in_hi = sem("in_hi")
        kv_lo, ctx_lo, x_lo = sem("kv_lo"), sem("ctx_lo"), sem("x_lo")
        cols_scaled = sem("cols_scaled")
        wide_done = sem("wide_done")
        qk_hi, qk_lo = sem("qk_hi"), sem("qk_lo")
        v_hi, v_lo = sem("v_hi"), sem("v_lo")
        o_hi, o_lo = sem("o_hi"), sem("o_lo")
        bank_filled = sem("bank_filled")
        bank_free = sem("bank_free")
        part_done = sem("part_done")
        v3_done = sem("v3_done")
        s0_filled, max0_done, exp0_done = sem("s0_filled"), sem("max0_done"), sem("exp0_done")
        t0_filled, t0_hi, t0_lo = sem("t0_filled"), sem("t0_hi"), sem("t0_lo")
        t1_copied, t1_hi, t1_cast, t1_lo = sem("t1_copied"), sem("t1_hi"), sem("t1_cast"), sem("t1_lo")
        pv0_done, pv0_free = sem("pv0_done"), sem("pv0_free")
        a0_done = sem("a0_done")
        row_added = sem("row_added")
        var_done, sqrt_done, ln_done = sem("var_done"), sem("sqrt_done"), sem("ln_done")
        turn_filled, h_done, h_hi, h_lo = sem("turn_filled"), sem("h_done"), sem("h_hi"), sem("h_lo")
        col_done = sem("col_done")
        proj_hi, proj_lo = sem("proj_hi"), sem("proj_lo")
        s_filled, raw_done, nm_done, exp_done = sem("s_filled"), sem("raw_done"), sem("nm_done"), sem("exp_done")
        t_filled, t_hi, t_lo = sem("t_filled"), sem("t_hi"), sem("t_lo")
        px_copied, c_hi, c_lo = sem("px_copied"), sem("c_hi"), sem("c_lo")
        den_done = sem("den_done")
        g_hi, g_lo, mlp_out = sem("g_hi"), sem("g_lo"), sem("mlp_out")
        out_ready, batch_done = sem("out_ready"), sem("batch_done")
        apart_sp, apart_pe, apart_dve = sem("apart_sp"), sem("apart_pe"), sem("apart_dve")
        dve_step = sem("dve_step")

        block = ctx.enter_context(nc.Block())

        def f32(t):
            return t.bitcast(F32)

        def k_half(h, i):
            return [x[:, i * 512:(i + 1) * 512] for x in kT[h]]

        def q_all(h):
            return [x[:] for x in qT[h]]

        def v_tiles(i):
            return [x[:, 2 * i:2 * i + 2, :] for x in v]

        def turned_bank(c):
            return ps_s[c // 2][:, c % 2 * 512:(c % 2 + 1) * 512]

        @block.sync
        def _(sp):
            def apart():
                sp.sem_inc(apart_sp, 1)

            def load_row(k, i):
                sp.wait_ge(row_added, k + 1)
                sp.dma_start(row[:], d["rows"][i, :].partition_broadcast(P)).then_inc(row_in, 16)

            def load_qk(use, src):
                sp.wait_ge(qk_lo, 2 * use + 2)
                sp.dma_start(stg_qk[:], src).then_inc(qk_in, 16)

            def load_v(use, src):
                sp.wait_ge(v_lo, use + 1)
                sp.dma_start(stg_v[:], src).then_inc(v_in, 16)

            def load_o(use, src):
                sp.wait_ge(o_lo, use + 1)
                sp.dma_start(stg_o[:], src).then_inc(o_in, 16)

            def load_bv(k, f):
                sp.wait_ge(proj_lo, 2 + F_PAIR * k)
                sp.dma_start(bv_row[:], d["bv"][f, :].partition_broadcast(P)).then_inc(bv_in, 16)

            def load_ctx(b, cs):
                for c in cs:
                    sp.dma_start(st_ctx[:, c, :], d["ctxT"][b, :, c, :]).then_inc(ctx_in[c], 16)

            def load_kv(b):
                sp.dma_start(st_kv[:], d["w0kv"]).then_inc(kv_in, 16)
                load_ctx(b, range(CT // 2))

            def load_x(b):
                load_ctx(b, range(CT // 2, CT))
                sp.dma_start(st_x[:], d["xT"][b, :, :, :]).then_inc(x_in, 16)

            def load_w0q(b):
                load_qk(b * QK_B, d["w0q"])
                sp.dma_start(mask[:], d["mask"][b, :, :, :]).then_inc(mask_in, 16)

            def batch(b, last):
                sp.wait_ge(batch_done, b + 1)
                def stack(i):
                    scr = scr_k[i, :, :, :] if i < 2 else scr_q[i - 2, :, :, :]
                    for j in range(len(Q_ORDER)):
                        part = (K_ORDER if i < 2 else Q_ORDER)[j]
                        rows_j = slice(HD * j, HD * j + HD)
                        dst = (k_stack[rows_j, :, i * 512:(i + 1) * 512] if i < 2 else
                               q_stack[rows_j, (i - 2) * 8:(i - 1) * 8, :])
                        src = scr[:, part, :].rearrange("(a e) n -> e a n", e=HD)
                        sp.dma_start(dst, src).then_inc(stack_in if i < 3 else stack_rest, 16)

                for i in range(6):
                    sp.wait_ge(part_done, b * 6 + i + 1)
                    scr = scr_k[i, :, :, :] if i < 2 else scr_q[i - 2, :, :, :]
                    sp.dma_start(scr, parts[i % 2][:]).then_inc(scr_out, 16)
                    if i == 0:
                        continue
                    sp.wait_ge(scr_out, 16 * (b * 6 + i + 1))
                    apart()
                    if i == 1:
                        stack(0)
                    stack(i)
                    if i == 1:
                        load_qk(b * QK_B + 1, d["w0o"])
                    if i == 2:
                        sp.dma_start(x_res[:], d["x"][b, :, :, :]).then_inc(xres_in, 16)
                        load_row(b * TURNS, 0)
                        sp.dma_start(stg_o[:], d["rows0"].partition_broadcast(P)).then_inc(rows0_in, 16)

                def pair_loads(f, o=True):
                    load_v(b * V_B + f, d["wv"][f, :, :])
                    load_bv(b * V_B + f, f)
                    load_qk(b * QK_B + 3 + f, d["wqk"][f + 1, :, :, :])

                load_qk(b * QK_B + 2, d["wqk"][0, :, :, :])
                for y in range(LAYERS):
                    pair_loads(y * PAIRS)
                    load_row(b * TURNS + 1 + y, y + 1)
                    if y == 0:
                        sp.wait_ge(row_added, b * TURNS + 3)
                        apart()
                    with sp.Fori(0, PAIRS - 1) as pr:
                        f = y * PAIRS + pr
                        load_o(b * O_B + f, d["wo"][f, :, :, :])
                        pair_loads(f + 1)
                    f = y * PAIRS + PAIRS - 1
                    load_o(b * O_B + f, d["wo"][f, :, :, :])
                load_row(b * TURNS + 3, 3)
                load_o(b * O_B + V_B, d["wo"][V_B, :, :, :])
                for fp in range(1, FPAIRS):
                    load_o(b * O_B + V_B + fp, d["wo"][V_B + fp, :, :, :])
                    if fp % 2 == 1 and fp < FPAIRS - 1:
                        load_qk(b * QK_B + 3 + V_B + fp // 2, d["wqk"][V_B + 1 + fp // 2, :, :, :])
                    if fp == FPAIRS - 3 and not last:
                        sp.wait_ge(h_lo, CT * (b * TURNS + 4))
                        load_kv(b + 1)
                    if fp == FPAIRS - 2 and not last:
                        load_x(b + 1)
                if not last:
                    load_w0q(b + 1)
                for lt in range(LT):
                    sp.wait_ge(out_ready, b * LT + lt + 1)
                    sp.dma_start(d["out"][b, :, lt, :], x_res[:, lt, :]).then_inc(out_done, 16)
                sp.wait_ge(out_done, 16 * LT * (b + 1))
                apart()

            load_kv(0)
            for dst, name in ((cols, "cols"), (cols0, "cols0"), (colf, "colf"), (lnc, "lnc"), (bv0, "bv0")):
                src = d[name]
                sp.dma_start(dst[:], src.partition_broadcast(P) if name == "bv0" else src).then_inc(const_in, 16)
            load_x(0)
            load_w0q(0)
            with sp.Fori(0, B - 1) as b:
                batch(b, False)
            batch(B - 1, True)

        @block.gpsimd
        def _(pool):
            nc.gpsimd.memset(zero[:], 0.0).then_inc(zero_made, 1)
            pool.wait_ge(zero_made, 1)
            nc.gpsimd.memset(ident[:], 0.0).then_inc(const_made, 1)
            pool.wait_ge(const_made, 1)
            nc.gpsimd.affine_select(out=ident[:], in_=ident[:], compare_op=ALU.not_equal, fill=1.0, base=0,
                                    pattern=[[-1, P]], channel_multiplier=1).then_inc(const_made, 1)
            pool.sem_inc(proj_lo, 2)
            pool.sem_inc(qk_lo, 2)
            pool.sem_inc(v_lo, 1)
            pool.sem_inc(o_lo, 1)
            pool.sem_inc(row_added, 1)

            def lo(out, x, hi):
                return nc.gpsimd.tensor_tensor(out, x, f32(hi), ALU.subtract)

            def lo_qk(use, slot):
                pool.wait_ge(qk_hi, 2 * use + slot + 1)
                flat = [w[:, slot].rearrange("p c n -> p (c n)") for w in wa]
                lo(flat[1], stg_qk[:, slot, :], flat[0]).then_inc(qk_lo, 1)

            def lo_v(use):
                pool.wait_ge(v_hi, use + 1)
                flat = [w[:, 2].rearrange("p c n -> p (c n)") for w in wa]
                lo(flat[1], stg_v[:], flat[0]).then_inc(v_lo, 1)

            def lo_o(use, w=wo):
                pool.wait_ge(o_hi, use + 1)
                lo(w[1][:], stg_o[:], w[0][:]).then_inc(o_lo, 1)

            def lo_w0(use, w):
                pool.wait_ge(qk_hi, 2 * use + 2)
                flat = [t[:].rearrange("p (s c) n -> p s (c n)", s=2) for t in w]
                lo(flat[1], stg_qk[:], flat[0]).then_inc(qk_lo, 2)

            def add_row(k):
                pool.wait_ge(row_in, 16 * (k + 1))
                nc.gpsimd.tensor_tensor(x_res[:], x_res[:], row[:].unsqueeze(1).to_broadcast([P, LT, D]),
                                        ALU.add).then_inc(row_added, 1)

            def lo_turn(k):
                for i in range(2):
                    pool.wait_ge(h_hi, CT * k + i + 1)
                    c = TURN_ORDER[i]
                    lo(hT[1][:, c, :], h_fea[:, c, :], hT[0][:, c, :]).then_inc(h_lo, 1)

            with pool.Fori(0, B) as b:
                pool.wait_ge(in_hi, b * (CT + 2) + 1)
                lo(w0kv[1][:], st_kv[:], w0kv[0][:]).then_inc(kv_lo, 1)
                for c in range(CT - 1):
                    pool.wait_ge(in_hi, b * (CT + 2) + 1 + c + 1)
                    lo(ctxT[1][:, c, :], st_ctx[:, c, :], ctxT[0][:, c, :]).then_inc(ctx_lo, 1)
                lo_w0(b * QK_B, w0q)
                lo_w0(b * QK_B + 1, w0o)
                pool.wait_ge(xres_in, 16 * (b + 1))
                add_row(b * TURNS)
                with pool.Fori(0, KVH * STEPS0 // 2) as pr:
                    for i in range(2):
                        t = b * KVH * STEPS0 + 2 * pr + i
                        pool.wait_ge(t1_copied, t + 2)
                        nc.gpsimd.tensor_tensor(p16[i][0][:, 6:8, :], p32[i][:, 2:4, :],
                                                zero[:].unsqueeze(2).to_broadcast([P, 2, P]), ALU.add).then_inc(t1_cast, 1)
                        pool.wait_ge(t1_cast, t + 1)
                        pool.wait_ge(t1_hi, t + 1)
                        nc.gpsimd.tensor_tensor(p16[i][1][:, 4:8, :], p32[i][:], p16[i][0][:, 4:8, :],
                                                ALU.subtract).then_inc(t1_lo, 1)
                for y in range(LAYERS):
                    def lo_proj(k, dst):
                        pool.wait_ge(proj_hi, F0 + k + 1)
                        x = proj[k % 2][:]
                        if len(dst[1].shape) == 3:
                            x = x.rearrange("p (s n) -> p s n", s=2)
                        lo(dst[1], x, dst[0]).then_inc(proj_lo, 1)

                    def lo_c(j):
                        pool.wait_ge(c_hi, 4 * it + j + 1)
                        h, off = j // 2, (j % 2) * 256
                        lo(cT[1][:, h, off:off + 256], cf[j % 2][:], cT[0][:, h, off:off + 256]).then_inc(c_lo, 1)

                    f0 = y * PAIRS
                    it = b * V_B + f0
                    F0 = it * F_PAIR
                    if y == 0:
                        lo_qk(b * QK_B + 2, 0)
                        lo_qk(b * QK_B + 2, 1)
                        lo_v(it)
                        for i in range(2):
                            lo_proj(FS_K0[i], k_half(0, i))
                        for i in range(2):
                            lo_proj(FS_K1[i], k_half(1, i))
                        lo_proj(FS_V[0], v_tiles(0))
                    lo_proj(FS_V[1], v_tiles(1))
                    lo_turn(b * TURNS + 1 + y)
                    lo_proj(FS_V[2], v_tiles(2))
                    lo_proj(FS_Q0, q_all(0))
                    lo_proj(FS_Q1, q_all(1))
                    lo_proj(FS_V[3], v_tiles(3))
                    pool.wait_ge(ln_done, (b * 3 + y + 1) * LT)
                    add_row(b * TURNS + 1 + y)
                    lo_qk(b * QK_B + 3 + f0, 0)
                    lo_qk(b * QK_B + 3 + f0, 1)
                    with pool.Fori(0, PAIRS - 1) as pr:
                        it = b * V_B + f0 + pr
                        f = f0 + pr
                        F0 = (it + 1) * F_PAIR
                        lo_proj(F_Q0, q_all(0))
                        lo_c(0)
                        lo_o(b * O_B + f)
                        lo_proj(F_K0[0], k_half(0, 0))
                        lo_c(1)
                        lo_proj(F_K0[1], k_half(0, 1))
                        lo_v(b * V_B + f + 1)
                        lo_c(2)
                        lo_proj(F_Q1, q_all(1))
                        lo_proj(F_K1[0], k_half(1, 0))
                        lo_proj(F_K1[1], k_half(1, 1))
                        lo_c(3)
                        lo_proj(F_V[0], v_tiles(0))
                        lo_qk(b * QK_B + 4 + f, 0)
                        lo_proj(F_V[1], v_tiles(1))
                        lo_proj(F_V[2], v_tiles(2))
                        lo_proj(F_V[3], v_tiles(3))
                        lo_qk(b * QK_B + 4 + f, 1)
                    it = b * V_B + f0 + PAIRS - 1
                    F0 = (it + 1) * F_PAIR
                    more = y + 1 < LAYERS
                    lo_c(0)
                    if more:
                        lo_proj(FS_K0[0], k_half(0, 0))
                    lo_o(b * O_B + f0 + PAIRS - 1)
                    if more:
                        lo_proj(FS_K0[1], k_half(0, 1))
                        lo_v(b * V_B + f0 + PAIRS)
                    lo_c(1)
                    if more:
                        lo_proj(FS_K1[0], k_half(1, 0))
                    lo_c(2)
                    if more:
                        lo_proj(FS_K1[1], k_half(1, 1))
                    lo_c(3)
                    if more:
                        lo_proj(FS_V[0], v_tiles(0))
                lo_turn(b * TURNS + 3)
                pool.wait_ge(ln_done, (b * 3 + 3) * LT)
                add_row(b * TURNS + 3)
                lo_o(b * O_B + V_B, w2[0])
                lo_o(b * O_B + V_B + 1, w2[1])
                for fp in range(1, FPAIRS - 1):
                    if fp % 2 == 1:
                        lo_qk(b * QK_B + 3 + V_B + fp // 2, 0)
                    lo_o(b * O_B + V_B + fp + 1, w2[(fp + 1) % 2])
                    if fp % 2 == 1:
                        lo_qk(b * QK_B + 3 + V_B + fp // 2, 1)

        @block.scalar
        def _(act):
            def copy(out, in_):
                return nc.scalar.activation(out, in_, ACT.Copy)

            def split_w0(use, w):
                act.wait_ge(qk_in, 16 * (use + 1))
                copy(w[0][:].rearrange("p (s c) n -> p s (c n)", s=2), stg_qk[:]).then_inc(qk_hi, 2)

            def split_qk(use, slot):
                act.wait_ge(qk_in, 16 * (use + 1))
                copy(wa[0][:, slot].rearrange("p c n -> p (c n)"), stg_qk[:, slot, :]).then_inc(qk_hi, 1)

            def split_v(use):
                act.wait_ge(v_in, 16 * (use + 1))
                copy(wa[0][:, 2].rearrange("p c n -> p (c n)"), stg_v[:]).then_inc(v_hi, 1)

            def split_o(use, w=wo):
                act.wait_ge(o_in, 16 * (use + 1))
                copy(w[0][:], stg_o[:]).then_inc(o_hi, 1)

            def root(k):
                act.wait_ge(var_done, k + 1)
                nc.scalar.activation(lnv[:, 1, :], lnv[:, 0, :], ACT.Sqrt).then_inc(sqrt_done, 1)

            def turn_hi(k):
                for i, c in enumerate(TURN_ORDER):
                    act.wait_ge(h_done, CT * k + i + 1)
                    copy(hT[0][:, c, :], h_fea[:, c, :]).then_inc(h_hi, 1)

            act.sem_inc(t1_copied, 1)
            with act.Fori(0, B) as b:
                act.wait_ge(kv_in, 16 * (b + 1))
                copy(w0kv[0][:], st_kv[:]).then_inc(in_hi, 1)
                for c in range(CT):
                    act.wait_ge(ctx_in[c], 16 * (b + 1))
                    copy(ctxT[0][:, c, :], st_ctx[:, c, :]).then_inc(in_hi, 1)
                act.wait_ge(x_in, 16 * (b + 1))
                copy(hT[0][:], st_x[:]).then_inc(in_hi, 1)
                act.wait_ge(mlp_out, b * FPAIRS + 1)
                split_w0(b * QK_B, w0q)
                act.wait_ge(ctx_lo, (CT - 1) * (b + 1))
                act.wait_ge(x_lo, 2 * (b + 1))
                act.wait_ge(kv_lo, b + 1)
                act.wait_ge(cols_scaled, 1)

                def wide(i, n, col, scale):
                    act.wait_ge(bank_filled, nb + n + 1)
                    act.wait_ge(bank_free, nb + n + 2)
                    if i >= 2:
                        act.wait_ge(part_done, b * 6 + i - 1)
                        act.wait_ge(scr_out, 16 * (b * 6 + max(i - 1, 2)))
                    nc.scalar.activation(tmp0[i % 2][:], ps_m[n % 2][:], ACT.Identity, bias=col, scale=scale)
                    nc.scalar.activation(parts[i % 2][:, 0, :], ps_m[n % 2][:], ACT.Identity, bias=col,
                                         scale=scale).then_inc(bank_free, 1)
                    act.wait_ge(bank_free, nb + n + 3)
                    act.sem_inc(wide_done, 1)

                nb = b * U_B
                for i in range(2):
                    wide(i, i, cols0[:, 4:5], 1.0)
                wide(2, P_Q[0], cols0q[:, 0:1], SCALE0)
                split_w0(b * QK_B + 1, w0o)
                for i in range(1, 3):
                    wide(2 + i, P_Q[i], cols0q[:, i:i + 1], SCALE0)

                def exp0(t):
                    act.wait_ge(max0_done, t0 + t + 1)
                    nc.scalar.activation(p0[t % 2][:], sm[t % 2][:], ACT.Exp, bias=nm0[:, t % 2:t % 2 + 1],
                                         scale=-1.0).then_inc(exp0_done, 1)

                def step0(t, ahead):
                    act.wait_ge(pv0_done, t0 + t + 1)
                    act.wait_ge(t0_filled, 2 * (t0 + t) + 1)
                    nc.scalar.activation(p16[t % 2][0][:, 0:4, :], ps_t[t % 2][:].rearrange("p (s n) -> p s n", s=4),
                                         ACT.Copy, scale=P_TOP).then_inc(t0_hi, 1)
                    act.wait_ge(t0_filled, 2 * (t0 + t) + 2)
                    nc.scalar.activation(p32[t % 2][:], ps_t[1 - t % 2][:].rearrange("p (s n) -> p s n", s=4),
                                         ACT.Copy, scale=P_TOP).then_inc(t1_copied, 1)
                    if ahead:
                        exp0(t + 2)

                t0 = b * KVH * STEPS0
                exp0(0)
                exp0(1)
                wide(5, P_Q[3], cols0q[:, 3:4], SCALE0)
                with act.Fori(0, KVH - 1) as kv:
                    t0 = (b * KVH + kv) * STEPS0
                    for t in range(STEPS0):
                        step0(t, True)
                t0 = (b * KVH + KVH - 1) * STEPS0
                for t in range(STEPS0):
                    step0(t, t + 2 < STEPS0)
                for i, c in enumerate(TURN_ORDER):
                    act.wait_ge(turn_filled, CT * (b * TURNS) + i + 1)
                    copy(hT[0][:, c, :], turned_bank(c)).then_inc(h_hi, 1)

                for y in range(LAYERS):
                    def hi_proj(n, k, dst):
                        act.wait_ge(bank_free, n0 + n + 3)
                        x = proj[k % 2][:]
                        if len(dst[0].shape) == 3:
                            x = x.rearrange("p (s n) -> p s n", s=2)
                        copy(dst[0], x).then_inc(proj_hi, 1)

                    def exp(t):
                        h, lt, i = t // LT % 2, t % LT, t % STEPS
                        act.wait_ge(nm_done, T + t + 1)
                        nc.scalar.activation(pext[:, i:i + 1], lb[:, h, lt:lt + 1], ACT.Exp,
                                             bias=nm[:, i:i + 1], scale=SCALE1)
                        nc.scalar.activation(p[t % 2][:], ps_s[t % 2][:], ACT.Exp, bias=nm[:, i:i + 1],
                                             scale=SCALE1, accum_out=sums[:, i:i + 1]).then_inc(exp_done, 1)

                    def turned(t):
                        off = (t % 2) * P
                        for q in range(2):
                            act.wait_ge(t_filled, 2 * (T + t) + q + 1)
                            copy(pT[t // 2 % 2][0][:, 4 * q:4 * q + 4, off:off + P],
                                 ps_t[q][:].rearrange("p (s n) -> p s n", s=4)).then_inc(t_hi, 1)

                    def extra_weights(n, j):
                        act.wait_ge(bank_filled, n0 + n + 1)
                        copy(pextb[j % 2][:], ps_m[n % 2][:, 256:512]).then_inc(px_copied, 1)

                    def c_halves(n, j):
                        act.wait_ge(bank_free, n0 + n + 3)
                        h, off = j // 2, (j % 2) * 256
                        copy(cT[0][:, h, off:off + 256], cf[j % 2][:]).then_inc(c_hi, 1)

                    f0 = y * PAIRS
                    it = b * V_B + f0
                    T = it * STEPS
                    n0 = b * U_B + (U_PROJ0 if y == 0 else U_END[y - 1])
                    start, vs = (T_START, T_V) if y == 0 else (L_START, L_V)
                    if y == 0:
                        split_qk(b * QK_B + 2, 0)
                        split_qk(b * QK_B + 2, 1)
                        split_v(it)
                        root(b * TURNS)
                        for i in range(2):
                            hi_proj(T_K0[i], FS_K0[i], k_half(0, i))
                        for i in range(2):
                            hi_proj(T_K1[i], FS_K1[i], k_half(1, i))
                    root(b * TURNS + 1 + y)
                    for i in range(2):
                        if y == 0 or i > 0:
                            hi_proj(vs[i], FS_V[i], v_tiles(i))
                    turn_hi(b * 3 + y)
                    hi_proj(start + S_V2, FS_V[2], v_tiles(2))
                    hi_proj(start + S_Q0, FS_Q0, q_all(0))
                    hi_proj(start + S_Q1, FS_Q1, q_all(1))
                    split_qk(b * QK_B + 3 + f0, 0)
                    exp(0)
                    exp(1)
                    hi_proj(start + S_V3, FS_V[3], v_tiles(3))
                    turned(0)
                    exp(2)
                    turned(1)
                    exp(3)
                    split_qk(b * QK_B + 3 + f0, 1)
                    with act.Fori(0, PAIRS - 1) as pr:
                        it = b * V_B + f0 + pr
                        f = f0 + pr
                        T = it * STEPS
                        n0 = b * U_B + U_LOOP[y] + pr * U_PAIR
                        for t in range(2, STEPS + 2):
                            turned(t)
                            if t == 4:
                                hi_proj(K0[0], F_K0[0], k_half(0, 0))
                            if t == 5:
                                hi_proj(K0[1], F_K0[1], k_half(0, 1))
                            if t == 8:
                                hi_proj(K1[1], F_K1[1], k_half(1, 1))
                            if t == 9:
                                hi_proj(V[1], F_V[1], v_tiles(1))
                            if t == 7:
                                hi_proj(Q1, F_Q1, q_all(1))
                            if t == 6:
                                extra_weights(PV[2], 2)
                            exp(t + 2)
                            if t == 2:
                                hi_proj(Q0, F_Q0, q_all(0))
                            if t % 2 == 0:
                                if t != 6:
                                    extra_weights(PV[t // 2 - 1], t // 2 - 1)
                                c_halves(PV[t // 2 - 1], t // 2 - 1)
                            if t == 3:
                                split_o(b * O_B + f)
                            if t == 5:
                                split_v(b * V_B + f + 1)
                            if t == 7:
                                hi_proj(K1[0], F_K1[0], k_half(1, 0))
                            if t == 8:
                                hi_proj(V[0], F_V[0], v_tiles(0))
                                split_qk(b * QK_B + 4 + f, 0)
                            if t == 9:
                                hi_proj(V[2], F_V[2], v_tiles(2))
                                hi_proj(V[3], F_V[3], v_tiles(3))
                                split_qk(b * QK_B + 4 + f, 1)
                    it = b * V_B + f0 + PAIRS - 1
                    T = it * STEPS
                    n0 = b * U_B + U_END[y]
                    more = y + 1 < LAYERS
                    pvs = L_PV if more else E_PV
                    for t in range(2, STEPS):
                        turned(t)
                        if t + 2 < STEPS:
                            exp(t + 2)
                        if t % 2 == 0:
                            extra_weights(pvs[t // 2 - 1], t // 2 - 1)
                        if t % 2 == 0:
                            c_halves(pvs[t // 2 - 1], t // 2 - 1)
                        if t in (2, 3) and more:
                            hi_proj(L_K0[t - 2], FS_K0[t - 2], k_half(0, t - 2))
                        if t == 2:
                            split_o(b * O_B + f0 + PAIRS - 1)
                        if t == 3 and more:
                            split_v(b * V_B + f0 + PAIRS)
                        if t in (5, 7) and more:
                            hi_proj(L_K1[t // 7], FS_K1[t // 7], k_half(1, t // 7))
                    extra_weights(pvs[3], 3)
                    c_halves(pvs[3], 3)
                    if more:
                        hi_proj(L_V[0], FS_V[0], v_tiles(0))

                root(b * TURNS + 3)
                turn_hi(b * 3 + 2)
                split_o(b * O_B + V_B, w2[0])

                def gelu(fp):
                    act.wait_ge(g_lo, (b * FPAIRS + fp) * 2 + 2)
                    for i in range(2):
                        act.wait_ge(bank_filled, b * U_B + U_B - U_MLP + 2 * fp + i + 1)
                        nc.scalar.activation(g[i][:], ps_m[i][:], ACT.Gelu,
                                             bias=colf[:, fp * 2 + i:fp * 2 + i + 1]).then_inc(bank_free, 1)
                    for i in range(2):
                        act.wait_ge(bank_free, b * U_B + U_B - U_MLP + 2 * fp + i + 3)
                        copy(gT[fp % 2][i][0][:], g[i][:]).then_inc(g_hi, 1)

                gelu(0)
                split_o(b * O_B + V_B + 1, w2[1])
                for fp in range(1, FPAIRS):
                    more = fp % 2 == 1 and fp < FPAIRS - 1
                    if more:
                        split_qk(b * QK_B + 3 + V_B + fp // 2, 0)
                    gelu(fp)
                    if fp + 1 < FPAIRS:
                        act.wait_ge(mlp_out, b * FPAIRS + fp + 2)
                        split_o(b * O_B + V_B + fp + 1, w2[(fp + 1) % 2])
                    if more:
                        split_qk(b * QK_B + 3 + V_B + fp // 2, 1)

        @block.tensor
        def _(pe):
            def passes(out, lhs, rhs, n_tiles, start=True, stop=True):
                for c in range(n_tiles):
                    for i, (x, y) in enumerate(PASSES):
                        mm = nc.tensor.matmul(out, lhs(x, c), rhs(y, c), start=start and c == 0 and i == 0,
                                              stop=stop and c == n_tiles - 1 and i == 2)
                return mm

            def normed(out, w, k, h_left=False):
                def mm(i, c, x, first, last):
                    h = hT[x[1]][:, c, :] if h_left is False else hT[x[1]][:, c, h_left]
                    l, r = (w(x[0], c), h) if h_left is False else (h, w(x[0], c))
                    return nc.tensor.matmul(out, l, r, start=first, stop=last)

                for i, c in enumerate(TURN_ORDER):
                    pe.wait_ge(h_hi, CT * k + i + 1)
                    mm(i, c, (0, 0), i == 0, False)
                    mm(i, c, (1, 0), False, False)
                pe.wait_ge(h_lo, CT * (k + 1))
                for i, c in enumerate(TURN_ORDER):
                    last = mm(i, c, (0, 1), False, i == CT - 1)
                return last

            def free(n):
                pe.wait_ge(bank_free, n + 1)

            def turn(k, src, ready=None):
                for lt in range(LT):
                    if ready is not None:
                        pe.wait_ge(ln_done, ready + lt + 1)
                    for c in TURN_ORDER:
                        mm = nc.tensor.transpose(turned_bank(c)[:, lt * P:(lt + 1) * P],
                                                 src[:, lt, c * P:(c + 1) * P], ident[:])
                        if lt == LT - 1:
                            mm.then_inc(turn_filled, 1)

            def apart():
                pe.sem_inc(apart_pe, 1)

            pe.wait_ge(const_made, 2)
            pe.sem_inc(pv0_done, 2)
            pe.sem_inc(mlp_out, 2)
            with pe.Fori(0, B) as b:
                nb = b * U_B
                pe.wait_ge(kv_lo, b + 1)
                for i in range(2):
                    free(nb + i)

                def add_k(i, c, x, y, start=False, stop=False):
                    return nc.tensor.matmul(ps_m[i][:], w0kv[x][:, c, 0:P], ctxT[y][:, c, i * 512:(i + 1) * 512],
                                            start=start, stop=stop)

                for c in range(CT):
                    pe.wait_ge(in_hi, b * (CT + 2) + 1 + c + 1)
                    for i in range(2):
                        add_k(i, c, 0, 0, start=c == 0)
                        add_k(i, c, 1, 0)
                for c in range(CT):
                    if c < CT - 1:
                        pe.wait_ge(ctx_lo, b * (CT - 1) + c + 1)
                    else:
                        pe.wait_ge(x_lo, 2 * b + 1)
                    for i in range(2):
                        mm = add_k(i, c, 0, 1, stop=c == CT - 1)
                        if c == CT - 1:
                            mm.then_inc(bank_filled, 1)
                def project_q0(i):
                    free(nb + P_Q[i])
                    passes(ps_m[P_Q[i] % 2][:], lambda x, c: w0q[x][:, c, i * P:(i + 1) * P],
                           lambda y, c: hT[y][:, c, :], CT).then_inc(bank_filled, 1)

                def project_v0(i):
                    free(nb + P_V[i])
                    for s in range(2):
                        st = 2 * i + s
                        mm = passes(ps_m[P_V[i] % 2][:, s * 256:(s + 1) * 256],
                                    lambda x, c: ctxT[x][:, c, st * P:(st + 1) * P],
                                    lambda y, c: w0kv[y][:, c, :], CT)
                    mm.then_inc(bank_filled, 1)

                for i in range(2):
                    project_v0(i)
                pe.wait_ge(x_lo, 2 * b + 2)
                pe.wait_ge(qk_lo, 2 * (b * QK_B) + 4)
                project_q0(0)
                for i in range(2, 4):
                    project_v0(i)
                for i in range(1, 4):
                    project_q0(i)

                pe.wait_ge(stack_in, 16 * 18 * (b + 1))
                pe.wait_ge(v3_done, b * 5 + 5)
                apart()

                def scores0(t):
                    lt, gr = divmod(t % STEPS0, GROUPS)
                    head = kv + t // STEPS0
                    if t >= 2:
                        pe.wait_ge(max0_done, t0 + t - 1)
                    for n in range(2):
                        mm = nc.tensor.matmul(ps_s[t % 2][:, n * 512:(n + 1) * 512],
                                              q_stack[:, bass.ds(head * GROUPS + gr, 1), lt * P:(lt + 1) * P],
                                              k_stack[:, bass.ds(head, 1), n * 512:(n + 1) * 512],
                                              start=True, stop=True)
                    mm.then_inc(s0_filled, 1)

                def turned0(t):
                    pe.wait_ge(exp0_done, t0 + t + 1)
                    for q in range(2):
                        pe.wait_ge((t1_copied, t0_lo)[q], t0 + t + 1)
                        for s in range(4):
                            st = 4 * q + s
                            mm = nc.tensor.transpose(ps_t[(t + q) % 2][:, s * P:(s + 1) * P],
                                                     p0[t % 2][:, st * P:(st + 1) * P], ident[:])
                        mm.then_inc(t0_filled, 1)

                def values0(t):
                    lt, gr = divmod(t, GROUPS)
                    if gr == 0:
                        pe.wait_ge(pv0_free, turns0 * LT + lt + 1)
                    pe.wait_ge(t0_lo, t0 + t + 2)
                    for st in range(ST):
                        if st == ST // 2:
                            pe.wait_ge(t1_lo, t0 + t + 1)
                        for x in range(2):
                            mm = nc.tensor.matmul(ps_m[lt % 2][:, gr * VW:gr * VW + 49], p16[t % 2][x][:, st, :],
                                                  v3[:, st, bass.ds(kv, 1), 0:49],
                                                  start=st == 0 and x == 0, stop=st == ST - 1 and x == 1)
                    mm.then_inc(pv0_done, 1)

                kv, turns0 = 0, b * KVH
                t0 = turns0 * STEPS0
                for t in range(3):
                    scores0(t)
                turned0(0)
                scores0(3)
                with pe.Fori(0, KVH - 1) as kv:
                    turns0 = b * KVH + kv
                    t0 = turns0 * STEPS0
                    for t in range(1, STEPS0 + 1):
                        turned0(t)
                        if t + 3 == STEPS0:
                            pe.wait_ge(stack_rest, 16 * 18 * (b + 1))
                        scores0(t + 3)
                        values0(t - 1)
                kv, turns0 = KVH - 1, b * KVH + KVH - 1
                t0 = turns0 * STEPS0
                for t in range(1, STEPS0):
                    turned0(t)
                    if t + 3 < STEPS0:
                        scores0(t + 3)
                    values0(t - 1)
                values0(STEPS0 - 1)

                n0 = nb + U_PROJ0
                pe.wait_ge(a0_done, KVH * LT * (b + 1))
                turn(b * TURNS, a0)
                pe.wait_ge(qk_lo, 2 * (b * QK_B) + 6)
                free(n0 + T_OUT)
                normed(ps_m[T_OUT % 2][:], lambda x, c: w0o[x][:, c, :], b * TURNS, slice(0, P)).then_inc(bank_filled, 1)
                for lt in range(1, LT):
                    free(n0 + T_OUT + lt)
                    passes(ps_m[(T_OUT + lt) % 2][:], lambda x, c: hT[x][:, c, lt * P:(lt + 1) * P],
                           lambda y, c: w0o[y][:, c, :], CT).then_inc(bank_filled, 1)

                for y in range(LAYERS):
                    def project(n, slot, h, src, tokens):
                        free(n0 + n)
                        passes(ps_m[n % 2][:], lambda x, c: wa[x][:, slot, c, h * P:(h + 1) * P],
                               lambda q, c: src[q][:, c, tokens], CT).then_inc(bank_filled, 1)

                    def project_k(n, h, i):
                        project(n, 1, h, ctxT, slice(i * 512, (i + 1) * 512))

                    def project_q(n, h):
                        project(n, 0, h, hT, slice(0, L))

                    def project_v(n, i):
                        free(n0 + n)
                        for s in range(2):
                            st = 2 * i + s
                            mm = passes(ps_m[n % 2][:, s * 256:(s + 1) * 256],
                                        lambda x, c: ctxT[x][:, c, st * P:(st + 1) * P],
                                        lambda q, c: wa[q][:, 2, c, :], CT)
                        mm.then_inc(bank_filled, 1)

                    def projected(k):
                        pe.wait_ge(proj_lo, F0 + k + 3)

                    def extra_logits(n, k, h):
                        free(n0 + n)
                        projected(k)
                        for lt in range(LT):
                            for x in range(2):
                                mm = nc.tensor.matmul(ps_m[n % 2][:, 2 * lt:2 * lt + 2],
                                                      qT[h][x][:, lt * P:(lt + 1) * P], bkx[:, h, :],
                                                      start=x == 0, stop=x == 1)
                        mm.then_inc(bank_filled, 1)

                    def scores(t):
                        h, lt = t // LT % 2, t % LT
                        for n in range(2):
                            mm = passes(ps_s[t % 2][:, n * 512:(n + 1) * 512],
                                        lambda x, c: qT[h][x][:, lt * P:(lt + 1) * P],
                                        lambda q, c: kT[h][q][:, n * 512:(n + 1) * 512], 1)
                        mm.then_inc(s_filled, 1)

                    def turned(t):
                        pe.wait_ge(exp_done, T + t + 1)
                        for q in range(2):
                            pe.wait_ge(t_lo, 2 * (T + t) + q + 1)
                            for s in range(4):
                                st = 4 * q + s
                                mm = nc.tensor.transpose(ps_t[q][:, s * P:(s + 1) * P],
                                                         p[t % 2][:, st * P:(st + 1) * P], ident[:])
                            mm.then_inc(t_filled, 1)

                    def values(n, j):
                        free(n0 + n)
                        for s in range(2):
                            t = 2 * j + s
                            nc.tensor.transpose(ps_m[n % 2][:, 256 + s * P:256 + (s + 1) * P],
                                                pext[:, t:t + 1].to_broadcast([P, P]), ident[:])
                        h = j // 2
                        pe.wait_ge(t_lo, 2 * (T + 2 * j + 2) + 2)
                        passes(ps_m[n % 2][:, 0:256], lambda x, st: v[x][:, st, h * P:(h + 1) * P],
                               lambda q, st: pT[j % 2][q][:, st, :], ST).then_inc(bank_filled, 1)

                    def output(ns, h, lts):
                        pe.wait_ge(c_lo, 4 * it + 2 * h + 2)
                        for n, lt in zip(ns, lts):
                            free(n0 + n)
                            passes(ps_m[n % 2][:], lambda x, c: cT[x][:, h, lt * P:(lt + 1) * P],
                                   lambda q, c: wo[q][:, h, :], 1).then_inc(bank_filled, 1)

                    f0 = y * PAIRS
                    it = b * V_B + f0
                    F0, T = it * F_PAIR, it * STEPS
                    if y == 0:
                        start, vs = T_START, T_V
                        pe.wait_ge(qk_lo, 2 * (b * QK_B + 2) + 4)
                        for i in range(2):
                            project_k(T_K0[i], 0, i)
                        for i in range(2):
                            project_k(T_K1[i], 1, i)
                    else:
                        n0, start, vs = nb + U_END[y - 1], L_START, L_V
                    pe.wait_ge(v_lo, it + 2)
                    for i in range(y, 2):
                        project_v(vs[i], i)
                    turn(b * TURNS + 1 + y, h_tok, (b * 3 + y) * LT)
                    project_v(start + S_V2, 2)
                    free(n0 + start + S_Q0)
                    normed(ps_m[(start + S_Q0) % 2][:], lambda x, c: wa[x][:, 0, c, 0:P], b * TURNS + 1 + y)\
                        .then_inc(bank_filled, 1)
                    project_q(start + S_Q1, 1)
                    pe.wait_ge(col_done, 2 * (it + 1))
                    extra_logits(start + S_EX0, FS_Q0, 0)
                    scores(0)
                    extra_logits(start + S_EX1, FS_Q1, 1)
                    scores(1)
                    project_v(start + S_V3, 3)
                    turned(0)
                    scores(2)
                    turned(1)
                    scores(3)
                    with pe.Fori(0, PAIRS - 1) as pr:
                        it = b * V_B + f0 + pr
                        f = f0 + pr
                        F0, T = (it + 1) * F_PAIR, it * STEPS
                        n0 = nb + U_LOOP[y] + pr * U_PAIR
                        turned(2)
                        projected(FS_Q1 - F_PAIR)
                        scores(4)
                        pe.wait_ge(qk_lo, 2 * (b * QK_B + 3 + f) + 3)
                        project_q(Q0, 0)
                        projected(-1)
                        values(PV[0], 0)
                        turned(3)
                        scores(5)
                        pe.wait_ge(qk_lo, 2 * (b * QK_B + 3 + f) + 4)
                        project_k(K0[0], 0, 0)
                        turned(4)
                        scores(6)
                        values(PV[1], 1)
                        project_k(K0[1], 0, 1)
                        turned(5)
                        scores(7)
                        pe.wait_ge(col_done, 2 * (it + 2))
                        extra_logits(EX0, F_Q0, 0)
                        pe.wait_ge(o_lo, b * O_B + f + 2)
                        output(OUT0[0:1], 0, [0])
                        turned(6)
                        output(OUT0[1:2], 0, [1])
                        projected(F_K0[1])
                        scores(8)
                        values(PV[2], 2)
                        output(OUT0[2:3], 0, [2])
                        turned(7)
                        project_q(Q1, 1)
                        output(OUT0[3:4], 0, [3])
                        scores(9)
                        project_k(K1[0], 1, 0)
                        project_k(K1[1], 1, 1)
                        extra_logits(EX1, F_Q1, 1)
                        turned(8)
                        scores(10)
                        values(PV[3], 3)
                        pe.wait_ge(v_lo, b * V_B + f + 3)
                        project_v(V[0], 0)
                        project_v(V[1], 1)
                        turned(9)
                        output(OUT1[0:1], 1, [0])
                        project_v(V[2], 2)
                        output(OUT1[1:2], 1, [1])
                        scores(11)
                        output(OUT1[2:3], 1, [2])
                        project_v(V[3], 3)
                        output(OUT1[3:4], 1, [3])
                    it = b * V_B + f0 + PAIRS - 1
                    F0, T = (it + 1) * F_PAIR, it * STEPS
                    n0 = nb + U_END[y]
                    more = y + 1 < LAYERS
                    pvs, out0, out1 = (L_PV, L_OUT0, L_OUT1) if more else (E_PV, E_OUT0, E_OUT1)
                    turned(2)
                    projected(FS_Q1 - F_PAIR)
                    scores(4)
                    projected(-1)
                    values(pvs[0], 0)
                    if more:
                        pe.wait_ge(qk_lo, 2 * (b * QK_B + 2 + f0 + PAIRS) + 4)
                        project_k(L_K0[0], 0, 0)
                    turned(3)
                    scores(5)
                    if more:
                        project_k(L_K0[1], 0, 1)
                    turned(4)
                    scores(6)
                    values(pvs[1], 1)
                    turned(5)
                    scores(7)
                    if more:
                        project_k(L_K1[0], 1, 0)
                    pe.wait_ge(o_lo, b * O_B + f0 + PAIRS + 1)
                    output(out0[0:1], 0, [0])
                    turned(6)
                    output(out0[1:2], 0, [1])
                    values(pvs[2], 2)
                    if more:
                        turned(7)
                    output(out0[2:3], 0, [2])
                    if more:
                        project_k(L_K1[1], 1, 1)
                    output(out0[3:4], 0, [3])
                    if not more:
                        turned(7)
                    values(pvs[3], 3)
                    if more:
                        pe.wait_ge(v_lo, b * V_B + f0 + PAIRS + 2)
                        project_v(L_V[0], 0)
                    output(out1, 1, range(LT))

                n0 = nb + U_B - U_MLP
                turn(b * TURNS + 3, h_tok, (b * 3 + 2) * LT)

                def hidden(fp):
                    slot = fp % 2
                    pe.wait_ge(qk_lo, 2 * (b * QK_B + 2 + V_B + fp // 2) + slot + 3)
                    for i in range(2):
                        free(n0 + 2 * fp + i)
                        w = lambda x, c: wa[x][:, slot, c, i * P:(i + 1) * P]
                        mm = (normed(ps_m[i][:], w, b * TURNS + 3) if fp == 0 and i == 0 else
                              passes(ps_m[i][:], w, lambda q, c: hT[q][:, c, :], CT))
                        mm.then_inc(bank_filled, 1)

                def product(fp):
                    pe.wait_ge(o_lo, b * O_B + V_B + fp + 2)
                    for i in range(2):
                        pe.wait_ge(g_lo, (b * FPAIRS + fp) * 2 + i + 3)
                        for lt in range(LT):
                            mm = passes(ps_s[lt // 2][:, (lt % 2) * 512:(lt % 2 + 1) * 512],
                                        lambda x, c: gT[fp % 2][i][x][:, lt * P:(lt + 1) * P],
                                        lambda q, c: w2[fp % 2][q][:, i, :], 1,
                                        start=fp == 0 and i == 0, stop=fp == FPAIRS - 1 and i == 1)
                    mm.then_inc(mlp_out, 1)

                hidden(0)
                for fp in range(FPAIRS):
                    if fp + 1 < FPAIRS:
                        hidden(fp + 1)
                    product(fp)

        @block.vector
        def _(dve):
            step = [0, 0]

            def link(ins):
                step[1] += 1
                ins.then_inc(dve_step, 1)
                dve.wait_ge(dve_step, step[0] + step[1])

            def apart():
                dve.sem_inc(apart_dve, 1)

            sub = ALU.subtract
            dve.sem_inc(bank_free, 2)
            dve.sem_inc(pv0_free, 2)
            dve.sem_inc(t0_lo, 1)
            dve.sem_inc(t_lo, 2)
            dve.sem_inc(g_lo, 2)
            dve.sem_inc(batch_done, 1)
            dve.wait_ge(const_in, 16 * 5)
            nc.vector.tensor_scalar(cols0q[:], cols0[:, 0:4], SCALE0, None, ALU.mult).then_inc(cols_scaled, 1)

            def summed(add, n):
                for lt in range(LT + 1):
                    if lt < LT:
                        add(lt)
                    if lt > 0:
                        dve.wait_ge(bank_free, n + lt + 2)
                        apart()
                        mm = nc.vector.bn_stats(stats[:, lt - 1, :], x_res[:, lt - 1, :])
                link(mm)
                apart()

            def norm(k, eps, between):
                for lt in range(LT):
                    mm = nc.vector.bn_aggr(mean_var[:, lt, :], stats[:, lt, :])
                link(mm)
                nc.vector.tensor_scalar(lnv[:, 0, :], mean_var[:, :, 1], eps, 0.25, ALU.add, ALU.mult).then_inc(var_done, 1)
                between()
                dve.wait_ge(sqrt_done, k + 1)
                link(nc.vector.reciprocal(lnv[:, 2, :], lnv[:, 1, :]))
                link(nc.vector.tensor_tensor(lnv[:, 2, :], lnv[:, 2, :], lnv[:, 0, :], ALU.mult))
                link(nc.vector.tensor_tensor(lnv[:, 3, :], lnv[:, 2, :], lnv[:, 1, :], ALU.add))
                link(nc.vector.reciprocal(lnv[:, 4, :], lnv[:, 3, :]))

            def normal(out, lt):
                return nc.vector.tensor_scalar(out[:, lt, :], x_res[:, lt, :], mean_var[:, lt, 0:1],
                                               lnv[:, 4, lt:lt + 1], sub, ALU.mult)

            def tokens_normal():
                for lt in range(LT):
                    normal(h_tok, lt).then_inc(ln_done, 1)

            def features(k, col):
                def column(i, c):
                    if isinstance(col, int):
                        return lnc[:, col + i * CT + c:col + i * CT + c + 1]
                    return lnc[:, bass.ds(col + i * CT + c, 1)]

                for i, c in enumerate(TURN_ORDER):
                    dve.wait_ge(turn_filled, CT * k + i + 1)
                    nc.vector.tensor_scalar(h_fea[:, c, :], turned_bank(c), column(0, c), column(1, c),
                                            ALU.mult, ALU.add).then_inc(h_done, 1)
                for i in range(2, CT):
                    c = TURN_ORDER[i]
                    dve.wait_ge(h_hi, CT * k + i + 1)
                    nc.vector.tensor_tensor(hT[1][:, c, :], h_fea[:, c, :], f32(hT[0][:, c, :]), sub).then_inc(h_lo, 1)

            with dve.Fori(0, B) as b:
                nb = b * U_B
                step[:] = b * DVE_B, 0
                dve.wait_ge(in_hi, b * (CT + 2) + CT + 1)
                nc.vector.tensor_tensor(ctxT[1][:, CT - 1, :], st_ctx[:, CT - 1, :], f32(ctxT[0][:, CT - 1, :]), sub)\
                    .then_inc(x_lo, 1)
                dve.wait_ge(in_hi, (b + 1) * (CT + 2))
                nc.vector.tensor_tensor(hT[1][:], st_x[:], f32(hT[0][:]), sub).then_inc(x_lo, 1)

                def three_parts(i):
                    dve.wait_ge(wide_done, b * 6 + i + 1)
                    apart()
                    t, u, part = tmp0[i % 2][:], tmp_lo[:], parts[i % 2]
                    link(nc.vector.tensor_tensor(u, t, part[:, 0, :], sub))
                    link(nc.vector.tensor_copy(part[:, 1, :], u))
                    nc.vector.tensor_tensor(part[:, 2, :], u, part[:, 1, :], sub).then_inc(part_done, 1)
                    dve.wait_ge(part_done, b * 6 + i + 1)

                for i in range(2):
                    three_parts(i)
                nc.vector.memset(v3[:, :, :, 48:49], 1.0).then_inc(v3_done, 1)
                for i in range(4):
                    if i == 2:
                        three_parts(2)
                    dve.wait_ge(bank_filled, nb + P_V[i] + 1)
                    bank = ps_m[P_V[i] % 2][:].rearrange("p (s n) -> p s n", s=2)
                    link(nc.vector.tensor_tensor(tmp_lo[:, 0:256].rearrange("p (s n) -> p s n", s=2), bank[:, :, P:256],
                                                 bv0[:].unsqueeze(1).to_broadcast([P, 2, P]), ALU.add))
                    dve.sem_inc(bank_free, 1)
                    t, u = [tmp_lo[:, x * 256:(x + 1) * 256].rearrange("p (s a e) -> p s a e", s=2, e=HD)
                            for x in range(2)]
                    dst = [v3[:, 2 * i:2 * i + 2, :, x * HD:(x + 1) * HD] for x in range(3)]
                    link(nc.vector.tensor_copy(dst[0], t))
                    link(nc.vector.tensor_tensor(u, t, dst[0], sub))
                    link(nc.vector.tensor_copy(dst[1], u))
                    nc.vector.tensor_tensor(dst[2], u, dst[1], sub).then_inc(v3_done, 1)
                    dve.wait_ge(v3_done, b * 5 + i + 2)
                for i in range(3, 5):
                    three_parts(i)

                dve.wait_ge(mask_in, 16 * (b + 1))
                apart()

                def maxima0(t):
                    lt, i = t % STEPS0 // GROUPS, t % 2
                    if t >= 2:
                        dve.wait_ge(exp0_done, t0 + t - 1)
                    dve.wait_ge(s0_filled, t0 + t + 1)
                    apart()
                    nc.vector.tensor_tensor_reduce(sm[i][:], ps_s[i][:], mask[:, lt, :], -1.0, 3.0e38,
                                                   ALU.add, ALU.min, nm0[:, i:i + 1]).then_inc(max0_done, 1)

                def lo0(t):
                    dve.wait_ge(t0_hi, t0 + t + 1)
                    part = p16[t % 2]
                    nc.vector.scalar_tensor_tensor(out=part[1][:, 0:4, :],
                                                   in0=ps_t[t % 2][:].rearrange("p (s n) -> p s n", s=4), scalar=P_TOP,
                                                   in1=part[0][:, 0:4, :], op0=ALU.mult, op1=sub).then_inc(t0_lo, 1)
                    dve.wait_ge(t1_copied, t0 + t + 2)
                    nc.vector.tensor_copy(part[0][:, 4:6, :], p32[t % 2][:, 0:2, :]).then_inc(t1_hi, 1)

                def sums0(t):
                    lt = t // GROUPS - 1
                    dve.wait_ge(pv0_done, t0 + (lt + 1) * GROUPS + 2)
                    out = ps_m[lt % 2][:, 0:GROUPS * VW].rearrange("p (g w) -> p g w", w=VW)
                    nc.vector.reciprocal(rden0[:], out[:, :, 48])
                    nc.vector.tensor_reduce(red0[:], out[:, :, 0:48].rearrange("p g (x e) -> p g e x", x=3),
                                            AX.X, ALU.add).then_inc(pv0_free, 1)

                def normalised(t):
                    lt = t // GROUPS - 1
                    dve.wait_ge(pv0_free, turns0 * LT + lt + 3)
                    dst = a0[:, lt, bass.ds(kv * GROUPS * HD, GROUPS * HD)].rearrange("p (g e) -> p g e", g=GROUPS)
                    nc.vector.tensor_tensor(dst, red0[:], rden0[:].unsqueeze(2).to_broadcast([P, GROUPS, HD]),
                                            ALU.mult).then_inc(a0_done, 1)

                def step0(t, ahead=True):
                    if ahead:
                        maxima0(t + 2)
                    if t >= GROUPS and t % GROUPS == 2:
                        normalised(t)
                    lo0(t)
                    if t % GROUPS == 1 and t >= GROUPS:
                        sums0(t)

                turns0 = b * KVH
                t0 = turns0 * STEPS0
                for t in range(2):
                    maxima0(t)
                three_parts(5)
                for t in range(3):
                    step0(t)
                dve.wait_ge(scr_out, 16 * 6 * (b + 1))
                apart()
                with dve.Fori(0, KVH - 1) as kv:
                    turns0 = b * KVH + kv
                    t0 = turns0 * STEPS0
                    for t in range(3, STEPS0 + 3):
                        step0(t)
                kv, turns0 = KVH - 1, b * KVH + KVH - 1
                t0 = turns0 * STEPS0
                for t in range(3, STEPS0):
                    step0(t, t + 2 < STEPS0)
                sums0(LT * GROUPS)
                normalised(LT * GROUPS)

                n0 = nb + U_PROJ0
                for i, c in enumerate(TURN_ORDER):
                    dve.wait_ge(h_hi, CT * (b * TURNS) + i + 1)
                    nc.vector.tensor_tensor(hT[1][:, c, :], turned_bank(c), f32(hT[0][:, c, :]), sub).then_inc(h_lo, 1)
                dve.wait_ge(row_added, b * TURNS + 2)

                def add_out(lt):
                    dve.wait_ge(bank_filled, n0 + T_OUT + lt + 1)
                    nc.vector.tensor_tensor(x_res[:, lt, :], ps_m[(T_OUT + lt) % 2][:], x_res[:, lt, :], ALU.add)\
                        .then_inc(bank_free, 1)

                summed(add_out, n0 + T_OUT)

                for y in range(LAYERS):
                    def column(kind, h):
                        return cols[:, bass.ds(at_cols + kind * HEADS + h, 1)]

                    def add_column(n, k, kind, h):
                        dve.wait_ge(bank_filled, n0 + n + 1)
                        dve.wait_ge(proj_lo, F0 + k + 1)
                        nc.vector.tensor_scalar(proj[k % 2][:], ps_m[n % 2][:], column(kind, h), None, ALU.add)\
                            .then_inc(bank_free, 1)

                    def add_bv(n, k):
                        dve.wait_ge(bank_filled, n0 + n + 1)
                        dve.wait_ge(proj_lo, F0 + k + 1)
                        nc.vector.tensor_tensor(proj[k % 2][:].rearrange("p (s n) -> p s n", s=2),
                                                ps_m[n % 2][:].rearrange("p (s n) -> p s n", s=2),
                                                bv_row[:].unsqueeze(1).to_broadcast([P, 2, 256]), ALU.add)\
                            .then_inc(bank_free, 1)

                    def extra_columns(pair):
                        bias_k = cols[:, bass.ds(at_cols + 2 * HEADS, 2)]
                        nc.vector.tensor_copy(bkx[:, :, 0], bias_k).then_inc(col_done, 1)
                        dve.wait_ge(col_done, 2 * pair + 1)
                        nc.vector.tensor_tensor(bkx[:, :, 1], bias_k, f32(bkx[:, :, 0]), sub).then_inc(col_done, 1)

                    def extra_logits(n, h):
                        dve.wait_ge(bank_filled, n0 + n + 1)
                        src = ps_m[n % 2][:, 0:2 * LT].rearrange("p (l x) -> p l x", x=2)
                        nc.vector.tensor_reduce(lb[:, h, :], src, AX.X, ALU.add)
                        nc.vector.tensor_reduce(nlb[:, h, :], src, AX.X, ALU.add, negate=True).then_inc(bank_free, 1)

                    def maxima(t, extra=None):
                        h, lt, i = t // LT % 2, t % LT, t % STEPS
                        dve.wait_ge(s_filled, T + t + 1)
                        nc.vector.tensor_reduce(nmx[:, i:i + 1], ps_s[t % 2][:], AX.X, ALU.max, negate=True)\
                            .then_inc(raw_done, 1)
                        dve.wait_ge(raw_done, T + t + 1)
                        if extra is not None:
                            dve.wait_ge(bank_free, n0 + extra + 3)
                        nc.vector.tensor_scalar(nm[:, i:i + 1], nmx[:, i:i + 1], nlb[:, h, lt:lt + 1], SCALE1,
                                                ALU.min, ALU.mult).then_inc(nm_done, 1)

                    def turned(t):
                        off = (t % 2) * P
                        for q in range(2):
                            dve.wait_ge(t_hi, 2 * (T + t) + q + 1)
                            part = [x[:, 4 * q:4 * q + 4, off:off + P] for x in pT[t // 2 % 2]]
                            nc.vector.tensor_tensor(part[1], ps_t[q][:].rearrange("p (s n) -> p s n", s=4),
                                                    f32(part[0]), sub).then_inc(t_lo, 1)

                    def extra_value(n, j):
                        h = j // 2
                        dve.wait_ge(px_copied, 4 * it + j + 1)
                        dve.wait_ge(bank_filled, n0 + n + 1)
                        if j >= 2:
                            dve.wait_ge(c_lo, 4 * it + j - 1)
                        nc.vector.scalar_tensor_tensor(out=cf[j % 2][:], in0=pextb[j % 2][:],
                                                       scalar=column(3, h), in1=ps_m[n % 2][:, 0:256],
                                                       op0=ALU.mult, op1=ALU.add).then_inc(bank_free, 1)

                    def denominators(h):
                        hs = slice(h * LT, (h + 1) * LT)
                        dve.wait_ge(exp_done, T + (h + 1) * LT)
                        nc.vector.tensor_tensor(z[:, hs], sums[:, hs], pext[:, hs], ALU.add).then_inc(den_done, 1)
                        dve.wait_ge(den_done, 4 * it + 2 * h + 1)
                        nc.vector.reciprocal(r[:, hs], z[:, hs]).then_inc(den_done, 1)

                    def output(ns, h, lts):
                        dve.wait_ge(den_done, 4 * it + 2 * h + 2)
                        for n, lt in zip(ns, lts):
                            dve.wait_ge(bank_filled, n0 + n + 1)
                            t = h * LT + lt
                            nc.vector.scalar_tensor_tensor(
                                out=x_res[:, lt, :], in0=ps_m[n % 2][:], scalar=r[:, t:t + 1],
                                in1=x_res[:, lt, :], op0=ALU.mult, op1=ALU.add).then_inc(bank_free, 1)

                    f0 = y * PAIRS
                    it = b * V_B + f0
                    F0, T = it * F_PAIR, it * STEPS
                    at_cols = y * 4 * HEADS
                    if y == 0:
                        start, vs = T_START, T_V

                        def k0():
                            for i in range(2):
                                add_column(T_K0[i], FS_K0[i], 1, 0)

                        norm(b * TURNS, EPS0, k0)
                        dve.wait_ge(rows0_in, 16 * (b + 1))
                        apart()
                        for i, (col, op) in enumerate(((mean_var[:, :, 0], sub), (lnv[:, 4, :], ALU.mult))):
                            for lt in range(LT):
                                mm = nc.vector.scalar_tensor_tensor(
                                    out=x_res[:, lt, :], in0=x_res[:, lt, :], scalar=col[:, lt:lt + 1],
                                    in1=stg_o[:, i, :], op0=op, op1=(ALU.mult, ALU.add)[i])
                            link(mm)
                            if i == 0:
                                for j in range(2):
                                    add_column(T_K1[j], FS_K1[j], 1, 1)
                        apart()
                        for lt in range(LT):
                            mm = nc.vector.bn_stats(stats[:, lt, :], x_res[:, lt, :])
                        link(mm)
                        apart()
                    else:
                        n0, start, vs = nb + U_END[y - 1], L_START, L_V

                    def v01():
                        dve.wait_ge(bv_in, 16 * (it + 1))
                        for i in range(y, 2):
                            add_bv(vs[i], FS_V[i])

                    norm(b * TURNS + 1 + y, EPS1, v01)
                    tokens_normal()
                    extra_columns(it)
                    features(b * TURNS + 1 + y, y * 2 * CT)
                    add_bv(start + S_V2, FS_V[2])
                    add_column(start + S_Q0, FS_Q0, 0, 0)
                    add_column(start + S_Q1, FS_Q1, 0, 1)
                    extra_logits(start + S_EX0, 0)
                    maxima(0, start + S_EX0)
                    extra_logits(start + S_EX1, 1)
                    maxima(1, start + S_EX1)
                    add_bv(start + S_V3, FS_V[3])
                    turned(0)
                    maxima(2)
                    turned(1)
                    maxima(3)
                    dve.wait_ge(row_added, b * TURNS + 3 + y)
                    apart()
                    with dve.Fori(0, PAIRS - 1) as pr:
                        it = b * V_B + f0 + pr
                        F0, T = (it + 1) * F_PAIR, it * STEPS
                        n0 = nb + U_LOOP[y] + pr * U_PAIR
                        at_this = y * 4 * HEADS + pr * 2
                        at_next = at_this + 2
                        for t in range(2, STEPS + 2):
                            turned(t)
                            if t == 6:
                                output(OUT0[1:2], 0, [1])
                            if t == 7:
                                add_column(Q1, F_Q1, 0, 1)
                                output(OUT0[3:4], 0, [3])
                            if t == 9:
                                output(OUT1[0:1], 1, [0])
                                add_bv(V[2], F_V[2])
                                output(OUT1[1:2], 1, [1])
                            maxima(t + 2, {6: EX0, 8: EX1}.get(t))
                            if t == 5:
                                extra_logits(EX0, 0)
                                output(OUT0[0:1], 0, [0])
                            at_cols = at_next
                            if t == 2:
                                extra_columns(it + 1)
                                add_column(Q0, F_Q0, 0, 0)
                            if t % 2 == 0:
                                at_cols = at_this
                                extra_value(PV[t // 2 - 1], t // 2 - 1)
                                at_cols = at_next
                            if t == 2:
                                denominators(0)
                            if t == 3:
                                add_column(K0[0], F_K0[0], 1, 0)
                            if t == 4:
                                add_column(K0[1], F_K0[1], 1, 0)
                            if t == 6:
                                output(OUT0[2:3], 0, [2])
                                denominators(1)
                            if t == 7:
                                add_column(K1[0], F_K1[0], 1, 1)
                                add_column(K1[1], F_K1[1], 1, 1)
                                extra_logits(EX1, 1)
                            if t == 8:
                                dve.wait_ge(bv_in, 16 * (it + 2))
                                add_bv(V[0], F_V[0])
                                add_bv(V[1], F_V[1])
                        output(OUT1[2:3], 1, [2])
                        add_bv(V[3], F_V[3])
                        output(OUT1[3:4], 1, [3])
                    it = b * V_B + f0 + PAIRS - 1
                    F0, T = (it + 1) * F_PAIR, it * STEPS
                    n0 = nb + U_END[y]
                    more = y + 1 < LAYERS
                    pvs, out0, out1 = (L_PV, L_OUT0, L_OUT1) if more else (E_PV, E_OUT0, E_OUT1)
                    at_this, at_next = y * 4 * HEADS + (PAIRS - 1) * 2, (y + 1) * 4 * HEADS
                    for t in range(2, STEPS - 1):
                        turned(t)
                        if t + 2 < STEPS:
                            maxima(t + 2)
                        if t == 5 and more:
                            add_column(L_K1[0], FS_K1[0], 1, 1)
                        if t == 5:
                            output(out0[0:1], 0, [0])
                        if t == 6:
                            output(out0[1:2], 0, [1])
                        if t % 2 == 0:
                            at_cols = at_this
                            extra_value(pvs[t // 2 - 1], t // 2 - 1)
                        at_cols = at_next
                        if t in (2, 3) and more:
                            add_column(L_K0[t - 2], FS_K0[t - 2], 1, 0)
                        if t == 3:
                            denominators(0)
                    if more:
                        turned(STEPS - 1)
                    output(out0[2:3], 0, [2])
                    if more:
                        add_column(L_K1[1], FS_K1[1], 1, 1)
                    denominators(1)
                    output(out0[3:4], 0, [3])
                    if not more:
                        turned(STEPS - 1)
                    at_cols = at_this
                    extra_value(pvs[3], 3)
                    if more:
                        dve.wait_ge(bv_in, 16 * (it + 2))
                        add_bv(L_V[0], FS_V[0])
                    summed(lambda lt: output(out1[lt:lt + 1], 1, [lt]), n0 + out1[0])

                norm(b * TURNS + 3, EPS1, lambda: None)
                tokens_normal()
                features(b * TURNS + 3, LAYERS * 2 * CT)
                for fp in range(FPAIRS):
                    for i in range(2):
                        dve.wait_ge(g_hi, (b * FPAIRS + fp) * 2 + i + 1)
                        nc.vector.tensor_tensor(gT[fp % 2][i][1][:], g[i][:], f32(gT[fp % 2][i][0][:]), sub)\
                            .then_inc(g_lo, 1)
                dve.wait_ge(row_added, b * TURNS + 5)
                dve.wait_ge(mlp_out, FPAIRS * (b + 1) + 2)
                for lt in range(LT):
                    nc.vector.tensor_tensor(x_res[:, lt, :], ps_s[lt // 2][:, (lt % 2) * 512:(lt % 2 + 1) * 512],
                                            x_res[:, lt, :], ALU.add).then_inc(out_ready, 1)
                dve.wait_ge(out_ready, LT * (b + 1))
                dve.sem_inc(batch_done, 1)
                assert step[1] == DVE_B, step


DVE_B = 6 * 2 + 4 * 4 + (LAYERS + 2) * 6 + 2


def laid_out(inputs):
    i = {k: np.asarray(v) for k, v in inputs.items()}
    x, c = i["x"], i["ctx_2048"]

    def tiles(w):
        return w.reshape(-1, P, w.shape[1]).transpose(1, 0, 2)

    def both(name):
        return [i[f"L1_xattn_{name}{y}"] for y in (1, 2)]

    d = {
        "x": x.reshape(B, LT, P, D).transpose(0, 2, 1, 3),
        "xT": x.transpose(0, 2, 1).reshape(B, CT, P, L).transpose(0, 2, 1, 3),
        "ctxT": c.transpose(0, 2, 1).reshape(B, CT, P, S).transpose(0, 2, 1, 3),
        "mask": i["mask_Bx1xSxS2_ff0"].reshape(B, LT, P, S).transpose(0, 2, 1, 3),
        "w0q": tiles(i["L0_xattn_Wq"]).reshape(P, 2, CT * 256),
        "w0o": tiles(i["L0_xattn_Wo"]).reshape(P, 2, CT * 256),
        "w0kv": tiles(np.concatenate([i["L0_xattn_Wk"], i["L0_xattn_Wv"]], axis=1)),
        "cols0": np.concatenate([i["L0_xattn_bq"].reshape(CT, P).T, i["L0_xattn_bk"].reshape(1, P).T], axis=1),
        "bv0": i["L0_xattn_bv"],
    }
    qkv = np.stack([np.stack([tiles(w).reshape(P, CT, PAIRS, 256).transpose(2, 0, 1, 3) for w in ws], axis=2)
                    for ws in zip(both("wq"), both("wk"), both("wv"))]).reshape(LAYERS * PAIRS, P, 3, CT * 256)
    w1 = tiles(i["L1_xattn_w_fc1"]).reshape(P, CT, FPAIRS // 2, 2, 256).transpose(2, 0, 3, 1, 4)
    d["wqk"] = np.concatenate([qkv[:, :, 0:2], w1.reshape(FPAIRS // 2, P, 2, CT * 256)])
    d["wv"] = qkv[:, :, 2]
    d["wo"] = np.concatenate([w.reshape(-1, 2, P, D).transpose(0, 2, 1, 3) for w in (*both("wo"), i["L1_xattn_w_fc2"])])
    d["bv"] = np.stack(both("bv")).reshape(LAYERS * PAIRS, 256)
    d["cols"] = np.stack([np.stack([a.reshape(HEADS, KD).T for a in cs], axis=1)
                          for cs in zip(both("bq"), both("bk"), both("bias_k"), both("bias_v"))], axis=1)\
        .reshape(P, LAYERS * 4 * HEADS)
    norms = [np.stack([i[f"L1_xattn_ln{n}_{w}"].reshape(CT, P).T for w in ("scale", "offset")], axis=1)
             for n in ("1", "2", "_mlp")]
    d["lnc"] = np.stack(norms, axis=1).reshape(P, (LAYERS + 1) * 2 * CT)
    d["rows0"] = np.stack([i["L0_xattn_gamma"], i["L0_xattn_beta"]])
    d["rows"] = np.stack([i[n] for n in ("L0_xattn_bo", "L1_xattn_bo1", "L1_xattn_bo2", "L1_xattn_b_fc2")])
    d["colf"] = i["L1_xattn_b_fc1"].reshape(F // P, P).T
    return {k: np.ascontiguousarray(a) for k, a in d.items()}


def kernel(**inputs):
    import concourse.bacc as bacc
    from concourse.bass_utils import run_bass_kernel_spmd

    nc = bacc.Bacc("TRN2", target_bir_lowering=False, num_devices=1)
    arrays = laid_out(inputs)
    d = {k: nc.dram_tensor(f"in_{k}", a.shape, F32, kind="ExternalInput").ap() for k, a in arrays.items()}
    d["out"] = nc.dram_tensor("out", [B, P, LT, D], F32, kind="ExternalOutput").ap()
    build(nc, d)
    got = run_bass_kernel_spmd(nc, [{f"in_{k}": a for k, a in arrays.items()}], core_ids=[0]).results[0]["out"]
    return np.ascontiguousarray(np.asarray(got).reshape(B, P, LT, D).transpose(0, 2, 1, 3).reshape(B, L, D))
```
